# Optimizing a Trainium2 kernel written in Bass

```python
import numpy as np
import jax
import jax.numpy as jnp

def _softmax(x, axis=-1):
    return jax.nn.softmax(x, axis=axis)

def _gelu(x):
    return jax.nn.gelu(x, approximate=True)

def _silu(x):
    return jax.nn.silu(x)

def _sigmoid(x):
    return jax.nn.sigmoid(x)

def _layernorm(x, axis=-1, eps=1e-05):
    m = jnp.mean(x, axis=axis, keepdims=True)
    v = jnp.var(x, axis=axis, keepdims=True)
    return (x - m) / jnp.sqrt(v + eps)

def _scatter_add(tgt, idx, src, axis=0):
    return tgt.at[idx].add(src)

def _segment_sum(src, seg, n):
    return jax.ops.segment_sum(src, seg, n)
kernel_name = 'mk_adj_resnorm_d4_adj_r2_140d26'

def setup_inputs(seed: int=0):
    np.random.seed(seed)
    _w = jnp.asarray

    def _rec_inputs():
        import jax
        import jax.numpy as jnp
        _gk = jax.random.key(seed)
        x = -0.0001117 + 0.9999 * jax.random.normal(jax.random.fold_in(_gk, 1), (16, 512, 256), jnp.float32)
        _a = jax.random.bernoulli(jax.random.fold_in(_gk, 2), 0.015625, (512, 512))
        _a = jnp.logical_or(_a, jnp.swapaxes(_a, -1, -2))
        _a = jnp.logical_or(_a, jnp.eye(512, dtype=bool))
        adj = _a.astype(jnp.int32)
        return (x, adj)
    x, adj = _rec_inputs()

    def _L0_gnn_setup():
        import jax, jax.numpy as jnp
        import numpy as np
        B, N, F, F1 = (512, 75, 256, 128)
        NEG = -1000000000.0
        ALPHA = 0.2
        key = jax.random.key(seed)
        k1, k2, k3, k4 = jax.random.split(key, 4)
        X = jax.random.normal(k1, (B, N, F), dtype=jnp.float32)
        A = jax.random.randint(k2, (N, N), 0, 2, dtype=jnp.int32)
        W = jax.random.normal(k3, (F, F1), dtype=jnp.float32) * (1.0 / np.sqrt(F))
        a = jax.random.normal(k4, (2, F1, 1), dtype=jnp.float32) * (1.0 / np.sqrt(F1))
        return {'X': X, 'A': A, 'W': W, 'a': a}
    _L0_gnn_all = _L0_gnn_setup()
    _L0_gnn_in = {k: v for k, v in _L0_gnn_all.items() if k in ('W', 'a')}
    del _L0_gnn_all

    def _L1_gnn_setup():
        import jax, jax.numpy as jnp
        import numpy as np
        LEAKY_ALPHA = 0.01
        NEG_INF = -1000000000.0
        LN_EPS = 1e-05

        def _gat_heads(x, adj, W, a):
            O = W.shape[-1]
            Wh = jnp.einsum('bnf,hfo->bhno', x, W)
            f1 = jnp.einsum('bhno,ho->bhn', Wh, a[:, :O])
            f2 = jnp.einsum('bhno,ho->bhn', Wh, a[:, O:])
            e = f1[:, :, :, None] + f2[:, :, None, :]
            e = jnp.where(e > 0, e, LEAKY_ALPHA * e)
            e = jnp.where(adj[None, None] > 0, e, NEG_INF)
            attn = jax.nn.softmax(e, axis=-1)
            return jnp.einsum('bhnm,bhmo->bhno', attn, Wh)
        key = jax.random.key(seed)
        ks = jax.random.split(key, 10)
        B, N, F_in, F_hid, H, F_out, D_ff = (8, 1024, 256, 256, 4, 256, 256)
        s = 0.05
        return {'enc_inputs': jax.random.normal(ks[0], (B, N, F_in), jnp.float32), 'adj': jax.random.randint(ks[1], (N, N), 0, 2, jnp.int32), 'W_heads': jax.random.normal(ks[2], (H, F_in, F_hid), jnp.float32) * s, 'a_heads': jax.random.normal(ks[3], (H, 2 * F_hid), jnp.float32) * s, 'W_out': jax.random.normal(ks[4], (H * F_hid, F_out), jnp.float32) * s, 'a_out': jax.random.normal(ks[5], (2 * F_out,), jnp.float32) * s, 'w1': jax.random.normal(ks[6], (F_out, D_ff), jnp.float32) * s, 'b1': jnp.zeros((D_ff,), jnp.float32), 'w2': jax.random.normal(ks[7], (D_ff, F_out), jnp.float32) * s, 'b2': jnp.zeros((F_out,), jnp.float32), 'ln_gamma': jnp.ones((F_out,), jnp.float32), 'ln_beta': jnp.zeros((F_out,), jnp.float32)}
    _L1_gnn_all = _L1_gnn_setup()
    _L1_gnn_in = {k: v for k, v in _L1_gnn_all.items() if k in ('W_heads', 'a_heads', 'W_out', 'a_out', 'w1', 'b1', 'w2', 'b2', 'ln_gamma', 'ln_beta')}
    del _L1_gnn_all

    def _L2_gnn_setup():
        import jax, jax.numpy as jnp
        import numpy as np
        B, K, DIN, DOUT = (32, 64, 256, 256)
        key = jax.random.key(seed)
        k1, k2, k3, k4 = jax.random.split(key, 4)
        x = jax.random.normal(k1, (B, K, DIN), dtype=jnp.float32)
        adj = jax.random.randint(k2, (K, K), 0, 2, dtype=jnp.int32)
        W = jax.random.normal(k3, (DOUT, 2 * DIN), dtype=jnp.float32) * 0.02
        b = jax.random.normal(k4, (DOUT,), dtype=jnp.float32) * 0.02
        return {'x': x, 'adj': adj, 'W': W, 'b': b}
    _L2_gnn_all = _L2_gnn_setup()
    _L2_gnn_in = {k: v for k, v in _L2_gnn_all.items() if k in ('W', 'b')}
    del _L2_gnn_all

    def _L3_gnn_setup():
        import jax, jax.numpy as jnp
        import numpy as np
        B, N, D = (8, 1024, 256)
        NEG_SLOPE = 0.2
        key = jax.random.key(seed)
        k1, k2, k3, k4, k5 = jax.random.split(key, 5)
        x = jax.random.normal(k1, (B, N, D), dtype=jnp.float32)
        adj = jax.random.randint(k2, (N, N), 0, 2, dtype=jnp.int32)
        adj = jnp.maximum(adj, jnp.eye(N, dtype=jnp.int32))
        W = jax.random.normal(k3, (D, D), dtype=jnp.float32) * (1.0 / np.sqrt(D))
        a_src = jax.random.normal(k4, (D,), dtype=jnp.float32) * (1.0 / np.sqrt(D))
        a_dst = jax.random.normal(k5, (D,), dtype=jnp.float32) * (1.0 / np.sqrt(D))
        return {'x': x, 'adj': adj, 'W': W, 'a_src': a_src, 'a_dst': a_dst}
    _L3_gnn_all = _L3_gnn_setup()
    _L3_gnn_in = {k: v for k, v in _L3_gnn_all.items() if k in ('W', 'a_src', 'a_dst')}
    del _L3_gnn_all
    return {'x': x, 'adj': adj, 'L0_gnn_W': _L0_gnn_in['W'], 'L0_gnn_a': _L0_gnn_in['a'], 'L1_gnn_W_heads': _L1_gnn_in['W_heads'], 'L1_gnn_a_heads': _L1_gnn_in['a_heads'], 'L1_gnn_W_out': _L1_gnn_in['W_out'], 'L1_gnn_a_out': _L1_gnn_in['a_out'], 'L1_gnn_w1': _L1_gnn_in['w1'], 'L1_gnn_b1': _L1_gnn_in['b1'], 'L1_gnn_w2': _L1_gnn_in['w2'], 'L1_gnn_b2': _L1_gnn_in['b2'], 'L1_gnn_ln_gamma': _L1_gnn_in['ln_gamma'], 'L1_gnn_ln_beta': _L1_gnn_in['ln_beta'], 'L2_gnn_W': _L2_gnn_in['W'], 'L2_gnn_b': _L2_gnn_in['b'], 'L3_gnn_W': _L3_gnn_in['W'], 'L3_gnn_a_src': _L3_gnn_in['a_src'], 'L3_gnn_a_dst': _L3_gnn_in['a_dst']}

def reference(x, adj, L0_gnn_W, L0_gnn_a, L1_gnn_W_heads, L1_gnn_a_heads, L1_gnn_W_out, L1_gnn_a_out, L1_gnn_w1, L1_gnn_b1, L1_gnn_w2, L1_gnn_b2, L1_gnn_ln_gamma, L1_gnn_ln_beta, L2_gnn_W, L2_gnn_b, L3_gnn_W, L3_gnn_a_src, L3_gnn_a_dst):
    import jax
    import jax.numpy as jnp

    def _L0_gnn_ref(X, A, W, a):
        import jax, jax.numpy as jnp
        import numpy as np
        B, N, F, F1 = (512, 75, 256, 128)
        NEG = -1000000000.0
        ALPHA = 0.2
        h = jnp.einsum('bnf,fo->bno', X, W)
        att_self = jnp.einsum('bno,od->bnd', h, a[0])
        att_neigh = jnp.einsum('bno,od->bnd', h, a[1])
        e = att_self + jnp.swapaxes(att_neigh, 1, 2)
        e = jax.nn.leaky_relu(e, ALPHA)
        adj = A.astype(h.dtype)
        e = e + NEG * (1.0 - adj)[None, :, :]
        alpha = jax.nn.softmax(e, axis=-1)
        out = jnp.einsum('bij,bjo->bio', alpha, h)
        return jnp.concatenate([out, h], axis=-1)

    def _L1_gnn_ref(enc_inputs, adj, W_heads, a_heads, W_out, a_out, w1, b1, w2, b2, ln_gamma, ln_beta):
        import jax, jax.numpy as jnp
        import numpy as np
        LEAKY_ALPHA = 0.01
        NEG_INF = -1000000000.0
        LN_EPS = 1e-05

        def _gat_heads(x, adj, W, a):
            O = W.shape[-1]
            Wh = jnp.einsum('bnf,hfo->bhno', x, W)
            f1 = jnp.einsum('bhno,ho->bhn', Wh, a[:, :O])
            f2 = jnp.einsum('bhno,ho->bhn', Wh, a[:, O:])
            e = f1[:, :, :, None] + f2[:, :, None, :]
            e = jnp.where(e > 0, e, LEAKY_ALPHA * e)
            e = jnp.where(adj[None, None] > 0, e, NEG_INF)
            attn = jax.nn.softmax(e, axis=-1)
            return jnp.einsum('bhnm,bhmo->bhno', attn, Wh)
        B, N, _ = enc_inputs.shape
        h = jax.nn.elu(_gat_heads(enc_inputs, adj, W_heads, a_heads))
        h = jnp.transpose(h, (0, 2, 1, 3)).reshape(B, N, -1)
        out = _gat_heads(h, adj, W_out[None], a_out[None])[:, 0]
        out = jax.nn.elu(out)
        ffn = jnp.maximum(out @ w1 + b1, 0.0) @ w2 + b2
        y = ffn + out
        mu = jnp.mean(y, axis=-1, keepdims=True)
        var = jnp.var(y, axis=-1, keepdims=True)
        return (y - mu) / jnp.sqrt(var + LN_EPS) * ln_gamma + ln_beta

    def _L2_gnn_ref(x, adj, W, b):
        import jax, jax.numpy as jnp
        import numpy as np
        B, K, DIN, DOUT = (32, 64, 256, 256)
        Din = x.shape[-1]
        Wi, Wj = (W[:, :Din], W[:, Din:])
        mi = jnp.einsum('bkd,od->bko', x, Wi)
        mj = jnp.einsum('bkd,od->bko', x, Wj)
        a = adj.astype(x.dtype)
        deg = a.sum(axis=1)
        out = deg[None, :, None] * (mi + b) + jnp.einsum('ij,bjo->bio', a, mj)
        return out

    def _L3_gnn_ref(x, adj, W, a_src, a_dst):
        import jax, jax.numpy as jnp
        import numpy as np
        B, N, D = (8, 1024, 256)
        NEG_SLOPE = 0.2
        Wh = jnp.einsum('bnd,de->bne', x, W)
        e_src = jnp.einsum('bnd,d->bn', Wh, a_src)
        e_dst = jnp.einsum('bnd,d->bn', Wh, a_dst)
        logits = e_src[:, :, None] + e_dst[:, None, :]
        logits = jnp.where(logits >= 0, logits, NEG_SLOPE * logits)
        mask = (adj == 0)[None, :, :]
        logits = jnp.where(mask, -jnp.inf, logits)
        attn = jax.nn.softmax(logits, axis=-1)
        attn = jnp.nan_to_num(attn, nan=0.0)
        out = jnp.einsum('bnm,bmd->bnd', attn, Wh)
        return out
    x = _layernorm(x + _L0_gnn_ref(x, adj, L0_gnn_W, L0_gnn_a), axis=-1)
    x = _layernorm(x + _L1_gnn_ref(x, adj, L1_gnn_W_heads, L1_gnn_a_heads, L1_gnn_W_out, L1_gnn_a_out, L1_gnn_w1, L1_gnn_b1, L1_gnn_w2, L1_gnn_b2, L1_gnn_ln_gamma, L1_gnn_ln_beta), axis=-1)
    x = _layernorm(x + _L2_gnn_ref(x, adj, L2_gnn_W, L2_gnn_b), axis=-1)
    x = _layernorm(x + _L3_gnn_ref(x, adj, L3_gnn_W, L3_gnn_a_src, L3_gnn_a_dst), axis=-1)
    return x

_drawn_inputs = setup_inputs


def setup_inputs(seed=0):
    import zlib

    import numpy as np

    out = dict(_drawn_inputs(seed))
    spreads = {'L1_gnn_b1': (0.0, 0.1),
     'L1_gnn_b2': (0.0, 0.1),
     'L1_gnn_ln_gamma': (1.0, 0.2),
     'L1_gnn_ln_beta': (0.0, 0.1)}
    factors = {}
    for name, (base, spread) in spreads.items():
        noise = np.random.default_rng([zlib.crc32(name.encode()), seed]).standard_normal(out[name].shape)
        drawn = base * np.exp(spread * noise) if base else spread * noise
        out[name] = jnp.asarray(drawn.astype(out[name].dtype))
    for name, factor in factors.items():
        out[name] = (out[name] * factor).astype(out[name].dtype)
    return out
```

```python
import concourse.bass as bass
from concourse import mybir
from concourse.alu_op_type import AluOpType as ALU
import itertools
from contextlib import ExitStack

B, N, D, H = 16, 512, 256, 4
P = 128
NI = N // P
KD = D // P
D0 = D // 2
KH = H * D // P
EPS = 1e-5
NEG = -1e9
ALPHA = {"L0": 0.2, "L1": 0.01, "L3": 0.2}
T_RING, O_RING = 2, 2

HEADS = [f"H{h}" for h in range(H)]
ELU = HEADS + ["O1"]


def kind(n):
    if not isinstance(n, int):
        return "loop"
    return {-1: "pre", 0: "first", B - 1: "last", B: "end"}.get(n, "loop")


class Tally:

    def __init__(self, **steps):
        self.steps = {k: steps.get(k, []) for k in ("pre", "first", "loop", "last", "end")}
        
    def before(self, n):
        s, c = self.steps, len(self.steps["loop"])
        if isinstance(n, int):
            return sum(len(s[kind(m)]) for m in range(-1, n))
        return n * c + (len(s["pre"]) + len(s["first"]) - c)

    def at(self, n, step):
        return self.before(n) + self.steps[kind(n)].index(step) + 1




def stages_of(k):
    return {"pre": ["L0"], "first": HEADS + ["L0", "O1"], "loop": HEADS + ["L0", "L3", "O1"],
            "last": HEADS + ["L3", "O1"], "end": ["L3"]}[k]


def group_before(n, stage):
    order = stages_of(kind(n))
    if stage != order[0]:
        return n, order[order.index(stage) - 1]
    return n - 1, ("L0" if kind(n) == "first" else "O1")


KINDS = ("pre", "first", "loop", "last", "end")
A_KINDS, B_KINDS, PRE_KINDS = ("first", "loop", "last"), ("loop", "last", "end"), ("pre", "first", "loop")
GROUPS = Tally(**{k: stages_of(k) for k in KINDS})
UNITS = Tally(**{k: [(s, i) for s in stages_of(k) for i in range(NI)] for k in KINDS})
ELU_UNITS = Tally(**{k: [(s, i) for s in stages_of(k) if s in ELU for i in range(NI)] for k in KINDS})


def two(name):
    return [(name, 0), (name, 1)]


def norm_steps(name):
    return [f"{name}_stats", f"{name}_aggr", f"{name}_var", f"{name}_out"]


PE_A = Tally(
    pre=two("x0T") + ["f0", "V0"],
    **{k: two("x1T") + ["fH"] + two("V0H") + two("V1H") + two("V2H") + two("T0H") + two("V3H") + two("T1H")
       + (two("x0T") + ["f0", "V0"] if k in PRE_KINDS else [])
       + two("T2H") + two("T3H") + two("VO") + ["fO"] for k in A_KINDS})
ACT_A = Tally(
    pre=two("x0T") + ["V0"],
    **{k: two("x1T") + two("V0H") + two("V1H") + two("V2H") + two("T0H") + two("V3H") + two("T1H")
       + (two("x0T") + ["V0"] if k in PRE_KINDS else [])
       + two("T2H") + two("T3H") + two("VO") for k in A_KINDS})
DVE_A = Tally(
    pre=two("x0T") + ["f0", "x0sum", "V0"] + norm_steps("ln0"),
    **{k: two("x1T") + ["fH"] + two("V0H") + two("V1H") + ["h0"] + two("V2H") + two("T0H") + ["h1"] + two("V3H")
       + two("T1H") + ["h2"]
       + (two("x0T") + ["f0", "x0sum", "V0"] if k in PRE_KINDS else [])
       + two("T2H") + ["h3"] + two("T3H") + two("VO") + ["fO"]
       + (norm_steps("ln0") if k in PRE_KINDS else []) for k in A_KINDS})
POOL_A = Tally(pre=["ln0"], first=["x1b", "ln0"], loop=["x1b", "ln0"], last=["x1b"])

NORMS = ["ln0", "ln1", "ln1o", "ln2", "ln3"]

PE_B = Tally(**{k: two("outT") + two("ffn1") + two("ffn2") + two("x2T") + two("mj") + two("mi") + two("Amj")
                + two("x3T") + ["f3"] + two("V3") for k in B_KINDS})
ACT_B = Tally(**{k: two("outT") + two("ffn1") + two("x2T") + two("mj") + two("x3T") + two("V3") for k in B_KINDS})
DVE_B = Tally(**{k: ["h1b"] + two("outT") + two("ffn1") + two("ffn2") + norm_steps("ln1") + ["res1"]
                 + norm_steps("ln1o") + two("x2T") + two("mj") + two("mi") + two("Amj") + norm_steps("ln2")
                 + two("x3T") + ["f3"] + two("V3") + norm_steps("ln3") for k in B_KINDS})
X_LOADS = Tally(pre=["x"], first=["x"], loop=["x"])
POOL_B = Tally(**{k: ["ob"] + two("glo") + ["ln1", "xg", "ln1o", "xb", "ln2", "ln3"] for k in B_KINDS})

PREP = ["edges", "mask", "deg", "has_edge", "wh", "wo", "w1", "w2", "adjT", "wl0", "wl1", "wl2", "wl3",
        "w0", "w3", "wa_high", "wa_low", "consts"]
PREP_ACT = ["wh", "wo", "w1", "w2", "wl0", "wl1", "wl2", "wl3", "w0", "w3"]


def prepared(step):
    return PREP.index(step) + 1


def graph_net_kernel(nc, x_in, adj_in, w0_in, a0_in, wh_in, ah_in, wo_in, ao_in, w1_in, b1_in, w2_in, b2_in,
                     gamma_in, beta_in, wl2_in, bl2_in, w3_in, asrc_in, adst_in, out):
    f32, f32r, bf16, i32 = mybir.dt.float32, mybir.dt.float32r, mybir.dt.bfloat16, mybir.dt.int32
    ACT = mybir.ActivationFunctionType
    AX = mybir.AxisListType

    with ExitStack() as ctx:
        def sb(name, shape, dtype=f32):
            return ctx.enter_context(nc.sbuf_tensor(name, shape, dtype))

        def sem(name):
            return ctx.enter_context(nc.semaphore(name))

        def split_sb(name, width):
            return [sb(f"{name}_{part}", [P, width], f32r) for part in ("high", "low")]

        w0, wh, wo = split_sb("w0", KD * D0), split_sb("wh", KD * H * D), split_sb("wo", KH * D)
        w1, w2 = split_sb("w1", KD * D), split_sb("w2", KD * D)
        wi, wj, w3 = split_sb("wi", KD * D), split_sb("wj", KD * D), split_sb("w3", KD * D)
        WA = {"L0": (0, KD, 2), "H": (4, KD, 2 * H), "O1": (20, KH, 2), "L3": (36, KD, 2)}
        wa_raw = sb("wa_raw", [P, 40])
        wa = split_sb("wa", 40)
        mask = sb("mask", [P, NI, N], bf16)
        adjT = sb("adjT", [P, NI, N], f32r)
        ident = sb("ident", [P, P])
        deg = sb("deg", [P, NI])
        has_edge = sb("has_edge", [P, NI])
        deg_b = sb("deg_b", [P, NI, D])
        b2m1, gamma, beta = sb("b2m1", [P, D]), sb("gamma", [P, D]), sb("beta", [P, D])
        b1c = sb("b1c", [P, KD])
        minus_half = sb("minus_half", [P, NI])
        settled = sb("settled", [P, NI + len(NORMS)])

        GP = sb("GP", [P, 2 * NI * N])
        G = GP[:, 0:NI * N].rearrange("p (r n) -> p r n", n=N)
        Pm = GP[:, NI * N:2 * NI * N].rearrange("p (r n) -> p r n", n=N)
        PT = [sb(f"PT_{part}", [P, T_RING, NI, P], f32r) for part in ("high", "low")]
        SLOTS = HEADS + ["L0", "L3", "O1"]
        row_sum, row_inv = sb("row_sum", [P, len(SLOTS), NI]), sb("row_inv", [P, len(SLOTS), NI])
        shift = sb("shift", [P, len(SLOTS), NI])
        gmax, gtop, gleaky = sb("gmax", [P, NI]), sb("gtop", [P, NI]), sb("gleaky", [P, NI])

        work = sb("work", [P, 8, NI * D])

        def view(k):
            return work[:, k, :].rearrange("p (i d) -> p i d", i=NI)

        hx, he, x1, x1b, xb, hb, eb, x0 = (view(k) for k in range(8))
        eb_wide = work[:, 6, :].rearrange("p (o n) -> p o n", n=N)

        xTa, xTb = split_sb("xTa", KD * N), split_sb("xTb", KD * N)
        V0 = split_sb("V0", NI * D0)
        VH = [split_sb("VH0", NI * D), split_sb("VH1", NI * D)]
        VB = split_sb("VB", NI * D)
        hT = split_sb("hT", KH * N)

        fcols = {s: (sb(f"f_{s}", [P, NI, 2 * nh]), sb(f"fa_{s}", [P, NI, nh]), sb(f"fb_{s}", [P, NI, nh]))
                 for s, nh in (("L0", 1), ("H", H), ("O1", 1), ("L3", 1))}
        norm = {s: (sb(f"bn_{s}", [P, NI, 6]), sb(f"mv_{s}", [P, NI, 2]), sb(f"var_{s}", [P, NI]),
                    sb(f"rstd_{s}", [P, NI])) for s in "ab"}

        bank = [ctx.enter_context(nc.psum_tensor(f"bank{k}", [P, N], f32)) for k in range(8)]
        T_bank, O_bank, A_bank, B_bank, F_bank = bank[0:2], bank[2:4], bank[4:6], bank[6], bank[7]

        loaded = {k: sem(f"loaded_{k}") for k in
                  ("adj", "wh", "wo", "ah", "wl", "rows", "w0", "w3", "a", "bl2")}
        prep_dve, prep_act, prep_pe, prep_pool = sem("prep_dve"), sem("prep_act"), sem("prep_pe"), sem("prep_pool")
        dot_done = sem("dot_done")
        x_loaded, eb_moved, EB_LOADS = sem("x_loaded"), sem("eb_moved"), 2
        g_ready, r_ready, z_ready, p_ready = sem("g_ready"), sem("r_ready"), sem("z_ready"), sem("p_ready")
        t_full, high_done, low_done, o_full = sem("t_full"), sem("high_done"), sem("low_done"), sem("o_full")
        o_dve, o_act = sem("o_dve"), sem("o_act")
        f_row, tops, shift_ready, inv_ready, l3_inv = (sem("f_row"), sem("tops"), sem("shift_ready"),
                                                       sem("inv_ready"), sem("l3_inv"))
        pe_a, act_a, dve_a, pool_a = sem("pe_a"), sem("act_a"), sem("dve_a"), sem("pool_a")
        pe_b, act_b, dve_b, pool_b = sem("pe_b"), sem("act_b"), sem("dve_b"), sem("pool_b")

        block = ctx.enter_context(nc.Block())

        def tiles(operand, width):
            return operand[:, :].rearrange("p (k n) -> p k n", n=width)

        def wa_of(part, s):
            at, nk, w = WA[s]
            return part[:, at:at + nk * w].rearrange("p (k c) -> p k c", c=w)

        def f_of(stage):
            return (fcols["H"], int(stage[1]), H) if stage in HEADS else (fcols[stage], 0, 1)

        def alpha_of(stage):
            return ALPHA.get(stage, ALPHA["L1"])

        def v_of(stage):
            if stage in HEADS:
                return VH[int(stage[1]) % 2], D
            return {"L0": (V0, D0), "O1": (VH[1], D), "L3": (VB, D)}[stage]

        def a_bank_of(n, step):
            return A_bank[PE_A.steps[kind(n)].index(step) % 2]

        @block.sync
        def _(sp):
            x_v = x_in.rearrange("b (i p) d -> b p i d", p=P)
            out_v = out.rearrange("b (i p) d -> b p i d", p=P)
            sp.dma_start(work[:, 2:4, :].rearrange("p a n -> p (a n)").bitcast(i32)
                         .rearrange("p (i n) -> p i n", n=N),
                         adj_in.rearrange("(i p) n -> p i n", p=P)).then_inc(loaded["adj"], 16)
            wh_stage = GP[:, 0:KD * H * D].rearrange("p (k h o) -> p k h o", k=KD, h=H)
            for k in range(KD):
                sp.dma_start(wh_stage[:, k, :, :], wh_in[:, k * P:(k + 1) * P, :].rearrange("h p o -> p h o"))\
                    .then_inc(loaded["wh"], 16)
            sp.dma_start(work[:, 0:2, :].rearrange("p a n -> p (a n)"),
                         ah_in.rearrange("h o -> (h o)").partition_broadcast(P)).then_inc(loaded["ah"], 16)
            sp.dma_start(GP[:, NI * N:2 * NI * N].rearrange("p (k o) -> p k o", k=KH),
                         wo_in.rearrange("(k p) o -> p k o", p=P)).then_inc(loaded["wo"], 16)
            sp.dma_start(work[:, 7, :].rearrange("p (k n) -> p k n", n=2 * D),
                         wl2_in.rearrange("(k p) n -> p k n", p=P)).then_inc(loaded["wl"], 16)
            sp.dma_start(work[:, 6, 0:KD * D].rearrange("p (k o) -> p k o", k=KD),
                         w1_in.rearrange("(k p) o -> p k o", p=P)).then_inc(eb_moved, 16)
            sp.dma_start(work[:, 6, KD * D:2 * KD * D].rearrange("p (k o) -> p k o", k=KD),
                         w2_in.rearrange("(k p) o -> p k o", p=P)).then_inc(eb_moved, 16)
            with nc.allow_non_contiguous_dma(reason="256 bias values, once"):
                sp.dma_start(b1c[:, :], b1_in.rearrange("(k p) -> p k", p=P)).then_inc(loaded["rows"], 16)
            sp.dma_start(b2m1[:, :], b2_in.partition_broadcast(P)).then_inc(loaded["rows"], 16)
            sp.dma_start(gamma[:, :], gamma_in.partition_broadcast(P)).then_inc(loaded["rows"], 16)
            sp.dma_start(beta[:, :], beta_in.partition_broadcast(P)).then_inc(loaded["rows"], 16)
            sp.wait_ge(prep_pe, 1 + 2 * KD)
            sp.dma_start(x0, x_v[0]).then_inc(x_loaded, 16)
            sp.wait_ge(prep_dve, prepared("wh"))
            sp.dma_start(GP[:, 0:KD * D0].rearrange("p (k o) -> p k o", k=KD),
                         w0_in.rearrange("(k p) o -> p k o", p=P)).then_inc(loaded["w0"], 16)
            sp.dma_start(GP[:, 256:256 + KD * D].rearrange("p (k o) -> p k o", k=KD),
                         w3_in.rearrange("(k p) o -> p k o", p=P)).then_inc(loaded["w3"], 16)
            sp.dma_start(GP[:, 768:1024], bl2_in.partition_broadcast(P)).then_inc(loaded["bl2"], 16)
            sp.dma_start(GP[:, 1024:1280], a0_in.rearrange("a o c -> (a o c)").partition_broadcast(P))\
                .then_inc(loaded["a"], 16)
            sp.dma_start(GP[:, 1280:1792], ao_in.partition_broadcast(P)).then_inc(loaded["a"], 16)
            sp.dma_start(GP[:, 1792:2048], asrc_in.partition_broadcast(P)).then_inc(loaded["a"], 16)
            sp.dma_start(work[:, 0, 0:D], adst_in.partition_broadcast(P)).then_inc(loaded["a"], 16)

            def body(n):
                if kind(n) in A_KINDS and kind(n) in PRE_KINDS:
                    sp.wait_ge(dve_a, DVE_A.at(n - 1, "ln0_out"))
                    sp.dma_start(x0, x_v[n + 1]).then_inc(x_loaded, 16)
                if kind(n) in B_KINDS:
                    sp.wait_ge(dve_b, DVE_B.at(n, "ln3_out"))
                    sp.dma_start(out_v[n - 1], eb).then_inc(eb_moved, 16)

            body(0)
            with sp.Fori(1, B - 1) as n:
                body(n)
            body(B - 1)
            body(B)
            sp.wait_ge(eb_moved, 16 * (EB_LOADS + B))

        @block.gpsimd
        def _(pool):
            pool.memset(minus_half[:, :], -0.5)
            pool.memset(ident[:, :], 0.0).then_inc(prep_pool, 1)
            pool.wait_ge(prep_pool, 1)
            pool.affine_select(out=ident[:, :], in_=ident[:, :], compare_op=ALU.not_equal, fill=1.0, base=0,
                               pattern=[[-1, P]], channel_multiplier=1).then_inc(prep_pool, 1)
            pool.wait_ge(prep_dve, len(PREP))

            def scores(stage, n):
                for i in range(NI):
                    pool.wait_ge(r_ready, UNITS.at(n, (stage, i)))
                    pool.tensor_tensor(G[:, i, :], G[:, i, :], Pm[:, i, :], ALU.add).then_inc(z_ready, 1)

            def rstd(stream, dve_sem, dve_tally, name, n, done):
                var, rs = norm[stream][2:]
                pool.wait_ge(dve_sem, dve_tally.at(n, f"{name}_var"))
                pool.tensor_tensor(rs[:, :], var[:, :], minus_half[:, :], ALU.pow).then_inc(done, 1)

            def all_rows(row):
                return row[:, :].unsqueeze(1).to_broadcast([P, NI, D])

            def body(n):
                k = kind(n)
                a, b, pre = k in A_KINDS, k in B_KINDS, k in PRE_KINDS
                if a:
                    scores("H0", n)
                    scores("H1", n)
                if b:
                    pool.wait_ge(pe_b, PE_B.at(n, ("outT", 1)))
                    pool.tensor_tensor(hb, hb, all_rows(b2m1), ALU.add).then_inc(pool_b, 1)
                if a:
                    scores("H2", n)
                if b:
                    for o in range(KD):
                        pool.wait_ge(dve_b, DVE_B.at(n, ("ffn1", o)))
                        pool.tensor_tensor(tiles(VB[1], N)[:, o, :], eb_wide[:, o, :],
                                           tiles(VB[0], N)[:, o, :].bitcast(f32), ALU.subtract)\
                            .then_inc(pool_b, 1)
                if a:
                    scores("H3", n)
                if b:
                    rstd("b", dve_b, DVE_B, "ln1", n, pool_b)
                    pool.wait_ge(dve_b, DVE_B.at(n, "ln1_out"))
                    pool.tensor_tensor(eb, eb, all_rows(gamma), ALU.mult).then_inc(pool_b, 1)
                if pre:
                    scores("L0", n)
                if b:
                    rstd("b", dve_b, DVE_B, "ln1o", n, pool_b)
                    pool.wait_ge(pe_b, PE_B.at(n, ("x2T", 1)))
                    pool.tensor_tensor(xb, xb, deg_b[:, :, :], ALU.add).then_inc(pool_b, 1)
                if a:
                    if b:
                        pool.wait_ge(dve_b, DVE_B.at(n, "res1"))
                    else:
                        pool.wait_ge(dve_a, DVE_A.at(n - 1, "ln0_out"))
                    pool.tensor_tensor(x1b, x1, all_rows(beta), ALU.add).then_inc(pool_a, 1)
                if b:
                    rstd("b", dve_b, DVE_B, "ln2", n, pool_b)
                    if k != "end":
                        scores("L3", n)
                if pre:
                    rstd("a", dve_a, DVE_A, "ln0", n, pool_a)
                if a:
                    scores("O1", n)
                if k == "end":
                    scores("L3", n)
                if b:
                    rstd("b", dve_b, DVE_B, "ln3", n, pool_b)

            body(-1)
            body(0)
            with pool.Fori(1, B - 1) as n:
                body(n)
            body(B - 1)
            body(B)

        @block.scalar
        def _(act):
            for arrived, count, dst, src in (
                    (loaded["wh"], 32, wh, GP[:, 0:NI * N]), (loaded["wo"], 16, wo, GP[:, NI * N:2 * NI * N]),
                    (eb_moved, 32, w1, work[:, 6, 0:KD * D]), (eb_moved, 32, w2, work[:, 6, KD * D:2 * KD * D])):
                act.wait_ge(arrived, count)
                act.activation(dst[0][:, :], src, ACT.Copy).then_inc(prep_act, 1)
            for c in range(2 * KD):
                act.wait_ge(prep_pe, 2 + c)
                act.activation(tiles((wi, wj)[c // KD][0], D)[:, c % KD, :], bank[4 + c][:, 0:D], ACT.Copy)\
                    .then_inc(prep_act, 1)
            for name, dst, src in (("w0", w0, GP[:, 0:KD * D0]), ("w3", w3, GP[:, 256:256 + KD * D])):
                act.wait_ge(loaded[name], 16)
                act.activation(dst[0][:, :], src, ACT.Copy).then_inc(prep_act, 1)
            act.wait_ge(prep_dve, len(PREP))

            def relu(stage, n, i):
                alpha, (_, _, fb), h = alpha_of(stage), f_of(stage)[0], f_of(stage)[1]
                u = UNITS.at(n, (stage, i))
                act.wait_ge(g_ready, u)
                if kind(n) != "pre":
                    act.wait_ge(t_full, u - NI)
                act.activation(Pm[:, i, :], G[:, i, :], ACT.Relu, bias=fb[:, i, h:h + 1],
                               scale=(1 - alpha) / alpha).then_inc(r_ready, 1)

            def exp(stage, n, i):
                s = SLOTS.index(stage)
                act.wait_ge(z_ready, UNITS.at(n, (stage, i)))
                if i == 0:
                    act.wait_ge(shift_ready, GROUPS.at(n, stage))
                act.activation(Pm[:, i, :], G[:, i, :], ACT.Exp, bias=shift[:, s, i:i + 1],
                               accum_out=row_sum[:, s, i:i + 1]).then_inc(p_ready, 1)

            def high(stage, n, i):
                u = UNITS.at(n, (stage, i))
                act.wait_ge(t_full, u)
                if kind(n) != "pre" or i >= T_RING:
                    act.wait_ge(o_full, u - T_RING)
                act.activation(PT[0][:, i % T_RING, :, :], T_bank[i % T_RING][:, :]
                               .rearrange("p (j n) -> p j n", n=P), ACT.Copy).then_inc(high_done, 1)

            def elu_exp(stage, n, i):
                if stage not in ELU:
                    return
                act.wait_ge(o_dve, UNITS.at(n, (stage, i)))
                if i == 0 and stage in HEADS[1:]:
                    act.wait_ge(dve_a, DVE_A.at(n, f"h{int(stage[1]) - 1}"))
                if i == 0 and stage == "O1":
                    act.wait_ge(eb_moved, 16 * (n + EB_LOADS))
                dst = eb if stage == "O1" else he
                s = SLOTS.index(stage)
                act.activation(dst[:, i, :], O_bank[i % O_RING][:, 0:D], ACT.Exp, scale=row_inv[:, s, i:i + 1])\
                    .then_inc(o_act, 1)

            def attention(p, pn, q, qn, mid1=None, mid2=None):
                for i in range(NI):
                    if p:
                        high(p, pn, i)
                    if q:
                        relu(q, qn, i)
                    if i == 1 and mid1:
                        mid1()
                    if i >= 2 and p:
                        elu_exp(p, pn, i - 2)
                if mid2:
                    mid2()
                for i in range(NI):
                    if q:
                        exp(q, qn, i)
                    if i < 2 and p:
                        elu_exp(p, pn, i + 2)

            def split_a(n, step, dst, bias=0.0):
                act.wait_ge(pe_a, PE_A.at(n, step))
                act.activation(dst, a_bank_of(n, step)[:, :], ACT.Copy, bias=bias).then_inc(act_a, 1)

            def split_b(n, step, dst, bias=0.0):
                act.wait_ge(pe_b, PE_B.at(n, step))
                act.activation(dst, B_bank[:, :], ACT.Copy, bias=bias).then_inc(act_b, 1)

            def two_tiles(split, n, name, dst, bias=0.0):
                for k in range(2):
                    split(n, (name, k), tiles(dst, N)[:, k, :], bias)

            def v_head(n, h):
                two_tiles(split_a, n, f"V{h}H", VH[h % 2][0])

            def t_head(n, h):
                for c in range(KD):
                    split_a(n, (f"T{h}H", c), tiles(hT[0], N)[:, KD * h + c, :], -1.0)

            def hidden(n):
                for o in range(KD):
                    act.wait_ge(pe_b, PE_B.at(n, ("ffn1", o)))
                    act.activation(tiles(VB[0], N)[:, o, :], B_bank[:, :], ACT.Relu, bias=b1c[:, o:o + 1])\
                        .then_inc(act_b, 1)

            def body(n):
                k = kind(n)
                a, b, pre = k in A_KINDS, k in B_KINDS, k in PRE_KINDS
                if a:
                    two_tiles(split_a, n, "x1T", xTa[0])
                    v_head(n, 0)
                attention("O1" if b else None, n - 1, "H0" if a else None, n)
                if a:
                    v_head(n, 1)
                    attention("H0", n, "H1", n, mid1=(lambda: two_tiles(split_b, n, "outT", xTb[0], -1.0)) if b else None)
                    v_head(n, 2)
                    attention("H1", n, "H2", n, mid1=lambda: t_head(n, 0), mid2=(lambda: hidden(n)) if b else None)
                    v_head(n, 3)
                    attention("H2", n, "H3", n, mid1=lambda: t_head(n, 1))
                elif b:
                    two_tiles(split_b, n, "outT", xTb[0], -1.0)
                    hidden(n)
                if pre:
                    two_tiles(split_a, n, "x0T", xTa[0])
                    split_a(n, "V0", V0[0][:, :])
                if a:
                    attention("H3", n, "L0" if pre else None, n, mid1=lambda: t_head(n, 2),
                              mid2=(lambda: two_tiles(split_b, n, "x2T", xTb[0])) if b else None)
                elif pre:
                    attention(None, n, "L0", n)
                elif b:
                    two_tiles(split_b, n, "x2T", xTb[0])
                if b:
                    two_tiles(split_b, n, "mj", VB[0])
                if a:
                    t_head(n, 3)
                    two_tiles(split_a, n, "VO", VH[1][0])
                if b:
                    two_tiles(split_b, n, "x3T", xTb[0])
                    two_tiles(split_b, n, "V3", VB[0])
                attention("L0" if pre else None, n, "L3" if b else None, n)
                attention("L3" if b else None, n, "O1" if a else None, n)

            body(-1)
            body(0)
            with act.Fori(1, B - 1) as n:
                body(n)
            body(B - 1)
            body(B)

        @block.tensor
        def _(pe):
            def product(dst, left, right, first=True, last=True):
                passes = [(0, 0), (0, 1), (1, 0)]
                for m, (a, b) in enumerate(passes):
                    mm = pe.matmul(dst, left(a), right(b), start=first and m == 0, stop=last and m == 2)
                return mm

            def sum_of(dst, terms):
                for m, (left, right) in enumerate(terms):
                    mm = product(dst, left, right, m == 0, m == len(terms) - 1)
                return mm

            pe.wait_ge(prep_pool, 2)
            pe.wait_ge(prep_dve, prepared("edges"))
            edges = work[:, 4:6, :].rearrange("p a n -> p (a n)").rearrange("p (i n) -> p i n", n=N)
            for j in range(NI):
                for i in range(NI):
                    mm = pe.transpose(bank[j][:, i * P:(i + 1) * P], edges[:, i, j * P:(j + 1) * P], ident[:, :])
            mm.then_inc(prep_pe, 1)
            pe.wait_ge(loaded["wl"], 16)
            wl = work[:, 7, :].rearrange("p (k n) -> p k n", n=2 * D)
            for c in range(2 * KD):
                for o in range(KD):
                    mm = pe.transpose(bank[4 + c][:, o * P:(o + 1) * P], wl[:, o, c * P:(c + 1) * P], ident[:, :])
                mm.then_inc(prep_pe, 1)
            pe.wait_ge(prep_dve, len(PREP))

            def f_rows(stage, n):
                raw, h, nh = f_of(stage)[0][0], f_of(stage)[1], f_of(stage)[2]
                if stage == "L3":
                    pe.wait_ge(dve_b, DVE_B.at(n, "f3"))
                else:
                    pe.wait_ge(dve_a, DVE_A.at(n, {"L0": "f0", "O1": "fO"}.get(stage, "fH")))
                if kind(n) != "pre":
                    pe.wait_ge(g_ready, UNITS.at(n, (stage, 0)) - 1)
                for i in range(NI):
                    mm = pe.transpose(F_bank[:, i * P:(i + 1) * P],
                                      raw[:, i, nh + h:nh + h + 1].to_broadcast([P, P]), ident[:, :])
                mm.then_inc(f_row, 1)

            def turn(stage, n, i):
                u = UNITS.at(n, (stage, i))
                pe.wait_ge(p_ready, u)
                if kind(n) != "pre" or i >= T_RING:
                    pe.wait_ge(low_done, u - T_RING)
                for j in range(NI):
                    mm = pe.transpose(T_bank[i % T_RING][:, j * P:(j + 1) * P], Pm[:, i, j * P:(j + 1) * P],
                                      ident[:, :])
                mm.then_inc(t_full, 1)

            def weighted(stage, n, i):
                V, width = v_of(stage)
                pe.wait_ge(low_done, UNITS.at(n, (stage, i)))
                if i == 0:
                    if stage == "L3":
                        pe.wait_ge(dve_b, DVE_B.at(n, ("V3", 1)))
                    else:
                        step = {"L0": "V0", "O1": ("VO", 1)}.get(stage, (f"V{stage[1]}H", 1))
                        pe.wait_ge(dve_a, DVE_A.at(n, step))
                m, s = (n, stage) if i >= O_RING else group_before(n, stage)
                before = (s, (i - O_RING) % NI)
                if kind(n) != "pre" or i >= O_RING:
                    if s in ELU:
                        pe.wait_ge(o_act, ELU_UNITS.at(m, before))
                    else:
                        pe.wait_ge(o_dve, UNITS.at(m, before))
                sum_of(O_bank[i % O_RING][:, 0:width],
                       [(lambda a, j=j: PT[a][:, i % T_RING, j, :], lambda b, j=j: tiles(V[b], width)[:, j, :])
                        for j in range(NI)]).then_inc(o_full, 1)

            def attention(p, pn, mid1=None, mid2=None):
                if p:
                    turn(p, pn, 0)
                    turn(p, pn, 1)
                if mid1:
                    mid1()
                if p:
                    weighted(p, pn, 0)
                    turn(p, pn, 2)
                    weighted(p, pn, 1)
                    turn(p, pn, 3)
                if mid2:
                    mid2()
                if p:
                    weighted(p, pn, 2)
                    weighted(p, pn, 3)

            def free_a(n, step):
                steps = PE_A.steps[kind(n)]
                m = steps.index(step)
                if m >= 2:
                    pe.wait_ge(dve_a, DVE_A.at(n, steps[m - 2]))
                elif kind(n) != "pre":
                    last = PE_A.steps["pre" if kind(n) == "first" else "loop"]
                    pe.wait_ge(dve_a, DVE_A.at(n - 1, last[m - 2]))
                return a_bank_of(n, step)

            def free_b(n, step):
                steps = PE_B.steps[kind(n)]
                m = steps.index(step)
                if m:
                    pe.wait_ge(dve_b, DVE_B.at(n, steps[m - 1]))
                return B_bank

            def transposed(free, done, n, step, src, k):
                dst = free(n, step)
                for i in range(NI):
                    mm = pe.transpose(dst[:, i * P:(i + 1) * P], src[:, i, k * P:(k + 1) * P], ident[:, :])
                mm.then_inc(done, 1)

            def rows_times(dst, left, nk, right, i):
                return sum_of(dst, [(lambda a, k=k: tiles(left[a], N)[:, k, i * P:(i + 1) * P],
                                     lambda b, k=k: right(b)[:, k, :]) for k in range(nk)])

            def scalars(free, done, n, step, left, nk, s):
                w = WA[s][2]
                dst = free(n, step)
                for i in range(NI):
                    mm = rows_times(dst[:, i * w:(i + 1) * w], left, nk, lambda b: wa_of(wa[b], s), i)
                mm.then_inc(done, 1)

            def half(free, done, n, name, m, left, nk, right):
                dst = free(n, (name, m))
                for i in (2 * m, 2 * m + 1):
                    mm = rows_times(dst[:, i % 2 * D:(i % 2 + 1) * D], left, nk, right, i)
                mm.then_inc(done, 1)

            def halves(free, done, n, name, left, nk, right):
                for m in range(2):
                    half(free, done, n, name, m, left, nk, right)

            def v_head(n, h):
                halves(free_a, pe_a, n, f"V{h}H", xTa, KD,
                       lambda b: wh[b][:, :].rearrange("p (k c) -> p k c", k=KD)[:, :, h * D:(h + 1) * D])

            def t_head(n, h):
                pe.wait_ge(dve_a, DVE_A.at(n, f"h{h}"))
                for c in range(KD):
                    transposed(free_a, pe_a, n, (f"T{h}H", c), hx, c)

            def out_turn(n):
                pe.wait_ge(dve_b, DVE_B.at(n, "h1b"))
                for k in range(KD):
                    transposed(free_b, pe_b, n, ("outT", k), hb, k)

            def hidden(n):
                pe.wait_ge(dve_b, DVE_B.at(n, ("outT", 1)))
                for o in range(KD):
                    dst = free_b(n, ("ffn1", o))
                    sum_of(dst[:, :], [(lambda a, k=k: tiles(w1[a], D)[:, k, o * P:(o + 1) * P],
                                        lambda b, k=k: tiles(xTb[b], N)[:, k, :]) for k in range(KD)])\
                        .then_inc(pe_b, 1)

            def ffn_out(n):
                pe.wait_ge(pool_b, POOL_B.at(n, ("glo", 1)))
                halves(free_b, pe_b, n, "ffn2", VB, KD, lambda b: tiles(w2[b], D))

            def x2_turn(n):
                pe.wait_ge(dve_b, DVE_B.at(n, "ln1o_out"))
                for k in range(KD):
                    transposed(free_b, pe_b, n, ("x2T", k), xb, k)

            def body(n):
                k = kind(n)
                a, b, pre = k in A_KINDS, k in B_KINDS, k in PRE_KINDS
                if a:
                    pe.wait_ge(dve_a, DVE_A.at(n - 1, "ln0_out"))
                    for c in range(KD):
                        transposed(free_a, pe_a, n, ("x1T", c), x1, c)
                    pe.wait_ge(dve_a, DVE_A.at(n, ("x1T", 1)))
                    scalars(free_a, pe_a, n, "fH", xTa, KD, "H")
                    f_rows("H0", n)
                    v_head(n, 0)
                attention("O1" if b else None, n - 1)
                if a:
                    f_rows("H1", n)
                    v_head(n, 1)
                    attention("H0", n, mid1=(lambda: out_turn(n)) if b else None)
                    f_rows("H2", n)
                    v_head(n, 2)
                    attention("H1", n, mid1=lambda: t_head(n, 0), mid2=(lambda: hidden(n)) if b else None)
                    f_rows("H3", n)
                    v_head(n, 3)
                    attention("H2", n, mid1=lambda: t_head(n, 1), mid2=(lambda: ffn_out(n)) if b else None)
                elif b:
                    out_turn(n)
                    hidden(n)
                    ffn_out(n)
                if pre:
                    pe.wait_ge(x_loaded, X_LOADS.at(n, "x") * 16)
                    for c in range(KD):
                        transposed(free_a, pe_a, n, ("x0T", c), x0, c)
                    pe.wait_ge(dve_a, DVE_A.at(n, ("x0T", 1)))
                    scalars(free_a, pe_a, n, "f0", xTa, KD, "L0")
                    dst = free_a(n, "V0")
                    for i in range(NI):
                        mm = rows_times(dst[:, i * D0:(i + 1) * D0], xTa, KD, lambda b: tiles(w0[b], D0), i)
                    mm.then_inc(pe_a, 1)
                    f_rows("L0", n)
                if a:
                    attention("H3", n, mid1=lambda: t_head(n, 2), mid2=(lambda: x2_turn(n)) if b else None)
                elif b:
                    x2_turn(n)
                if b:
                    pe.wait_ge(dve_b, DVE_B.at(n, ("x2T", 1)))
                    halves(free_b, pe_b, n, "mj", xTb, KD, lambda b: tiles(wj[b], D))
                if a:
                    t_head(n, 3)
                if b:
                    halves(free_b, pe_b, n, "mi", xTb, KD, lambda b: tiles(wi[b], D))
                if a:
                    pe.wait_ge(dve_a, DVE_A.at(n, ("T3H", 1)))
                    half(free_a, pe_a, n, "VO", 0, hT, KH, lambda b: tiles(wo[b], D))
                if b:
                    for m in range(2):
                        dst = free_b(n, ("Amj", m))
                        for i in (2 * m, 2 * m + 1):
                            for t in range(2 * NI):
                                mm = pe.matmul(dst[:, i % 2 * D:(i % 2 + 1) * D], adjT[:, t // 2, i * P:(i + 1) * P],
                                               tiles(VB[t % 2], D)[:, t // 2, :], start=t == 0, stop=t == 2 * NI - 1)
                        mm.then_inc(pe_b, 1)
                if a:
                    half(free_a, pe_a, n, "VO", 1, hT, KH, lambda b: tiles(wo[b], D))
                    scalars(free_a, pe_a, n, "fO", hT, KH, "O1")
                if b:
                    pe.wait_ge(dve_b, DVE_B.at(n, "ln2_out"))
                    for c in range(KD):
                        transposed(free_b, pe_b, n, ("x3T", c), xb, c)
                    pe.wait_ge(dve_b, DVE_B.at(n, ("x3T", 1)))
                    scalars(free_b, pe_b, n, "f3", xTb, KD, "L3")
                    f_rows("L3", n)
                    halves(free_b, pe_b, n, "V3", xTb, KD, lambda b: tiles(w3[b], D))
                attention("L0" if pre else None, n)
                if a:
                    f_rows("O1", n)
                attention("L3" if b else None, n)

            body(-1)
            body(0)
            with pe.Fori(1, B - 1) as n:
                body(n)
            body(B - 1)
            body(B)

        @block.vector
        def _(dve):
            edges = work[:, 4:6, :].rearrange("p a n -> p (a n)").rearrange("p (i n) -> p i n", n=N)
            dots = itertools.count()
            dve.wait_ge(loaded["adj"], 16)
            dve.tensor_copy(edges, work[:, 2:4, :].rearrange("p a n -> p (a n)").bitcast(i32)
                            .rearrange("p (i n) -> p i n", n=N)).then_inc(prep_dve, 1)
            dve.wait_ge(prep_dve, prepared("edges"))
            dve.tensor_scalar(mask[:, :, :], edges, -NEG, NEG, ALU.mult, ALU.add).then_inc(prep_dve, 1)
            dve.tensor_reduce(deg[:, :], edges, AX.X, ALU.add).then_inc(prep_dve, 1)
            dve.wait_ge(prep_dve, prepared("deg"))
            dve.tensor_scalar(has_edge[:, :], deg[:, :], 1.0, None, ALU.min).then_inc(prep_dve, 1)

            def dot_columns(s, k, col, w, a):
                m = next(dots)
                if m >= NI:
                    dve.wait_ge(dot_done, m - NI + 1)
                dve.tensor_tensor_reduce(deg_b[:, m % NI, 0:w.shape[-1]], w, a, 1.0, 0.0, ALU.mult, ALU.add,
                                                wa_of(wa_raw, s)[:, k, col:col + 1]).then_inc(dot_done, 1)

            dve.wait_ge(loaded["wh"], 32)
            dve.wait_ge(loaded["ah"], 16)
            a_heads = work[:, 0:2, :].rearrange("p a n -> p (a n)")
            for k in range(KD):
                for h in range(H):
                    for c in range(2):
                        dot_columns("H", k, c * H + h, GP[:, (k * H + h) * D:(k * H + h + 1) * D],
                                           a_heads[:, (2 * h + c) * D:(2 * h + c + 1) * D])

            def low_part(name, dst, src):
                dve.wait_ge(prep_act, PREP_ACT.index(name) + 1)
                dve.tensor_tensor(dst[1], src, dst[0].bitcast(f32), ALU.subtract).then_inc(prep_dve, 1)

            def flat(w):
                return [part[:, :] for part in w]

            low_part("wh", flat(wh), GP[:, 0:NI * N])
            low_part("wo", flat(wo), GP[:, NI * N:2 * NI * N])
            low_part("w1", flat(w1), work[:, 6, 0:KD * D])
            low_part("w2", flat(w2), work[:, 6, KD * D:2 * KD * D])
            dve.wait_ge(prep_pe, 1)
            for j in range(NI):
                last = dve.tensor_copy(adjT[:, j, :], bank[j][:, :])
            last.then_inc(prep_dve, 1)
            for c in range(2 * KD):
                low_part(f"wl{c}", [tiles(part, D)[:, c % KD, :] for part in (wi, wj)[c // KD]], bank[4 + c][:, 0:D])
            dve.wait_ge(loaded["a"], 64)
            for k in range(KH):
                for c in range(2):
                    dot_columns("O1", k, c, GP[:, NI * N + k * D:NI * N + (k + 1) * D],
                                       GP[:, 1280 + c * D:1280 + (c + 1) * D])
            dve.wait_ge(loaded["w0"], 16)
            for k in range(KD):
                for c in range(2):
                    dot_columns("L0", k, c, GP[:, k * D0:(k + 1) * D0], GP[:, 1024 + c * D0:1024 + (c + 1) * D0])
            low_part("w0", flat(w0), GP[:, 0:KD * D0])
            dve.wait_ge(loaded["w3"], 16)
            for k in range(KD):
                for c, a in enumerate((GP[:, 1792:2048], work[:, 0, 0:D])):
                    dot_columns("L3", k, c, GP[:, 256 + k * D:256 + (k + 1) * D], a)
            low_part("w3", flat(w3), GP[:, 256:256 + KD * D])
            dve.wait_ge(dot_done, next(dots))
            dve.tensor_copy(wa[0][:, :], wa_raw[:, :]).then_inc(prep_dve, 1)
            dve.wait_ge(prep_dve, prepared("wa_high"))
            dve.tensor_tensor(wa[1][:, :], wa_raw[:, :], wa[0][:, :].bitcast(f32), ALU.subtract)\
                .then_inc(prep_dve, 1)
            dve.wait_ge(loaded["bl2"], 16)
            dve.wait_ge(loaded["rows"], 64)
            for i in range(NI):
                dve.tensor_scalar(deg_b[:, i, :], GP[:, 768:1024], deg[:, i:i + 1], None, ALU.mult)
            dve.tensor_scalar(b2m1[:, :], b2m1[:, :], -1.0, None, ALU.add).then_inc(prep_dve, 1)
            dve.wait_ge(prep_dve, len(PREP))

            def settle(place):
                dve.memset(settled[:, place:place + 1], 0.0)

            def mask_max(stage, n, i):
                u = UNITS.at(n, (stage, i))
                if i == 0:
                    dve.wait_ge(f_row, GROUPS.at(n, stage))
                if kind(n) != "pre":
                    dve.wait_ge(p_ready, u - NI)
                settle(i)
                dve.tensor_tensor_reduce(G[:, i, :], F_bank[:, :], mask[:, i, :], alpha_of(stage), -3e38,
                                         ALU.add, ALU.max, gmax[:, i:i + 1]).then_inc(g_ready, 1)

            def shifts(stage, n):
                (_, fa, _), h, _ = f_of(stage)
                g = GROUPS.at(n, stage)
                dve.wait_ge(g_ready, UNITS.at(n, (stage, NI - 1)))
                dve.tensor_tensor(gtop[:, :], gmax[:, :], fa[:, :, h], ALU.add).then_inc(tops, 1)
                dve.wait_ge(tops, 2 * g - 1)
                dve.scalar_tensor_tensor(gleaky[:, :], gtop[:, :], 1 / alpha_of(stage), gtop[:, :],
                                         ALU.mult, ALU.max).then_inc(tops, 1)
                dve.wait_ge(tops, 2 * g)
                dve.tensor_tensor(shift[:, SLOTS.index(stage), :], fa[:, :, h], gleaky[:, :], ALU.subtract)\
                    .then_inc(shift_ready, 1)

            def inverses(stage, n):
                s = SLOTS.index(stage)
                dve.wait_ge(p_ready, UNITS.at(n, (stage, NI - 1)))
                if stage == "L3":
                    dve.reciprocal(row_inv[:, s, :], row_sum[:, s, :]).then_inc(l3_inv, 1)
                    dve.wait_ge(l3_inv, n)
                    dve.tensor_tensor(row_inv[:, s, :], row_inv[:, s, :], has_edge[:, :], ALU.mult)\
                        .then_inc(inv_ready, 1)
                else:
                    dve.reciprocal(row_inv[:, s, :], row_sum[:, s, :]).then_inc(inv_ready, 1)
                dve.wait_ge(inv_ready, GROUPS.at(n, stage))

            def low(stage, n, i):
                dve.wait_ge(high_done, UNITS.at(n, (stage, i)))
                dve.tensor_tensor(PT[1][:, i % T_RING, :, :],
                                  T_bank[i % T_RING][:, :].rearrange("p (j n) -> p j n", n=P),
                                  PT[0][:, i % T_RING, :, :].bitcast(f32), ALU.subtract).then_inc(low_done, 1)

            def evacuate(stage, n, i):
                inv = row_inv[:, SLOTS.index(stage), i:i + 1]
                O = O_bank[i % O_RING]
                dve.wait_ge(o_full, UNITS.at(n, (stage, i)))
                if stage == "L0":
                    dve.scalar_tensor_tensor(x0[:, i, 0:D0], O[:, 0:D0], inv, x0[:, i, 0:D0], ALU.mult, ALU.add)\
                        .then_inc(o_dve, 1)
                elif stage == "L3":
                    dve.scalar_tensor_tensor(xb[:, i, :], O[:, 0:D], inv, xb[:, i, :], ALU.mult, ALU.add)\
                        .then_inc(o_dve, 1)
                else:
                    if i == 0 and stage in HEADS[1:]:
                        dve.wait_ge(pe_a, PE_A.at(n, (f"T{int(stage[1]) - 1}H", 1)))
                    dve.tensor_scalar((hb if stage == "O1" else hx)[:, i, :], O[:, 0:D], inv, 0.0,
                                      ALU.mult, ALU.max).then_inc(o_dve, 1)

            def attention(p, pn, q, qn, mid1=None, mid2=None):
                if p:
                    inverses(p, pn)
                for i in range(NI):
                    if q:
                        mask_max(q, qn, i)
                    if p:
                        low(p, pn, i)
                    if i == 1 and mid1:
                        mid1()
                    if i >= 2 and p:
                        evacuate(p, pn, i - 2)
                if q:
                    shifts(q, qn)
                if mid2:
                    mid2()
                if p:
                    evacuate(p, pn, 2)
                    evacuate(p, pn, 3)

            def split_a(n, step, dst, high_part, bias=0.0):
                dve.wait_ge(act_a, ACT_A.at(n, step))
                dve.scalar_tensor_tensor(dst, a_bank_of(n, step)[:, :], bias, high_part.bitcast(f32),
                                         ALU.add, ALU.subtract).then_inc(dve_a, 1)

            def split_b(n, step, dst, high_part, bias=0.0):
                dve.wait_ge(act_b, ACT_B.at(n, step))
                dve.scalar_tensor_tensor(dst, B_bank[:, :], bias, high_part.bitcast(f32),
                                         ALU.add, ALU.subtract).then_inc(dve_b, 1)

            def two_tiles(split, n, name, dst, bias=0.0):
                for k in range(2):
                    split(n, (name, k), tiles(dst[1], N)[:, k, :], tiles(dst[0], N)[:, k, :], bias)

            def v_head(n, h):
                two_tiles(split_a, n, f"V{h}H", VH[h % 2])

            def t_head(n, h):
                for c in range(KD):
                    k = KD * h + c
                    split_a(n, (f"T{h}H", c), tiles(hT[1], N)[:, k, :], tiles(hT[0], N)[:, k, :], -1.0)

            def elu(n, h):
                dve.wait_ge(o_act, ELU_UNITS.at(n, (f"H{h}", NI - 1)))
                dve.wait_ge(o_dve, UNITS.at(n, (f"H{h}", NI - 1)))
                dve.scalar_tensor_tensor(hx, he, 1.0, hx, ALU.min, ALU.add).then_inc(dve_a, 1)

            def scalars(n, s, src, sem_in, count, done):
                raw, fa, fb = fcols[s]
                nh, alpha = WA[s][2] // 2, ALPHA.get(s, ALPHA["L1"])
                F = src[:, 0:NI * 2 * nh].rearrange("p (i c) -> p i c", i=NI)
                dve.wait_ge(sem_in, count)
                dve.tensor_copy(raw[:, :, :], F)
                dve.tensor_scalar(fa[:, :, :], F[:, :, 0:nh], alpha, None, ALU.mult)
                dve.tensor_scalar(fb[:, :, :], F[:, :, 0:nh], 1 - alpha, None, ALU.mult).then_inc(done, 1)

            def layer_norm(stream, n, name, src, dst):
                bn, mv, var, rs = norm[stream]
                steps, tally, rsteps, rtally = ((dve_a, DVE_A, pool_a, POOL_A) if stream == "a"
                                                else (dve_b, DVE_B, pool_b, POOL_B))
                for i in range(NI):
                    last = dve.bn_stats(bn[:, i, :], src[:, i, :])
                last.then_inc(steps, 1)
                dve.wait_ge(steps, tally.at(n, f"{name}_stats"))
                settle(NI + NORMS.index(name))
                for i in range(NI):
                    last = dve.bn_aggr(mv[:, i, :], bn[:, i, :])
                last.then_inc(steps, 1)
                dve.wait_ge(steps, tally.at(n, f"{name}_aggr"))
                dve.tensor_scalar(var[:, :], mv[:, :, 1], EPS, None, ALU.add).then_inc(steps, 1)
                dve.wait_ge(rsteps, rtally.at(n, name))
                for i in range(NI):
                    last = dve.tensor_scalar(dst[:, i, :], src[:, i, :], mv[:, i, 0:1], rs[:, i:i + 1],
                                             ALU.subtract, ALU.mult)
                last.then_inc(steps, 1)

            def hidden(n):
                for o in range(KD):
                    dve.wait_ge(act_b, ACT_B.at(n, ("ffn1", o)))
                    dve.tensor_scalar(eb_wide[:, o, :], B_bank[:, :], b1c[:, o:o + 1], 0.0, ALU.add, ALU.max)\
                        .then_inc(dve_b, 1)

            def add_bank(n, name, m, dst):
                dve.wait_ge(pe_b, PE_B.at(n, (name, m)))
                part = dst[:, 2 * m:2 * m + 2, :]
                dve.tensor_tensor(part, B_bank[:, :].rearrange("p (i d) -> p i d", d=D), part, ALU.add)\
                    .then_inc(dve_b, 1)

            def ffn_out(n):
                dve.wait_ge(pool_b, POOL_B.at(n, "ob"))
                for m in range(2):
                    add_bank(n, "ffn2", m, hb)

            def inner_norm(n):
                dve.wait_ge(dve_b, DVE_B.at(n, ("ffn2", 1)))
                layer_norm("b", n, "ln1", hb, eb)
                dve.wait_ge(pool_b, POOL_B.at(n, "xg"))
                dve.wait_ge(pool_a, POOL_A.at(n - 1, "x1b"))
                dve.tensor_tensor(xb, eb, x1b, ALU.add).then_inc(dve_b, 1)

            def outer_norm(n):
                dve.wait_ge(dve_b, DVE_B.at(n, "res1"))
                layer_norm("b", n, "ln1o", xb, xb)
                two_tiles(split_b, n, "x2T", xTb)

            def elu_out(n):
                dve.wait_ge(o_act, ELU_UNITS.at(n - 1, ("O1", NI - 1)))
                dve.wait_ge(o_dve, UNITS.at(n - 1, ("O1", NI - 1)))
                dve.scalar_tensor_tensor(hb, eb, 1.0, hb, ALU.min, ALU.add).then_inc(dve_b, 1)

            def body(n):
                k = kind(n)
                a, b, pre = k in A_KINDS, k in B_KINDS, k in PRE_KINDS
                if a:
                    two_tiles(split_a, n, "x1T", xTa)
                    scalars(n, "H", a_bank_of(n, "fH"), pe_a, PE_A.at(n, "fH"), dve_a)
                    v_head(n, 0)
                attention("O1" if b else None, n - 1, "H0" if a else None, n)
                if b:
                    elu_out(n)
                if a:
                    v_head(n, 1)
                    attention("H0", n, "H1", n, mid1=(lambda: two_tiles(split_b, n, "outT", xTb, -1.0)) if b else None)
                    elu(n, 0)
                    v_head(n, 2)
                    attention("H1", n, "H2", n, mid1=lambda: t_head(n, 0), mid2=(lambda: hidden(n)) if b else None)
                    elu(n, 1)
                    v_head(n, 3)
                    attention("H2", n, "H3", n, mid1=lambda: t_head(n, 1), mid2=(lambda: ffn_out(n)) if b else None)
                    elu(n, 2)
                elif b:
                    two_tiles(split_b, n, "outT", xTb, -1.0)
                    hidden(n)
                    ffn_out(n)
                if pre:
                    two_tiles(split_a, n, "x0T", xTa)
                    scalars(n, "L0", a_bank_of(n, "f0"), pe_a, PE_A.at(n, "f0"), dve_a)
                    dve.wait_ge(act_a, ACT_A.at(n, "V0"))
                    V = a_bank_of(n, "V0")[:, :]
                    dve.tensor_tensor(x0[:, :, D0:D], V.rearrange("p (i d) -> p i d", d=D0), x0[:, :, D0:D], ALU.add)\
                        .then_inc(dve_a, 1)
                    dve.tensor_tensor(V0[1][:, :], V, V0[0][:, :].bitcast(f32), ALU.subtract).then_inc(dve_a, 1)
                if b:
                    inner_norm(n)
                if a:
                    attention("H3", n, "L0" if pre else None, n, mid1=lambda: t_head(n, 2),
                              mid2=(lambda: outer_norm(n)) if b else None)
                    elu(n, 3)
                elif pre:
                    attention(None, n, "L0", n)
                elif b:
                    outer_norm(n)
                if b:
                    two_tiles(split_b, n, "mj", VB)
                if a:
                    t_head(n, 3)
                if b:
                    dve.wait_ge(pool_b, POOL_B.at(n, "xb"))
                    for m in range(2):
                        dve.wait_ge(pe_b, PE_B.at(n, ("mi", m)))
                        for i in (2 * m, 2 * m + 1):
                            last = dve.scalar_tensor_tensor(xb[:, i, :], B_bank[:, i % 2 * D:(i % 2 + 1) * D],
                                                            deg[:, i:i + 1], xb[:, i, :], ALU.mult, ALU.add)
                        last.then_inc(dve_b, 1)
                if a:
                    split_a(n, ("VO", 0), tiles(VH[1][1], N)[:, 0, :], tiles(VH[1][0], N)[:, 0, :])
                if b:
                    dve.wait_ge(dve_b, DVE_B.at(n, ("mi", 1)))
                    for m in range(2):
                        add_bank(n, "Amj", m, xb)
                if a:
                    split_a(n, ("VO", 1), tiles(VH[1][1], N)[:, 1, :], tiles(VH[1][0], N)[:, 1, :])
                    scalars(n, "O1", a_bank_of(n, "fO"), pe_a, PE_A.at(n, "fO"), dve_a)
                if b:
                    dve.wait_ge(dve_b, DVE_B.at(n, ("Amj", 1)))
                    layer_norm("b", n, "ln2", xb, xb)
                    two_tiles(split_b, n, "x3T", xTb)
                    scalars(n, "L3", B_bank, pe_b, PE_B.at(n, "f3"), dve_b)
                    two_tiles(split_b, n, "V3", VB)
                attention("L0" if pre else None, n, "L3" if b else None, n)
                if pre:
                    dve.wait_ge(o_dve, UNITS.at(n, ("L0", NI - 1)))
                    dve.wait_ge(dve_a, DVE_A.at(n, "x0sum"))
                    layer_norm("a", n, "ln0", x0, x1)
                attention("L3" if b else None, n, "O1" if a else None, n)
                if b:
                    dve.wait_ge(o_dve, UNITS.at(n, ("L3", NI - 1)))
                    layer_norm("b", n, "ln3", xb, eb)

            body(-1)
            body(0)
            with dve.Fori(1, B - 1) as n:
                body(n)
            body(B - 1)
            body(B)


_INS = ['x', 'adj', 'L0_gnn_W', 'L0_gnn_a', 'L1_gnn_W_heads', 'L1_gnn_a_heads', 'L1_gnn_W_out', 'L1_gnn_a_out',
        'L1_gnn_w1', 'L1_gnn_b1', 'L1_gnn_w2', 'L1_gnn_b2', 'L1_gnn_ln_gamma', 'L1_gnn_ln_beta', 'L2_gnn_W',
        'L2_gnn_b', 'L3_gnn_W', 'L3_gnn_a_src', 'L3_gnn_a_dst']


def kernel(**inputs):
    import numpy as _np
    import concourse.bacc as _bacc
    from concourse import mybir as _mybir
    from concourse.bass_utils import run_bass_kernel_spmd as _run

    nc = _bacc.Bacc("TRN2", target_bir_lowering=False, num_devices=1)
    arrays, args = {}, []
    for name in _INS:
        a = _np.ascontiguousarray(inputs[name])
        arrays[f"in_{name}"] = a
        args.append(nc.dram_tensor(f"in_{name}", a.shape, _mybir.dt.from_np(a.dtype), kind="ExternalInput").ap())
    args.append(nc.dram_tensor("out_x", (B, N, D), _mybir.dt.float32, kind="ExternalOutput").ap())
    graph_net_kernel(nc, *args)
    r = _run(nc, [arrays], core_ids=[0])
    return r.results[0]["out_x"]
```

```python
import concourse.bass as bass
from concourse import mybir
from concourse.alu_op_type import AluOpType as ALU
import itertools
from contextlib import ExitStack

B, N, D, H = 16, 512, 256, 4
P = 128
NI = N // P
KD = D // P
D0 = D // 2
KH = H * D // P
EPS = 1e-5
NEG = -1e9
ALPHA = {"L0": 0.2, "L1": 0.01, "L3": 0.2}
T_RING, O_RING = 2, 2

HEADS = [f"H{h}" for h in range(H)]
ELU = HEADS + ["O1"]


def kind(n):
    if not isinstance(n, int):
        return "loop"
    return {-1: "pre", 0: "first", B - 1: "last", B: "end"}.get(n, "loop")


class Tally:

    def __init__(self, **steps):
        self.steps = {k: steps.get(k, []) for k in ("pre", "first", "loop", "last", "end")}
        
    def before(self, n):
        s, c = self.steps, len(self.steps["loop"])
        if isinstance(n, int):
            return sum(len(s[kind(m)]) for m in range(-1, n))
        return n * c + (len(s["pre"]) + len(s["first"]) - c)

    def at(self, n, step):
        return self.before(n) + self.steps[kind(n)].index(step) + 1




def stages_of(k):
    return {"pre": ["L0"], "first": HEADS + ["L0", "O1"], "loop": HEADS + ["L0", "L3", "O1"],
            "last": HEADS + ["L3", "O1"], "end": ["L3"]}[k]


def group_before(n, stage):
    order = stages_of(kind(n))
    if stage != order[0]:
        return n, order[order.index(stage) - 1]
    return n - 1, ("L0" if kind(n) == "first" else "O1")


KINDS = ("pre", "first", "loop", "last", "end")
A_KINDS, B_KINDS, PRE_KINDS = ("first", "loop", "last"), ("loop", "last", "end"), ("pre", "first", "loop")
GROUPS = Tally(**{k: stages_of(k) for k in KINDS})
UNITS = Tally(**{k: [(s, i) for s in stages_of(k) for i in range(NI)] for k in KINDS})
ELU_UNITS = Tally(**{k: [(s, i) for s in stages_of(k) if s in ELU for i in range(NI)] for k in KINDS})


NEXT = {"x0T", "f0", "f0_high", "f0_raw", "V0", "x0sum", "ln0"} | {f"ln0_{s}" for s in ("stats", "aggr", "var", "out")}


def in_turn(stream, *steps):
    def kinds(step):
        if stream == "B":
            return B_KINDS
        return PRE_KINDS if (step if isinstance(step, str) else step[0]) in NEXT else A_KINDS

    return Tally(**{k: [s for s in steps if k in kinds(s)] for k in KINDS})


PE_A = in_turn(
    "A", ("x1T", 0), ("x1T", 1), "fH", ("V0H", 0), ("V0H", 1), ("V1H", 0), ("V1H", 1), ("V2H", 0), ("V2H", 1),
    ("T0H", 0), ("T0H", 1), ("T1H", 0), ("T1H", 1), ("V3H", 0), ("V3H", 1), ("x0T", 0), ("x0T", 1),
    ("T2H", 0), "f0", ("T2H", 1), "V0", ("T3H", 0), ("T3H", 1), "fO", ("VO", 0), ("VO", 1))
PE_B = in_turn(
    "B", ("outT", 0), ("outT", 1), ("ffn1", 0), ("ffn1", 1), ("ffn2", 0), ("ffn2", 1), ("x2T", 0), ("x2T", 1),
    ("mj", 0), ("mi", 0), ("mj", 1), ("mi", 1), ("Amj", 0), ("Amj", 1), ("x3T", 0), ("x3T", 1), "f3",
    ("V3", 0), ("V3", 1))
ACT_A = in_turn(
    "A", ("x1T", 0), ("x1T", 1), ("V0H", 0), ("V0H", 1), ("V1H", 0), ("V1H", 1), ("V2H", 0), ("V2H", 1),
    ("T0H", 0), ("T0H", 1), ("T1H", 0), ("T1H", 1), ("V3H", 0), ("V3H", 1), ("x0T", 0), ("x0T", 1),
    ("T2H", 0), ("T2H", 1), "V0", ("T3H", 0), ("T3H", 1), ("VO", 0), ("VO", 1))
ACT_B = in_turn(
    "B", ("outT", 0), ("outT", 1), ("ffn1", 0), ("ffn1", 1), ("x2T", 0), ("x2T", 1), ("mj", 0), ("mj", 1),
    ("x3T", 0), ("x3T", 1), ("V3", 0), ("V3", 1))
DVE_A = in_turn(
    "A", ("x1T", 0), ("x1T", 1), "fH_high", "fH_raw", "fH", ("V0H", 0), ("V0H", 1), ("V1H", 0), ("V1H", 1), "h0",
    ("V2H", 0), ("V2H", 1), "h1", ("T0H", 0), ("T0H", 1), ("T1H", 0), ("T1H", 1), ("V3H", 0), "h2",
    ("V3H", 1), ("x0T", 0), ("x0T", 1), ("T2H", 0), "f0_high", "f0_raw", "f0", ("T2H", 1), "x0sum", "V0",
    "h3", ("T3H", 0), ("T3H", 1), "fO_high", "fO_raw", "fO", "ln0_stats", "ln0_aggr", "ln0_var", "ln0_out",
    ("VO", 0), ("VO", 1))
DVE_B = in_turn(
    "B", "h1b", ("outT", 0), ("outT", 1), ("ffn1", 0), ("ffn1", 1), ("ffn2", 0), ("ffn2", 1), "ln1_stats",
    "ln1_aggr", "ln1_var", "ln1_out", "res1", "ln1o_stats", "ln1o_aggr", "ln1o_var", "ln1o_out", ("x2T", 0),
    ("x2T", 1), ("mj", 0), ("mi", 0), ("mj", 1), ("mi", 1), ("Amj", 0), ("Amj", 1), "ln2_stats", "ln2_aggr",
    "ln2_var", "ln2_out", ("x3T", 0), ("x3T", 1), "f3_high", "f3_raw", "f3", ("V3", 0), ("V3", 1),
    "ln3_stats", "ln3_aggr", "ln3_var", "ln3_out")
POOL_A = in_turn(
    "A", "x1b", "ln0")
POOL_B = in_turn(
    "B", "ob", ("glo", 0), ("glo", 1), "ln1", "xg", "ln1o", "xb", "ln2", "ln3")
X_LOADS = Tally(pre=["x"], first=["x"], loop=["x"])
NORMS = ["ln0", "ln1", "ln1o", "ln2", "ln3"]

PREP = ["edges", "mask", "deg", "has_edge", "wh", "wo", "w1", "w2", "adjT", "wl0", "wl1", "wl2", "wl3",
        "w0", "w3", "wa_high", "wa_low", "consts"]
PREP_ACT = ["wh", "wo", "w1", "w2", "wl0", "wl1", "wl2", "wl3", "w0", "w3"]


def prepared(step):
    return PREP.index(step) + 1


def graph_net_kernel(nc, x_in, adj_in, w0_in, a0_in, wh_in, ah_in, wo_in, ao_in, w1_in, b1_in, w2_in, b2_in,
                     gamma_in, beta_in, wl2_in, bl2_in, w3_in, asrc_in, adst_in, out):
    f32, f32r, bf16, i32 = mybir.dt.float32, mybir.dt.float32r, mybir.dt.bfloat16, mybir.dt.int32
    ACT = mybir.ActivationFunctionType
    AX = mybir.AxisListType

    with ExitStack() as ctx:
        def sb(name, shape, dtype=f32):
            return ctx.enter_context(nc.sbuf_tensor(name, shape, dtype))

        def sem(name):
            return ctx.enter_context(nc.semaphore(name))

        def split_sb(name, width):
            return [sb(f"{name}_{part}", [P, width], f32r) for part in ("high", "low")]

        w0, wh, wo = split_sb("w0", KD * D0), split_sb("wh", KD * H * D), split_sb("wo", KH * D)
        w1, w2 = split_sb("w1", KD * D), split_sb("w2", KD * D)
        wi, wj, w3 = split_sb("wi", KD * D), split_sb("wj", KD * D), split_sb("w3", KD * D)
        WA = {"L0": (0, KD, 2), "H": (4, KD, 2 * H), "O1": (20, KH, 2), "L3": (36, KD, 2)}
        wa_raw = sb("wa_raw", [P, 40])
        wa = sb("wa", [P, 2, 40], f32r)
        mask = sb("mask", [P, NI, N], bf16)
        adjT = sb("adjT", [P, NI, N], f32r)
        ident = sb("ident", [P, P])
        deg = sb("deg", [P, NI])
        has_edge = sb("has_edge", [P, NI])
        deg_b = sb("deg_b", [P, NI, D])
        b2m1, gamma, beta = sb("b2m1", [P, D]), sb("gamma", [P, D]), sb("beta", [P, D])
        b1c = sb("b1c", [P, KD])
        minus_half = sb("minus_half", [P, NI])
        settled = sb("settled", [P, NI + len(NORMS)])

        GP = sb("GP", [P, 2 * NI * N])
        G = GP[:, 0:NI * N].rearrange("p (r n) -> p r n", n=N)
        Pm = GP[:, NI * N:2 * NI * N].rearrange("p (r n) -> p r n", n=N)
        PT = [sb(f"PT_{part}", [P, T_RING, NI, P], f32r) for part in ("high", "low")]
        SLOTS = HEADS + ["L0", "L3", "O1"]
        row_sum, row_inv = sb("row_sum", [P, len(SLOTS), NI]), sb("row_inv", [P, len(SLOTS), NI])
        shift = sb("shift", [P, len(SLOTS), NI])
        gmax, gtop, gleaky = sb("gmax", [P, NI]), sb("gtop", [P, NI]), sb("gleaky", [P, NI])

        work = sb("work", [P, 8, NI * D])

        def view(k):
            return work[:, k, :].rearrange("p (i d) -> p i d", i=NI)

        hx, he, x1, x1b, xb, hb, eb, x0 = (view(k) for k in range(8))
        eb_wide = work[:, 6, :].rearrange("p (o n) -> p o n", n=N)

        xTa, xTb = split_sb("xTa", KD * N), split_sb("xTb", KD * N)
        V0 = split_sb("V0", NI * D0)
        VH = [split_sb("VH0", NI * D), split_sb("VH1", NI * D)]
        VB = split_sb("VB", NI * D)
        hT = split_sb("hT", KH * N)

        fcols = {s: (sb(f"f_{s}", [P, NI, 2 * nh]), sb(f"fa_{s}", [P, NI, nh]), sb(f"fb_{s}", [P, NI, nh]))
                 for s, nh in (("L0", 1), ("H", H), ("O1", 1), ("L3", 1))}
        norm = {s: (sb(f"bn_{s}", [P, NI, 6]), sb(f"mv_{s}", [P, NI, 2]), sb(f"var_{s}", [P, NI]),
                    sb(f"rstd_{s}", [P, NI])) for s in "ab"}

        bank = [ctx.enter_context(nc.psum_tensor(f"bank{k}", [P, N], f32)) for k in range(8)]
        T_bank, O_bank, A_bank, B_bank, F_bank = bank[0:2], bank[2:4], bank[4:6], bank[6], bank[7]

        loaded = {k: sem(f"loaded_{k}") for k in
                  ("adj", "wh", "wo", "ah", "wl", "rows", "w0", "w3", "a", "bl2")}
        prep_dve, prep_act, prep_pe, prep_pool = sem("prep_dve"), sem("prep_act"), sem("prep_pe"), sem("prep_pool")
        dot_done = sem("dot_done")
        x_loaded, eb_moved, EB_LOADS = sem("x_loaded"), sem("eb_moved"), 2
        g_ready, r_ready, z_ready, p_ready = sem("g_ready"), sem("r_ready"), sem("z_ready"), sem("p_ready")
        t_full, high_done, low_done, o_full = sem("t_full"), sem("high_done"), sem("low_done"), sem("o_full")
        o_dve, o_act = sem("o_dve"), sem("o_act")
        f_row, tops, shift_ready, inv_ready, l3_inv = (sem("f_row"), sem("tops"), sem("shift_ready"),
                                                       sem("inv_ready"), sem("l3_inv"))
        pe_a, act_a, dve_a, pool_a = sem("pe_a"), sem("act_a"), sem("dve_a"), sem("pool_a")
        pe_b, act_b, dve_b, pool_b = sem("pe_b"), sem("act_b"), sem("dve_b"), sem("pool_b")

        block = ctx.enter_context(nc.Block())

        def tiles(operand, width):
            return operand[:, :].rearrange("p (k n) -> p k n", n=width)

        def wa_of(s, k):
            at, _, w = WA[s]
            return slice(at + k * w, at + (k + 1) * w)

        def f_of(stage):
            return (fcols["H"], int(stage[1]), H) if stage in HEADS else (fcols[stage], 0, 1)

        def alpha_of(stage):
            return ALPHA.get(stage, ALPHA["L1"])

        def v_of(stage):
            if stage in HEADS:
                return VH[int(stage[1]) % 2], D
            return {"L0": (V0, D0), "O1": (VH[1], D), "L3": (VB, D)}[stage]

        def a_bank_of(n, step):
            return A_bank[PE_A.steps[kind(n)].index(step) % 2]

        @block.sync
        def _(sp):
            x_v = x_in.rearrange("b (i p) d -> b p i d", p=P)
            out_v = out.rearrange("b (i p) d -> b p i d", p=P)
            sp.dma_start(work[:, 2:4, :].rearrange("p a n -> p (a n)").bitcast(i32)
                         .rearrange("p (i n) -> p i n", n=N),
                         adj_in.rearrange("(i p) n -> p i n", p=P)).then_inc(loaded["adj"], 16)
            wh_stage = GP[:, 0:KD * H * D].rearrange("p (k h o) -> p k h o", k=KD, h=H)
            for k in range(KD):
                sp.dma_start(wh_stage[:, k, :, :], wh_in[:, k * P:(k + 1) * P, :].rearrange("h p o -> p h o"))\
                    .then_inc(loaded["wh"], 16)
            sp.dma_start(work[:, 0:2, :].rearrange("p a n -> p (a n)"),
                         ah_in.rearrange("h o -> (h o)").partition_broadcast(P)).then_inc(loaded["ah"], 16)
            sp.dma_start(GP[:, NI * N:2 * NI * N].rearrange("p (k o) -> p k o", k=KH),
                         wo_in.rearrange("(k p) o -> p k o", p=P)).then_inc(loaded["wo"], 16)
            sp.dma_start(work[:, 7, :].rearrange("p (k n) -> p k n", n=2 * D),
                         wl2_in.rearrange("(k p) n -> p k n", p=P)).then_inc(loaded["wl"], 16)
            sp.dma_start(work[:, 6, 0:KD * D].rearrange("p (k o) -> p k o", k=KD),
                         w1_in.rearrange("(k p) o -> p k o", p=P)).then_inc(eb_moved, 16)
            sp.dma_start(work[:, 6, KD * D:2 * KD * D].rearrange("p (k o) -> p k o", k=KD),
                         w2_in.rearrange("(k p) o -> p k o", p=P)).then_inc(eb_moved, 16)
            with nc.allow_non_contiguous_dma(reason="256 bias values, once"):
                sp.dma_start(b1c[:, :], b1_in.rearrange("(k p) -> p k", p=P)).then_inc(loaded["rows"], 16)
            sp.dma_start(b2m1[:, :], b2_in.partition_broadcast(P)).then_inc(loaded["rows"], 16)
            sp.dma_start(gamma[:, :], gamma_in.partition_broadcast(P)).then_inc(loaded["rows"], 16)
            sp.dma_start(beta[:, :], beta_in.partition_broadcast(P)).then_inc(loaded["rows"], 16)
            sp.wait_ge(prep_pe, 1 + 2 * KD)
            sp.dma_start(x0, x_v[0]).then_inc(x_loaded, 16)
            sp.wait_ge(prep_dve, prepared("wh"))
            sp.dma_start(GP[:, 0:KD * D0].rearrange("p (k o) -> p k o", k=KD),
                         w0_in.rearrange("(k p) o -> p k o", p=P)).then_inc(loaded["w0"], 16)
            sp.dma_start(GP[:, 256:256 + KD * D].rearrange("p (k o) -> p k o", k=KD),
                         w3_in.rearrange("(k p) o -> p k o", p=P)).then_inc(loaded["w3"], 16)
            sp.dma_start(GP[:, 768:1024], bl2_in.partition_broadcast(P)).then_inc(loaded["bl2"], 16)
            sp.dma_start(GP[:, 1024:1280], a0_in.rearrange("a o c -> (a o c)").partition_broadcast(P))\
                .then_inc(loaded["a"], 16)
            sp.dma_start(GP[:, 1280:1792], ao_in.partition_broadcast(P)).then_inc(loaded["a"], 16)
            sp.dma_start(GP[:, 1792:2048], asrc_in.partition_broadcast(P)).then_inc(loaded["a"], 16)
            sp.dma_start(work[:, 0, 0:D], adst_in.partition_broadcast(P)).then_inc(loaded["a"], 16)

            def body(n):
                if kind(n) in A_KINDS and kind(n) in PRE_KINDS:
                    sp.wait_ge(dve_a, DVE_A.at(n - 1, "ln0_out"))
                    sp.dma_start(x0, x_v[n + 1]).then_inc(x_loaded, 16)
                if kind(n) in B_KINDS:
                    sp.wait_ge(dve_b, DVE_B.at(n, "ln3_out"))
                    sp.dma_start(out_v[n - 1], eb).then_inc(eb_moved, 16)

            body(0)
            with sp.Fori(1, B - 1) as n:
                body(n)
            body(B - 1)
            body(B)
            sp.wait_ge(eb_moved, 16 * (EB_LOADS + B))

        @block.gpsimd
        def _(pool):
            pool.memset(minus_half[:, :], -0.5)
            pool.memset(ident[:, :], 0.0).then_inc(prep_pool, 1)
            pool.wait_ge(prep_pool, 1)
            pool.affine_select(out=ident[:, :], in_=ident[:, :], compare_op=ALU.not_equal, fill=1.0, base=0,
                               pattern=[[-1, P]], channel_multiplier=1).then_inc(prep_pool, 1)
            pool.wait_ge(prep_dve, len(PREP))

            def scores(stage, n, i):
                pool.wait_ge(r_ready, UNITS.at(n, (stage, i)))
                pool.tensor_tensor(G[:, i, :], G[:, i, :], Pm[:, i, :], ALU.add).then_inc(z_ready, 1)

            def rstd(stream, dve_sem, dve_tally, name, n, done):
                var, rs = norm[stream][2:]
                pool.wait_ge(dve_sem, dve_tally.at(n, f"{name}_var"))
                pool.tensor_tensor(rs[:, :], var[:, :], minus_half[:, :], ALU.pow).then_inc(done, 1)

            def all_rows(row):
                return row[:, :].unsqueeze(1).to_broadcast([P, NI, D])

            def out_bias(n):
                pool.wait_ge(pe_b, PE_B.at(n, ("outT", 1)))
                pool.tensor_tensor(hb, hb, all_rows(b2m1), ALU.add).then_inc(pool_b, 1)

            def hidden_low(n, o):
                pool.wait_ge(dve_b, DVE_B.at(n, ("ffn1", o)))
                pool.tensor_tensor(tiles(VB[1], N)[:, o, :], eb_wide[:, o, :],
                                   tiles(VB[0], N)[:, o, :].bitcast(f32), ALU.subtract).then_inc(pool_b, 1)

            def times_gamma(n):
                pool.wait_ge(dve_b, DVE_B.at(n, "ln1_out"))
                pool.tensor_tensor(eb, eb, all_rows(gamma), ALU.mult).then_inc(pool_b, 1)

            def message_bias(n):
                pool.wait_ge(pe_b, PE_B.at(n, ("x2T", 1)))
                pool.tensor_tensor(xb, xb, deg_b[:, :, :], ALU.add).then_inc(pool_b, 1)

            def plus_beta(n):
                if kind(n) in B_KINDS:
                    pool.wait_ge(dve_b, DVE_B.at(n, "res1"))
                else:
                    pool.wait_ge(dve_a, DVE_A.at(n - 1, "ln0_out"))
                pool.tensor_tensor(x1b, x1, all_rows(beta), ALU.add).then_inc(pool_a, 1)

            def rstd_b(name, n):
                rstd("b", dve_b, DVE_B, name, n, pool_b)

            def rstd_a(name, n):
                rstd("a", dve_a, DVE_A, name, n, pool_a)

            def body(n):
                k = kind(n)
                a, b, pre = k in A_KINDS, k in B_KINDS, k in PRE_KINDS
                if a:
                    scores("H0", n, 0)
                    scores("H0", n, 1)
                    scores("H0", n, 2)
                    scores("H0", n, 3)
                if b:
                    out_bias(n)
                if a:
                    scores("H1", n, 0)
                if b:
                    hidden_low(n, 0)
                if a:
                    scores("H1", n, 1)
                    scores("H1", n, 2)
                if b:
                    hidden_low(n, 1)
                if a:
                    scores("H1", n, 3)
                    scores("H2", n, 0)
                    scores("H2", n, 1)
                if b:
                    rstd_b("ln1", n)
                    times_gamma(n)
                if a:
                    scores("H2", n, 2)
                    scores("H2", n, 3)
                    scores("H3", n, 0)
                if b:
                    rstd_b("ln1o", n)
                if a:
                    plus_beta(n)
                    scores("H3", n, 1)
                if b:
                    message_bias(n)
                if a:
                    scores("H3", n, 2)
                    scores("H3", n, 3)
                if b:
                    rstd_b("ln2", n)
                if pre:
                    scores("L0", n, 0)
                    scores("L0", n, 1)
                    scores("L0", n, 2)
                    scores("L0", n, 3)
                if b:
                    scores("L3", n, 0)
                    scores("L3", n, 1)
                    scores("L3", n, 2)
                    scores("L3", n, 3)
                if a:
                    scores("O1", n, 0)
                    scores("O1", n, 1)
                    scores("O1", n, 2)
                    scores("O1", n, 3)
                if pre:
                    rstd_a("ln0", n)
                if b:
                    rstd_b("ln3", n)

            body(-1)
            body(0)
            with pool.Fori(1, B - 1) as n:
                body(n)
            body(B - 1)
            body(B)

        @block.scalar
        def _(act):
            for arrived, count, dst, src in (
                    (loaded["wh"], 32, wh, GP[:, 0:NI * N]), (loaded["wo"], 16, wo, GP[:, NI * N:2 * NI * N]),
                    (eb_moved, 32, w1, work[:, 6, 0:KD * D]), (eb_moved, 32, w2, work[:, 6, KD * D:2 * KD * D])):
                act.wait_ge(arrived, count)
                act.activation(dst[0][:, :], src, ACT.Copy).then_inc(prep_act, 1)
            for c in range(2 * KD):
                act.wait_ge(prep_pe, 2 + c)
                act.activation(tiles((wi, wj)[c // KD][0], D)[:, c % KD, :], bank[4 + c][:, 0:D], ACT.Copy)\
                    .then_inc(prep_act, 1)
            for name, dst, src in (("w0", w0, GP[:, 0:KD * D0]), ("w3", w3, GP[:, 256:256 + KD * D])):
                act.wait_ge(loaded[name], 16)
                act.activation(dst[0][:, :], src, ACT.Copy).then_inc(prep_act, 1)
            act.wait_ge(prep_dve, len(PREP))

            def relu(stage, n, i):
                alpha, (_, _, fb), h = alpha_of(stage), f_of(stage)[0], f_of(stage)[1]
                u = UNITS.at(n, (stage, i))
                act.wait_ge(g_ready, u)
                if kind(n) != "pre":
                    act.wait_ge(t_full, u - NI)
                act.activation(Pm[:, i, :], G[:, i, :], ACT.Relu, bias=fb[:, i, h:h + 1],
                               scale=(1 - alpha) / alpha).then_inc(r_ready, 1)

            def exp(stage, n, i):
                s = SLOTS.index(stage)
                act.wait_ge(z_ready, UNITS.at(n, (stage, i)))
                if i == 0:
                    act.wait_ge(shift_ready, GROUPS.at(n, stage))
                act.activation(Pm[:, i, :], G[:, i, :], ACT.Exp, bias=shift[:, s, i:i + 1],
                               accum_out=row_sum[:, s, i:i + 1]).then_inc(p_ready, 1)

            def high(stage, n, i):
                u = UNITS.at(n, (stage, i))
                act.wait_ge(t_full, u)
                if kind(n) != "pre" or i >= T_RING:
                    act.wait_ge(o_full, u - T_RING)
                act.activation(PT[0][:, i % T_RING, :, :], T_bank[i % T_RING][:, :]
                               .rearrange("p (j n) -> p j n", n=P), ACT.Copy).then_inc(high_done, 1)

            def elu_exp(stage, n, i):
                act.wait_ge(o_dve, UNITS.at(n, (stage, i)))
                if i == 0 and stage in HEADS[1:]:
                    act.wait_ge(dve_a, DVE_A.at(n, f"h{int(stage[1]) - 1}"))
                if i == 0 and stage == "H0" and kind(n) != "first":
                    act.wait_ge(dve_a, DVE_A.at(n - 1, "h3"))
                if i == 0 and stage == "O1":
                    act.wait_ge(eb_moved, 16 * (n + EB_LOADS))
                dst = eb if stage == "O1" else he
                s = SLOTS.index(stage)
                act.activation(dst[:, i, :], O_bank[i % O_RING][:, 0:D], ACT.Exp, scale=row_inv[:, s, i:i + 1])\
                    .then_inc(o_act, 1)

            def split_a(n, step, dst, bias=0.0):
                act.wait_ge(pe_a, PE_A.at(n, step))
                act.activation(dst, a_bank_of(n, step)[:, :], ACT.Copy, bias=bias).then_inc(act_a, 1)

            def split_b(n, step, dst, bias=0.0):
                act.wait_ge(pe_b, PE_B.at(n, step))
                act.activation(dst, B_bank[:, :], ACT.Copy, bias=bias).then_inc(act_b, 1)

            def tile_a(n, name, k, dst, bias=0.0):
                split_a(n, (name, k), tiles(dst, N)[:, k, :], bias)

            def tile_b(n, name, k, dst, bias=0.0):
                split_b(n, (name, k), tiles(dst, N)[:, k, :], bias)

            def v_head(n, h, m):
                last = {1: (n - 1, ("O1", NI - 1)), 2: (n, ("H0", NI - 1)), 3: (n, ("H1", NI - 1))}
                if m == 0 and h and (h > 1 or kind(n) != "first"):
                    act.wait_ge(o_full, UNITS.at(*last[h]))
                tile_a(n, f"V{h}H", m, VH[h % 2][0])

            def v_out(n, m):
                if m == 0:
                    act.wait_ge(o_full, UNITS.at(n, ("H3", NI - 1)))
                tile_a(n, "VO", m, VH[1][0])

            def t_head(n, h, c):
                split_a(n, (f"T{h}H", c), tiles(hT[0], N)[:, KD * h + c, :], -1.0)

            def x0_turn(n, c):
                if kind(n) != "pre":
                    act.wait_ge(pe_a, PE_A.at(n, ("V3H", 1)))
                tile_a(n, "x0T", c, xTa[0])

            def hidden(n, o):
                act.wait_ge(pe_b, PE_B.at(n, ("ffn1", o)))
                act.activation(tiles(VB[0], N)[:, o, :], B_bank[:, :], ACT.Relu, bias=b1c[:, o:o + 1])\
                    .then_inc(act_b, 1)

            def body(n):
                k = kind(n)
                a, b, pre = k in A_KINDS, k in B_KINDS, k in PRE_KINDS
                if b:
                    high("O1", n - 1, 0)
                    high("O1", n - 1, 1)
                if a:
                    tile_a(n, "x1T", 0, xTa[0])
                    tile_a(n, "x1T", 1, xTa[0])
                if b:
                    high("O1", n - 1, 2)
                    elu_exp("O1", n - 1, 0)
                    high("O1", n - 1, 3)
                    elu_exp("O1", n - 1, 1)
                    elu_exp("O1", n - 1, 2)
                    elu_exp("O1", n - 1, 3)
                if a:
                    relu("H0", n, 0)
                    v_head(n, 0, 0)
                    relu("H0", n, 1)
                if b:
                    tile_b(n, "outT", 0, xTb[0], -1.0)
                if a:
                    relu("H0", n, 2)
                    v_head(n, 0, 1)
                    relu("H0", n, 3)
                if b:
                    tile_b(n, "outT", 1, xTb[0], -1.0)
                if a:
                    exp("H0", n, 0)
                    exp("H0", n, 1)
                    exp("H0", n, 2)
                    exp("H0", n, 3)
                if b:
                    hidden(n, 0)
                if a:
                    relu("H1", n, 0)
                    relu("H1", n, 1)
                    high("H0", n, 0)
                    high("H0", n, 1)
                    exp("H1", n, 0)
                if b:
                    hidden(n, 1)
                if a:
                    relu("H1", n, 2)
                    relu("H1", n, 3)
                    exp("H1", n, 1)
                    high("H0", n, 2)
                    elu_exp("H0", n, 0)
                    v_head(n, 1, 0)
                    high("H0", n, 3)
                    v_head(n, 1, 1)
                    elu_exp("H0", n, 1)
                    exp("H1", n, 2)
                    exp("H1", n, 3)
                    relu("H2", n, 0)
                    relu("H2", n, 1)
                    exp("H2", n, 0)
                    exp("H2", n, 1)
                    high("H1", n, 0)
                    elu_exp("H0", n, 2)
                    v_head(n, 2, 0)
                    high("H1", n, 1)
                    v_head(n, 2, 1)
                    elu_exp("H0", n, 3)
                    high("H1", n, 2)
                    relu("H2", n, 2)
                    relu("H2", n, 3)
                    relu("H3", n, 0)
                    high("H1", n, 3)
                    exp("H2", n, 2)
                    exp("H2", n, 3)
                    t_head(n, 0, 0)
                    t_head(n, 0, 1)
                    elu_exp("H1", n, 0)
                if b:
                    tile_b(n, "x2T", 0, xTb[0])
                if a:
                    elu_exp("H1", n, 1)
                    relu("H3", n, 1)
                    high("H2", n, 0)
                    elu_exp("H1", n, 2)
                    high("H2", n, 1)
                if b:
                    tile_b(n, "x2T", 1, xTb[0])
                if a:
                    elu_exp("H1", n, 3)
                    relu("H3", n, 2)
                    high("H2", n, 2)
                if b:
                    tile_b(n, "mj", 0, VB[0])
                if a:
                    exp("H3", n, 0)
                    exp("H3", n, 1)
                    exp("H3", n, 2)
                    t_head(n, 1, 0)
                    high("H2", n, 3)
                    elu_exp("H2", n, 0)
                    elu_exp("H2", n, 1)
                    relu("H3", n, 3)
                if b:
                    tile_b(n, "mj", 1, VB[0])
                if a:
                    t_head(n, 1, 1)
                    v_head(n, 3, 0)
                    exp("H3", n, 3)
                    high("H3", n, 0)
                    elu_exp("H2", n, 2)
                    high("H3", n, 1)
                    elu_exp("H2", n, 3)
                    v_head(n, 3, 1)
                if pre:
                    x0_turn(n, 0)
                    x0_turn(n, 1)
                if a:
                    t_head(n, 2, 0)
                    high("H3", n, 2)
                    t_head(n, 2, 1)
                    high("H3", n, 3)
                if b:
                    tile_b(n, "x3T", 0, xTb[0])
                if a:
                    elu_exp("H3", n, 0)
                    elu_exp("H3", n, 1)
                if pre:
                    relu("L0", n, 0)
                    relu("L0", n, 1)
                    split_a(n, "V0", V0[0][:, :])
                    relu("L0", n, 2)
                if b:
                    tile_b(n, "x3T", 1, xTb[0])
                if a:
                    elu_exp("H3", n, 2)
                if pre:
                    relu("L0", n, 3)
                    exp("L0", n, 0)
                if a:
                    elu_exp("H3", n, 3)
                if pre:
                    exp("L0", n, 1)
                    exp("L0", n, 2)
                    high("L0", n, 0)
                    high("L0", n, 1)
                    exp("L0", n, 3)
                if a:
                    t_head(n, 3, 0)
                    t_head(n, 3, 1)
                if b:
                    relu("L3", n, 0)
                    relu("L3", n, 1)
                    relu("L3", n, 2)
                if pre:
                    high("L0", n, 2)
                if b:
                    exp("L3", n, 0)
                    exp("L3", n, 1)
                    relu("L3", n, 3)
                    exp("L3", n, 2)
                if pre:
                    high("L0", n, 3)
                if b:
                    tile_b(n, "V3", 0, VB[0])
                    exp("L3", n, 3)
                    tile_b(n, "V3", 1, VB[0])
                    high("L3", n, 0)
                    high("L3", n, 1)
                if a:
                    relu("O1", n, 0)
                if b:
                    high("L3", n, 2)
                if a:
                    relu("O1", n, 1)
                if b:
                    high("L3", n, 3)
                if a:
                    relu("O1", n, 2)
                    relu("O1", n, 3)
                    exp("O1", n, 0)
                    exp("O1", n, 1)
                    exp("O1", n, 2)
                    exp("O1", n, 3)
                    v_out(n, 0)
                    v_out(n, 1)

            body(-1)
            body(0)
            with act.Fori(1, B - 1) as n:
                body(n)
            body(B - 1)
            body(B)

        @block.tensor
        def _(pe):
            def product(dst, left, right, first=True, last=True):
                passes = [(0, 0), (0, 1), (1, 0)]
                for m, (a, b) in enumerate(passes):
                    mm = pe.matmul(dst, left(a), right(b), start=first and m == 0, stop=last and m == 2)
                return mm

            def sum_of(dst, terms):
                for m, (left, right) in enumerate(terms):
                    mm = product(dst, left, right, m == 0, m == len(terms) - 1)
                return mm

            pe.wait_ge(prep_pool, 2)
            pe.wait_ge(prep_dve, prepared("edges"))
            edges = work[:, 4:6, :].rearrange("p a n -> p (a n)").rearrange("p (i n) -> p i n", n=N)
            for j in range(NI):
                for i in range(NI):
                    mm = pe.transpose(bank[j][:, i * P:(i + 1) * P], edges[:, i, j * P:(j + 1) * P], ident[:, :])
            mm.then_inc(prep_pe, 1)
            pe.wait_ge(loaded["wl"], 16)
            wl = work[:, 7, :].rearrange("p (k n) -> p k n", n=2 * D)
            for c in range(2 * KD):
                for o in range(KD):
                    mm = pe.transpose(bank[4 + c][:, o * P:(o + 1) * P], wl[:, o, c * P:(c + 1) * P], ident[:, :])
                mm.then_inc(prep_pe, 1)
            pe.wait_ge(prep_dve, len(PREP))

            def f_rows(stage, n):
                raw, h, nh = f_of(stage)[0][0], f_of(stage)[1], f_of(stage)[2]
                if stage == "L3":
                    pe.wait_ge(dve_b, DVE_B.at(n, "f3"))
                else:
                    pe.wait_ge(dve_a, DVE_A.at(n, {"L0": "f0", "O1": "fO"}.get(stage, "fH")))
                if kind(n) != "pre":
                    pe.wait_ge(g_ready, UNITS.at(n, (stage, 0)) - 1)
                for i in range(NI):
                    mm = pe.transpose(F_bank[:, i * P:(i + 1) * P],
                                      raw[:, i, nh + h:nh + h + 1].to_broadcast([P, P]), ident[:, :])
                mm.then_inc(f_row, 1)

            def turn(stage, n, i):
                u = UNITS.at(n, (stage, i))
                pe.wait_ge(p_ready, u)
                if kind(n) != "pre" or i >= T_RING:
                    pe.wait_ge(low_done, u - T_RING)
                for j in range(NI):
                    mm = pe.transpose(T_bank[i % T_RING][:, j * P:(j + 1) * P], Pm[:, i, j * P:(j + 1) * P],
                                      ident[:, :])
                mm.then_inc(t_full, 1)

            def weighted(stage, n, i):
                V, width = v_of(stage)
                pe.wait_ge(low_done, UNITS.at(n, (stage, i)))
                if i == 0:
                    if stage == "L3":
                        pe.wait_ge(dve_b, DVE_B.at(n, ("V3", 1)))
                    else:
                        step = {"L0": "V0", "O1": ("VO", 1)}.get(stage, (f"V{stage[1]}H", 1))
                        pe.wait_ge(dve_a, DVE_A.at(n, step))
                m, s = (n, stage) if i >= O_RING else group_before(n, stage)
                before = (s, (i - O_RING) % NI)
                if kind(n) != "pre" or i >= O_RING:
                    if s in ELU:
                        pe.wait_ge(o_act, ELU_UNITS.at(m, before))
                    else:
                        pe.wait_ge(o_dve, UNITS.at(m, before))
                sum_of(O_bank[i % O_RING][:, 0:width],
                       [(lambda a, j=j: PT[a][:, i % T_RING, j, :], lambda b, j=j: tiles(V[b], width)[:, j, :])
                        for j in range(NI)]).then_inc(o_full, 1)

            def free_a(n, step):
                steps = PE_A.steps[kind(n)]
                m = steps.index(step)
                if m >= 2:
                    pe.wait_ge(dve_a, DVE_A.at(n, steps[m - 2]))
                elif kind(n) != "pre":
                    last = PE_A.steps["pre" if kind(n) == "first" else "loop"]
                    pe.wait_ge(dve_a, DVE_A.at(n - 1, last[m - 2]))
                return a_bank_of(n, step)

            def free_b(n, step):
                steps = PE_B.steps[kind(n)]
                m = steps.index(step)
                if m:
                    pe.wait_ge(dve_b, DVE_B.at(n, steps[m - 1]))
                return B_bank

            def transposed(free, done, n, step, src, k):
                dst = free(n, step)
                for i in range(NI):
                    mm = pe.transpose(dst[:, i * P:(i + 1) * P], src[:, i, k * P:(k + 1) * P], ident[:, :])
                mm.then_inc(done, 1)

            def rows_times(dst, left, nk, right, i):
                return sum_of(dst, [(lambda a, k=k: tiles(left[a], N)[:, k, i * P:(i + 1) * P],
                                     lambda b, k=k: right(b)[:, k, :]) for k in range(nk)])

            def scalars(free, done, n, step, left, s):
                nk, w = WA[s][1:]
                dst = free(n, step)
                for i in range(NI):
                    for k in range(nk):
                        for part in range(2):
                            mm = pe.matmul(dst[:, i * 2 * w:(i + 1) * 2 * w].rearrange("p (s c) -> p s c", s=2),
                                           tiles(left[part], N)[:, k, i * P:(i + 1) * P], wa[:, :, wa_of(s, k)],
                                           start=k == part == 0, stop=k == nk - 1 and part == 1)
                mm.then_inc(done, 1)

            def half(free, done, n, name, m, left, nk, right):
                dst = free(n, (name, m))
                for i in (2 * m, 2 * m + 1):
                    mm = rows_times(dst[:, i % 2 * D:(i % 2 + 1) * D], left, nk, right, i)
                mm.then_inc(done, 1)

            def x1_turn(n, c):
                pe.wait_ge(dve_a, DVE_A.at(n - 1, "ln0_out"))
                transposed(free_a, pe_a, n, ("x1T", c), x1, c)

            def scalars_a(n, step):
                before, left, s = {"fH": (("x1T", 1), xTa, "H"), "f0": (("x0T", 1), xTa, "L0"),
                                   "fO": (("T3H", 1), hT, "O1")}[step]
                pe.wait_ge(dve_a, DVE_A.at(n, before))
                scalars(free_a, pe_a, n, step, left, s)

            def v_head(n, h, m):
                pe.wait_ge(dve_a, DVE_A.at(n, ("x1T", 1)))
                half(free_a, pe_a, n, f"V{h}H", m, xTa, KD,
                     lambda b: wh[b][:, :].rearrange("p (k c) -> p k c", k=KD)[:, :, h * D:(h + 1) * D])

            def t_head(n, h, c):
                pe.wait_ge(dve_a, DVE_A.at(n, f"h{h}"))
                transposed(free_a, pe_a, n, (f"T{h}H", c), hx, c)

            def x0_turn(n, c):
                pe.wait_ge(x_loaded, X_LOADS.at(n, "x") * 16)
                transposed(free_a, pe_a, n, ("x0T", c), x0, c)

            def v_first(n):
                pe.wait_ge(dve_a, DVE_A.at(n, ("x0T", 1)))
                dst = free_a(n, "V0")
                for i in range(NI):
                    mm = rows_times(dst[:, i * D0:(i + 1) * D0], xTa, KD, lambda b: tiles(w0[b], D0), i)
                mm.then_inc(pe_a, 1)

            def v_out(n, m):
                pe.wait_ge(dve_a, DVE_A.at(n, ("T3H", 1)))
                half(free_a, pe_a, n, "VO", m, hT, KH, lambda b: tiles(wo[b], D))

            def out_turn(n, k):
                pe.wait_ge(dve_b, DVE_B.at(n, "h1b"))
                transposed(free_b, pe_b, n, ("outT", k), hb, k)

            def hidden(n, o):
                pe.wait_ge(dve_b, DVE_B.at(n, ("outT", 1)))
                dst = free_b(n, ("ffn1", o))
                sum_of(dst[:, :], [(lambda a, k=k: tiles(w1[a], D)[:, k, o * P:(o + 1) * P],
                                    lambda b, k=k: tiles(xTb[b], N)[:, k, :]) for k in range(KD)])\
                    .then_inc(pe_b, 1)

            def ffn_out(n, m):
                pe.wait_ge(pool_b, POOL_B.at(n, ("glo", 1)))
                half(free_b, pe_b, n, "ffn2", m, VB, KD, lambda b: tiles(w2[b], D))

            def x2_turn(n, k):
                pe.wait_ge(dve_b, DVE_B.at(n, "ln1o_out"))
                transposed(free_b, pe_b, n, ("x2T", k), xb, k)

            def message(n, name, m):
                pe.wait_ge(dve_b, DVE_B.at(n, ("x2T", 1)))
                half(free_b, pe_b, n, name, m, xTb, KD, lambda b: tiles((wi if name == "mi" else wj)[b], D))

            def neighbours(n, m):
                pe.wait_ge(dve_b, DVE_B.at(n, ("mj", 1)))
                dst = free_b(n, ("Amj", m))
                for i in (2 * m, 2 * m + 1):
                    for t in range(2 * NI):
                        mm = pe.matmul(dst[:, i % 2 * D:(i % 2 + 1) * D], adjT[:, t // 2, i * P:(i + 1) * P],
                                       tiles(VB[t % 2], D)[:, t // 2, :], start=t == 0, stop=t == 2 * NI - 1)
                mm.then_inc(pe_b, 1)

            def x3_turn(n, c):
                pe.wait_ge(dve_b, DVE_B.at(n, "ln2_out"))
                transposed(free_b, pe_b, n, ("x3T", c), xb, c)

            def scalars_b(n):
                pe.wait_ge(dve_b, DVE_B.at(n, ("x3T", 1)))
                scalars(free_b, pe_b, n, "f3", xTb, "L3")

            def v_last(n, m):
                pe.wait_ge(dve_b, DVE_B.at(n, ("x3T", 1)))
                half(free_b, pe_b, n, "V3", m, xTb, KD, lambda b: tiles(w3[b], D))

            def body(n):
                k = kind(n)
                a, b, pre = k in A_KINDS, k in B_KINDS, k in PRE_KINDS
                if b:
                    turn("O1", n - 1, 0)
                    turn("O1", n - 1, 1)
                if a:
                    x1_turn(n, 0)
                    x1_turn(n, 1)
                if b:
                    turn("O1", n - 1, 2)
                    weighted("O1", n - 1, 0)
                    turn("O1", n - 1, 3)
                    weighted("O1", n - 1, 1)
                    weighted("O1", n - 1, 2)
                if a:
                    scalars_a(n, "fH")
                if b:
                    weighted("O1", n - 1, 3)
                if a:
                    f_rows("H0", n)
                    v_head(n, 0, 0)
                    v_head(n, 0, 1)
                if b:
                    out_turn(n, 0)
                if a:
                    f_rows("H1", n)
                if b:
                    out_turn(n, 1)
                if a:
                    v_head(n, 1, 0)
                if b:
                    hidden(n, 0)
                if a:
                    turn("H0", n, 0)
                    turn("H0", n, 1)
                    v_head(n, 1, 1)
                if b:
                    hidden(n, 1)
                if a:
                    f_rows("H2", n)
                    turn("H0", n, 2)
                    turn("H0", n, 3)
                    weighted("H0", n, 0)
                    weighted("H0", n, 1)
                if b:
                    ffn_out(n, 0)
                if a:
                    turn("H1", n, 0)
                    turn("H1", n, 1)
                    v_head(n, 2, 0)
                if b:
                    ffn_out(n, 1)
                if a:
                    v_head(n, 2, 1)
                    f_rows("H3", n)
                    weighted("H0", n, 2)
                    weighted("H0", n, 3)
                    weighted("H1", n, 0)
                    turn("H1", n, 2)
                    weighted("H1", n, 1)
                    turn("H1", n, 3)
                    turn("H2", n, 0)
                    turn("H2", n, 1)
                    t_head(n, 0, 0)
                    t_head(n, 0, 1)
                if b:
                    x2_turn(n, 0)
                if a:
                    weighted("H1", n, 2)
                    weighted("H1", n, 3)
                if b:
                    x2_turn(n, 1)
                if a:
                    turn("H2", n, 2)
                    weighted("H2", n, 0)
                if b:
                    message(n, "mj", 0)
                if a:
                    weighted("H2", n, 1)
                if b:
                    message(n, "mi", 0)
                if a:
                    t_head(n, 1, 0)
                    t_head(n, 1, 1)
                    turn("H2", n, 3)
                    turn("H3", n, 0)
                if b:
                    message(n, "mj", 1)
                if a:
                    v_head(n, 3, 0)
                    turn("H3", n, 1)
                    weighted("H2", n, 2)
                if b:
                    message(n, "mi", 1)
                if a:
                    weighted("H2", n, 3)
                if b:
                    neighbours(n, 0)
                if a:
                    v_head(n, 3, 1)
                if pre:
                    x0_turn(n, 0)
                if b:
                    neighbours(n, 1)
                if pre:
                    x0_turn(n, 1)
                if a:
                    weighted("H3", n, 0)
                    t_head(n, 2, 0)
                    turn("H3", n, 2)
                    weighted("H3", n, 1)
                if pre:
                    scalars_a(n, "f0")
                if a:
                    t_head(n, 2, 1)
                    turn("H3", n, 3)
                if b:
                    x3_turn(n, 0)
                if pre:
                    f_rows("L0", n)
                    v_first(n)
                if a:
                    weighted("H3", n, 2)
                if b:
                    x3_turn(n, 1)
                if a:
                    weighted("H3", n, 3)
                if b:
                    scalars_b(n)
                if pre:
                    turn("L0", n, 0)
                    turn("L0", n, 1)
                if a:
                    t_head(n, 3, 0)
                if b:
                    f_rows("L3", n)
                if a:
                    t_head(n, 3, 1)
                if pre:
                    weighted("L0", n, 0)
                    turn("L0", n, 2)
                    weighted("L0", n, 1)
                if b:
                    v_last(n, 0)
                if pre:
                    turn("L0", n, 3)
                if a:
                    scalars_a(n, "fO")
                if b:
                    turn("L3", n, 0)
                    turn("L3", n, 1)
                    v_last(n, 1)
                if pre:
                    weighted("L0", n, 2)
                    weighted("L0", n, 3)
                if a:
                    f_rows("O1", n)
                if b:
                    weighted("L3", n, 0)
                    turn("L3", n, 2)
                    weighted("L3", n, 1)
                    turn("L3", n, 3)
                    weighted("L3", n, 2)
                if a:
                    v_out(n, 0)
                if b:
                    weighted("L3", n, 3)
                if a:
                    v_out(n, 1)

            body(-1)
            body(0)
            with pe.Fori(1, B - 1) as n:
                body(n)
            body(B - 1)
            body(B)

        @block.vector
        def _(dve):
            edges = work[:, 4:6, :].rearrange("p a n -> p (a n)").rearrange("p (i n) -> p i n", n=N)
            dots = itertools.count()
            dve.wait_ge(loaded["adj"], 16)
            dve.tensor_copy(edges, work[:, 2:4, :].rearrange("p a n -> p (a n)").bitcast(i32)
                            .rearrange("p (i n) -> p i n", n=N)).then_inc(prep_dve, 1)
            dve.wait_ge(prep_dve, prepared("edges"))
            dve.tensor_scalar(mask[:, :, :], edges, -NEG, NEG, ALU.mult, ALU.add).then_inc(prep_dve, 1)
            dve.tensor_reduce(deg[:, :], edges, AX.X, ALU.add).then_inc(prep_dve, 1)
            dve.wait_ge(prep_dve, prepared("deg"))
            dve.tensor_scalar(has_edge[:, :], deg[:, :], 1.0, None, ALU.min).then_inc(prep_dve, 1)

            def dot_columns(s, k, col, w, a):
                m = next(dots)
                if m >= NI:
                    dve.wait_ge(dot_done, m - NI + 1)
                dve.tensor_tensor_reduce(deg_b[:, m % NI, 0:w.shape[-1]], w, a, 1.0, 0.0, ALU.mult, ALU.add,
                                                wa_raw[:, wa_of(s, k)][:, col:col + 1]).then_inc(dot_done, 1)

            dve.wait_ge(loaded["wh"], 32)
            dve.wait_ge(loaded["ah"], 16)
            a_heads = work[:, 0:2, :].rearrange("p a n -> p (a n)")
            for k in range(KD):
                for h in range(H):
                    for c in range(2):
                        dot_columns("H", k, c * H + h, GP[:, (k * H + h) * D:(k * H + h + 1) * D],
                                           a_heads[:, (2 * h + c) * D:(2 * h + c + 1) * D])

            def low_part(name, dst, src):
                dve.wait_ge(prep_act, PREP_ACT.index(name) + 1)
                dve.tensor_tensor(dst[1], src, dst[0].bitcast(f32), ALU.subtract).then_inc(prep_dve, 1)

            def flat(w):
                return [part[:, :] for part in w]

            low_part("wh", flat(wh), GP[:, 0:NI * N])
            low_part("wo", flat(wo), GP[:, NI * N:2 * NI * N])
            low_part("w1", flat(w1), work[:, 6, 0:KD * D])
            low_part("w2", flat(w2), work[:, 6, KD * D:2 * KD * D])
            dve.wait_ge(prep_pe, 1)
            for j in range(NI):
                last = dve.tensor_copy(adjT[:, j, :], bank[j][:, :])
            last.then_inc(prep_dve, 1)
            for c in range(2 * KD):
                low_part(f"wl{c}", [tiles(part, D)[:, c % KD, :] for part in (wi, wj)[c // KD]], bank[4 + c][:, 0:D])
            dve.wait_ge(loaded["a"], 64)
            for k in range(KH):
                for c in range(2):
                    dot_columns("O1", k, c, GP[:, NI * N + k * D:NI * N + (k + 1) * D],
                                       GP[:, 1280 + c * D:1280 + (c + 1) * D])
            dve.wait_ge(loaded["w0"], 16)
            for k in range(KD):
                for c in range(2):
                    dot_columns("L0", k, c, GP[:, k * D0:(k + 1) * D0], GP[:, 1024 + c * D0:1024 + (c + 1) * D0])
            low_part("w0", flat(w0), GP[:, 0:KD * D0])
            dve.wait_ge(loaded["w3"], 16)
            for k in range(KD):
                for c, a in enumerate((GP[:, 1792:2048], work[:, 0, 0:D])):
                    dot_columns("L3", k, c, GP[:, 256 + k * D:256 + (k + 1) * D], a)
            low_part("w3", flat(w3), GP[:, 256:256 + KD * D])
            dve.wait_ge(dot_done, next(dots))
            dve.tensor_copy(wa[:, 0, :], wa_raw[:, :]).then_inc(prep_dve, 1)
            dve.wait_ge(prep_dve, prepared("wa_high"))
            dve.tensor_tensor(wa[:, 1, :], wa_raw[:, :], wa[:, 0, :].bitcast(f32), ALU.subtract)\
                .then_inc(prep_dve, 1)
            dve.wait_ge(loaded["bl2"], 16)
            dve.wait_ge(loaded["rows"], 64)
            for i in range(NI):
                dve.tensor_scalar(deg_b[:, i, :], GP[:, 768:1024], deg[:, i:i + 1], None, ALU.mult)
            dve.tensor_scalar(b2m1[:, :], b2m1[:, :], -1.0, None, ALU.add).then_inc(prep_dve, 1)
            dve.wait_ge(prep_dve, len(PREP))

            def settle(place):
                dve.memset(settled[:, place:place + 1], 0.0)

            def mask_max(stage, n, i):
                u = UNITS.at(n, (stage, i))
                if i == 0:
                    dve.wait_ge(f_row, GROUPS.at(n, stage))
                if kind(n) != "pre":
                    dve.wait_ge(p_ready, u - NI)
                settle(i)
                dve.tensor_tensor_reduce(G[:, i, :], F_bank[:, :], mask[:, i, :], alpha_of(stage), -3e38,
                                         ALU.add, ALU.max, gmax[:, i:i + 1]).then_inc(g_ready, 1)

            def shifts(stage, n):
                (_, fa, _), h, _ = f_of(stage)
                g = GROUPS.at(n, stage)
                dve.wait_ge(g_ready, UNITS.at(n, (stage, NI - 1)))
                dve.tensor_tensor(gtop[:, :], gmax[:, :], fa[:, :, h], ALU.add).then_inc(tops, 1)
                dve.wait_ge(tops, 2 * g - 1)
                dve.scalar_tensor_tensor(gleaky[:, :], gtop[:, :], 1 / alpha_of(stage), gtop[:, :],
                                         ALU.mult, ALU.max).then_inc(tops, 1)
                dve.wait_ge(tops, 2 * g)
                dve.tensor_tensor(shift[:, SLOTS.index(stage), :], fa[:, :, h], gleaky[:, :], ALU.subtract)\
                    .then_inc(shift_ready, 1)

            def inverses(stage, n):
                s = SLOTS.index(stage)
                dve.wait_ge(p_ready, UNITS.at(n, (stage, NI - 1)))
                if stage == "L3":
                    dve.reciprocal(row_inv[:, s, :], row_sum[:, s, :]).then_inc(l3_inv, 1)
                    dve.wait_ge(l3_inv, n)
                    dve.tensor_tensor(row_inv[:, s, :], row_inv[:, s, :], has_edge[:, :], ALU.mult)\
                        .then_inc(inv_ready, 1)
                else:
                    dve.reciprocal(row_inv[:, s, :], row_sum[:, s, :]).then_inc(inv_ready, 1)

            def low(stage, n, i):
                dve.wait_ge(high_done, UNITS.at(n, (stage, i)))
                dve.tensor_tensor(PT[1][:, i % T_RING, :, :],
                                  T_bank[i % T_RING][:, :].rearrange("p (j n) -> p j n", n=P),
                                  PT[0][:, i % T_RING, :, :].bitcast(f32), ALU.subtract).then_inc(low_done, 1)

            def evacuate(stage, n, i):
                inv = row_inv[:, SLOTS.index(stage), i:i + 1]
                O = O_bank[i % O_RING]
                if i == 0:
                    dve.wait_ge(inv_ready, GROUPS.at(n, stage))
                dve.wait_ge(o_full, UNITS.at(n, (stage, i)))
                if stage == "L0":
                    dve.scalar_tensor_tensor(x0[:, i, 0:D0], O[:, 0:D0], inv, x0[:, i, 0:D0], ALU.mult, ALU.add)\
                        .then_inc(o_dve, 1)
                elif stage == "L3":
                    dve.scalar_tensor_tensor(xb[:, i, :], O[:, 0:D], inv, xb[:, i, :], ALU.mult, ALU.add)\
                        .then_inc(o_dve, 1)
                else:
                    if i == 0 and stage in HEADS[1:]:
                        dve.wait_ge(pe_a, PE_A.at(n, (f"T{int(stage[1]) - 1}H", 1)))
                    dve.tensor_scalar((hb if stage == "O1" else hx)[:, i, :], O[:, 0:D], inv, 0.0,
                                      ALU.mult, ALU.max).then_inc(o_dve, 1)

            def split_a(n, step, dst, high_part, bias=0.0):
                dve.wait_ge(act_a, ACT_A.at(n, step))
                dve.scalar_tensor_tensor(dst, a_bank_of(n, step)[:, :], bias, high_part.bitcast(f32),
                                         ALU.add, ALU.subtract).then_inc(dve_a, 1)

            def split_b(n, step, dst, high_part, bias=0.0):
                dve.wait_ge(act_b, ACT_B.at(n, step))
                dve.scalar_tensor_tensor(dst, B_bank[:, :], bias, high_part.bitcast(f32),
                                         ALU.add, ALU.subtract).then_inc(dve_b, 1)

            def tile_a(n, name, k, dst, bias=0.0):
                split_a(n, (name, k), tiles(dst[1], N)[:, k, :], tiles(dst[0], N)[:, k, :], bias)

            def tile_b(n, name, k, dst, bias=0.0):
                split_b(n, (name, k), tiles(dst[1], N)[:, k, :], tiles(dst[0], N)[:, k, :], bias)

            def t_head(n, h, c):
                k = KD * h + c
                split_a(n, (f"T{h}H", c), tiles(hT[1], N)[:, k, :], tiles(hT[0], N)[:, k, :], -1.0)

            def elu(n, h):
                dve.wait_ge(o_act, ELU_UNITS.at(n, (f"H{h}", NI - 1)))
                dve.wait_ge(o_dve, UNITS.at(n, (f"H{h}", NI - 1)))
                dve.scalar_tensor_tensor(hx, he, 1.0, hx, ALU.min, ALU.add).then_inc(dve_a, 1)

            def scalars(n, s, step, stream="a"):
                raw, fa, fb = fcols[s]
                nh, alpha = WA[s][2] // 2, ALPHA.get(s, ALPHA["L1"])
                src, pe_sem, pe_tally, done, tally = (
                    (a_bank_of(n, step), pe_a, PE_A, dve_a, DVE_A) if stream == "a" else
                    (B_bank, pe_b, PE_B, dve_b, DVE_B))
                F = src[:, 0:NI * 4 * nh].rearrange("p (i s c) -> p i s c", i=NI, s=2)
                dve.wait_ge(pe_sem, pe_tally.at(n, step))
                dve.tensor_copy(raw[:, :, :], F[:, :, 0, :]).then_inc(done, 1)
                dve.wait_ge(done, tally.at(n, f"{step}_high"))
                dve.tensor_tensor(raw[:, :, :], raw[:, :, :], F[:, :, 1, :], ALU.add).then_inc(done, 1)
                dve.wait_ge(done, tally.at(n, f"{step}_raw"))
                dve.tensor_scalar(fa[:, :, :], raw[:, :, 0:nh], alpha, None, ALU.mult)
                dve.tensor_scalar(fb[:, :, :], raw[:, :, 0:nh], 1 - alpha, None, ALU.mult).then_inc(done, 1)

            def first_sum(n):
                dve.wait_ge(act_a, ACT_A.at(n, "V0"))
                V = a_bank_of(n, "V0")[:, :]
                dve.tensor_tensor(x0[:, :, D0:D], V.rearrange("p (i d) -> p i d", d=D0), x0[:, :, D0:D], ALU.add)\
                    .then_inc(dve_a, 1)

            def v_first(n):
                dve.wait_ge(act_a, ACT_A.at(n, "V0"))
                dve.tensor_tensor(V0[1][:, :], a_bank_of(n, "V0")[:, :], V0[0][:, :].bitcast(f32), ALU.subtract)\
                    .then_inc(dve_a, 1)

            def counts(name):
                return ((norm["a"], dve_a, DVE_A, pool_a, POOL_A) if name == "ln0" else
                        (norm["b"], dve_b, DVE_B, pool_b, POOL_B))

            def norm_stats(name, n, src):
                (bn, _, _, _), steps, tally, _, _ = counts(name)
                if name == "ln0":
                    dve.wait_ge(dve_a, DVE_A.at(n, "x0sum"))
                    dve.wait_ge(o_dve, UNITS.at(n, ("L0", NI - 1)))
                elif name == "ln3":
                    dve.wait_ge(o_dve, UNITS.at(n, ("L3", NI - 1)))
                else:
                    dve.wait_ge(dve_b, DVE_B.at(n, {"ln1": ("ffn2", 1), "ln1o": "res1", "ln2": ("Amj", 1)}[name]))
                for i in range(NI):
                    last = dve.bn_stats(bn[:, i, :], src[:, i, :])
                last.then_inc(steps, 1)

            def norm_aggr(name, n):
                (bn, mv, _, _), steps, tally, _, _ = counts(name)
                dve.wait_ge(steps, tally.at(n, f"{name}_stats"))
                settle(NI + NORMS.index(name))
                for i in range(NI):
                    last = dve.bn_aggr(mv[:, i, :], bn[:, i, :])
                last.then_inc(steps, 1)

            def norm_var(name, n):
                (_, mv, var, _), steps, tally, _, _ = counts(name)
                dve.wait_ge(steps, tally.at(n, f"{name}_aggr"))
                dve.tensor_scalar(var[:, :], mv[:, :, 1], EPS, None, ALU.add).then_inc(steps, 1)

            def norm_out(name, n, src, dst):
                (_, mv, _, rs), steps, tally, rsteps, rtally = counts(name)
                if name == "ln0" and kind(n) in A_KINDS:
                    dve.wait_ge(pool_a, POOL_A.at(n, "x1b"))
                dve.wait_ge(rsteps, rtally.at(n, name))
                for i in range(NI):
                    last = dve.tensor_scalar(dst[:, i, :], src[:, i, :], mv[:, i, 0:1], rs[:, i:i + 1],
                                             ALU.subtract, ALU.mult)
                last.then_inc(steps, 1)

            def elu_out(n):
                dve.wait_ge(o_act, ELU_UNITS.at(n - 1, ("O1", NI - 1)))
                dve.wait_ge(o_dve, UNITS.at(n - 1, ("O1", NI - 1)))
                dve.scalar_tensor_tensor(hb, eb, 1.0, hb, ALU.min, ALU.add).then_inc(dve_b, 1)

            def hidden(n, o):
                dve.wait_ge(act_b, ACT_B.at(n, ("ffn1", o)))
                dve.tensor_scalar(eb_wide[:, o, :], B_bank[:, :], b1c[:, o:o + 1], 0.0, ALU.add, ALU.max)\
                    .then_inc(dve_b, 1)

            def add_bank(n, name, m, dst):
                if name == "ffn2":
                    dve.wait_ge(pool_b, POOL_B.at(n, "ob"))
                else:
                    dve.wait_ge(dve_b, DVE_B.at(n, ("mi", m)))
                dve.wait_ge(pe_b, PE_B.at(n, (name, m)))
                part = dst[:, 2 * m:2 * m + 2, :]
                dve.tensor_tensor(part, B_bank[:, :].rearrange("p (i d) -> p i d", d=D), part, ALU.add)\
                    .then_inc(dve_b, 1)

            def residual(n):
                dve.wait_ge(pool_b, POOL_B.at(n, "xg"))
                dve.wait_ge(pool_a, POOL_A.at(n - 1, "x1b"))
                dve.tensor_tensor(xb, eb, x1b, ALU.add).then_inc(dve_b, 1)

            def own_message(n, m):
                dve.wait_ge(pool_b, POOL_B.at(n, "xb"))
                dve.wait_ge(pe_b, PE_B.at(n, ("mi", m)))
                for i in (2 * m, 2 * m + 1):
                    last = dve.scalar_tensor_tensor(xb[:, i, :], B_bank[:, i % 2 * D:(i % 2 + 1) * D],
                                                    deg[:, i:i + 1], xb[:, i, :], ALU.mult, ALU.add)
                last.then_inc(dve_b, 1)

            def body(n):
                k = kind(n)
                a, b, pre = k in A_KINDS, k in B_KINDS, k in PRE_KINDS
                if b:
                    low("O1", n - 1, 0)
                    low("O1", n - 1, 1)
                    inverses("O1", n - 1)
                if a:
                    tile_a(n, "x1T", 0, xTa)
                    tile_a(n, "x1T", 1, xTa)
                if b:
                    evacuate("O1", n - 1, 0)
                    low("O1", n - 1, 2)
                    evacuate("O1", n - 1, 1)
                    low("O1", n - 1, 3)
                    evacuate("O1", n - 1, 2)
                if a:
                    scalars(n, "H", "fH")
                if b:
                    evacuate("O1", n - 1, 3)
                if a:
                    mask_max("H0", n, 0)
                if b:
                    elu_out(n)
                if a:
                    mask_max("H0", n, 1)
                    mask_max("H0", n, 2)
                    mask_max("H0", n, 3)
                if b:
                    tile_b(n, "outT", 0, xTb, -1.0)
                if a:
                    shifts("H0", n)
                    tile_a(n, "V0H", 0, VH[0])
                    tile_a(n, "V0H", 1, VH[0])
                if b:
                    tile_b(n, "outT", 1, xTb, -1.0)
                if a:
                    mask_max("H1", n, 0)
                    mask_max("H1", n, 1)
                    mask_max("H1", n, 2)
                    mask_max("H1", n, 3)
                if b:
                    hidden(n, 0)
                if a:
                    shifts("H1", n)
                    inverses("H0", n)
                    low("H0", n, 0)
                    low("H0", n, 1)
                    mask_max("H2", n, 0)
                if b:
                    hidden(n, 1)
                if a:
                    evacuate("H0", n, 0)
                    mask_max("H2", n, 1)
                    low("H0", n, 2)
                    evacuate("H0", n, 1)
                    low("H0", n, 3)
                    tile_a(n, "V1H", 0, VH[1])
                if b:
                    add_bank(n, "ffn2", 0, hb)
                if a:
                    tile_a(n, "V1H", 1, VH[1])
                    mask_max("H2", n, 2)
                    inverses("H1", n)
                    mask_max("H2", n, 3)
                    shifts("H2", n)
                if b:
                    add_bank(n, "ffn2", 1, hb)
                    norm_stats("ln1", n, hb)
                    norm_aggr("ln1", n)
                    norm_var("ln1", n)
                if a:
                    mask_max("H3", n, 0)
                    evacuate("H0", n, 2)
                    low("H1", n, 0)
                if b:
                    norm_out("ln1", n, hb, eb)
                if a:
                    evacuate("H0", n, 3)
                    low("H1", n, 1)
                    elu(n, 0)
                    low("H1", n, 2)
                if b:
                    residual(n)
                    norm_stats("ln1o", n, xb)
                    norm_aggr("ln1o", n)
                    norm_var("ln1o", n)
                if a:
                    low("H1", n, 3)
                    tile_a(n, "V2H", 0, VH[0])
                    tile_a(n, "V2H", 1, VH[0])
                if b:
                    norm_out("ln1o", n, xb, xb)
                if a:
                    evacuate("H1", n, 0)
                    evacuate("H1", n, 1)
                    inverses("H2", n)
                    mask_max("H3", n, 1)
                if b:
                    tile_b(n, "x2T", 0, xTb)
                if a:
                    mask_max("H3", n, 2)
                    evacuate("H1", n, 2)
                    low("H2", n, 0)
                    evacuate("H1", n, 3)
                    mask_max("H3", n, 3)
                if b:
                    tile_b(n, "x2T", 1, xTb)
                if a:
                    elu(n, 1)
                    low("H2", n, 1)
                    low("H2", n, 2)
                if b:
                    tile_b(n, "mj", 0, VB)
                if a:
                    shifts("H3", n)
                    t_head(n, 0, 0)
                    t_head(n, 0, 1)
                if b:
                    own_message(n, 0)
                if a:
                    evacuate("H2", n, 0)
                    evacuate("H2", n, 1)
                    t_head(n, 1, 0)
                    low("H2", n, 3)
                if b:
                    tile_b(n, "mj", 1, VB)
                if a:
                    t_head(n, 1, 1)
                    tile_a(n, "V3H", 0, VH[1])
                    inverses("H3", n)
                    evacuate("H2", n, 2)
                    low("H3", n, 0)
                if b:
                    own_message(n, 1)
                if a:
                    evacuate("H2", n, 3)
                    low("H3", n, 1)
                    elu(n, 2)
                if b:
                    add_bank(n, "Amj", 0, xb)
                if a:
                    tile_a(n, "V3H", 1, VH[1])
                if pre:
                    tile_a(n, "x0T", 0, xTa)
                if b:
                    add_bank(n, "Amj", 1, xb)
                    norm_stats("ln2", n, xb)
                if pre:
                    tile_a(n, "x0T", 1, xTa)
                if b:
                    norm_aggr("ln2", n)
                    norm_var("ln2", n)
                if a:
                    low("H3", n, 2)
                    t_head(n, 2, 0)
                if b:
                    norm_out("ln2", n, xb, xb)
                if pre:
                    scalars(n, "L0", "f0")
                if a:
                    evacuate("H3", n, 0)
                    evacuate("H3", n, 1)
                    t_head(n, 2, 1)
                if pre:
                    mask_max("L0", n, 0)
                    mask_max("L0", n, 1)
                if a:
                    low("H3", n, 3)
                if b:
                    tile_b(n, "x3T", 0, xTb)
                if pre:
                    mask_max("L0", n, 2)
                    mask_max("L0", n, 3)
                if a:
                    evacuate("H3", n, 2)
                if pre:
                    shifts("L0", n)
                if b:
                    tile_b(n, "x3T", 1, xTb)
                if a:
                    evacuate("H3", n, 3)
                if pre:
                    first_sum(n)
                    v_first(n)
                if a:
                    elu(n, 3)
                if b:
                    scalars(n, "L3", "f3", "b")
                if pre:
                    low("L0", n, 0)
                    low("L0", n, 1)
                if b:
                    mask_max("L3", n, 0)
                    mask_max("L3", n, 1)
                    mask_max("L3", n, 2)
                    mask_max("L3", n, 3)
                    shifts("L3", n)
                if a:
                    t_head(n, 3, 0)
                    t_head(n, 3, 1)
                if pre:
                    inverses("L0", n)
                    low("L0", n, 2)
                    evacuate("L0", n, 0)
                    evacuate("L0", n, 1)
                    low("L0", n, 3)
                if b:
                    tile_b(n, "V3", 0, VB)
                    inverses("L3", n)
                if a:
                    scalars(n, "O1", "fO")
                if b:
                    tile_b(n, "V3", 1, VB)
                if pre:
                    evacuate("L0", n, 2)
                if b:
                    low("L3", n, 0)
                if pre:
                    evacuate("L0", n, 3)
                if a:
                    mask_max("O1", n, 0)
                if b:
                    low("L3", n, 1)
                    evacuate("L3", n, 0)
                if a:
                    mask_max("O1", n, 1)
                if b:
                    low("L3", n, 2)
                    evacuate("L3", n, 1)
                if a:
                    mask_max("O1", n, 2)
                if b:
                    low("L3", n, 3)
                    evacuate("L3", n, 2)
                if a:
                    mask_max("O1", n, 3)
                if pre:
                    norm_stats("ln0", n, x0)
                if a:
                    shifts("O1", n)
                if pre:
                    norm_aggr("ln0", n)
                    norm_var("ln0", n)
                    norm_out("ln0", n, x0, x1)
                if b:
                    evacuate("L3", n, 3)
                if a:
                    tile_a(n, "VO", 0, VH[1])
                if b:
                    norm_stats("ln3", n, xb)
                    norm_aggr("ln3", n)
                    norm_var("ln3", n)
                    norm_out("ln3", n, xb, eb)
                if a:
                    tile_a(n, "VO", 1, VH[1])

            body(-1)
            body(0)
            with dve.Fori(1, B - 1) as n:
                body(n)
            body(B - 1)
            body(B)


_INS = ['x', 'adj', 'L0_gnn_W', 'L0_gnn_a', 'L1_gnn_W_heads', 'L1_gnn_a_heads', 'L1_gnn_W_out', 'L1_gnn_a_out',
        'L1_gnn_w1', 'L1_gnn_b1', 'L1_gnn_w2', 'L1_gnn_b2', 'L1_gnn_ln_gamma', 'L1_gnn_ln_beta', 'L2_gnn_W',
        'L2_gnn_b', 'L3_gnn_W', 'L3_gnn_a_src', 'L3_gnn_a_dst']


def kernel(**inputs):
    import numpy as _np
    import concourse.bacc as _bacc
    from concourse import mybir as _mybir
    from concourse.bass_utils import run_bass_kernel_spmd as _run

    nc = _bacc.Bacc("TRN2", target_bir_lowering=False, num_devices=1)
    arrays, args = {}, []
    for name in _INS:
        a = _np.ascontiguousarray(inputs[name])
        arrays[f"in_{name}"] = a
        args.append(nc.dram_tensor(f"in_{name}", a.shape, _mybir.dt.from_np(a.dtype), kind="ExternalInput").ap())
    args.append(nc.dram_tensor("out_x", (B, N, D), _mybir.dt.float32, kind="ExternalOutput").ap())
    graph_net_kernel(nc, *args)
    r = _run(nc, [arrays], core_ids=[0])
    return r.results[0]["out_x"]
```

```python
import concourse.bass as bass
from concourse import mybir
from concourse.alu_op_type import AluOpType as ALU
import itertools
from contextlib import ExitStack

B, N, D, H = 16, 512, 256, 4
P = 128
NI = N // P
KD = D // P
D0 = D // 2
KH = H * D // P
EPS = 1e-5
NEG = -1e9
ALPHA = {"L0": 0.2, "L1": 0.01, "L3": 0.2}
T_RING, O_RING = 2, 2

HEADS = [f"H{h}" for h in range(H)]
ELU = HEADS + ["O1"]


def kind(n):
    if not isinstance(n, int):
        return "loop"
    return {-1: "pre", 0: "first", B - 1: "last", B: "end"}.get(n, "loop")


class Tally:

    def __init__(self, **steps):
        self.steps = {k: steps.get(k, []) for k in ("pre", "first", "loop", "last", "end")}

    def before(self, n):
        s, c = self.steps, len(self.steps["loop"])
        if isinstance(n, int):
            return sum(len(s[kind(m)]) for m in range(-1, n))
        return n * c + (len(s["pre"]) + len(s["first"]) - c)

    def at(self, n, step):
        return self.before(n) + self.steps[kind(n)].index(step) + 1


def stages_of(k):
    return {"pre": ["L0"], "first": HEADS + ["L0", "O1"], "loop": HEADS + ["L0", "L3", "O1"],
            "last": HEADS + ["L3", "O1"], "end": ["L3"]}[k]


def group_before(n, stage):
    order = stages_of(kind(n))
    if stage != order[0]:
        return n, order[order.index(stage) - 1]
    return n - 1, ("L0" if kind(n) == "first" else "O1")


KINDS = ("pre", "first", "loop", "last", "end")
A_KINDS, B_KINDS, PRE_KINDS = ("first", "loop", "last"), ("loop", "last", "end"), ("pre", "first", "loop")
GROUPS = Tally(**{k: stages_of(k) for k in KINDS})
UNITS = Tally(**{k: [(s, i) for s in stages_of(k) for i in range(NI)] for k in KINDS})
PLAIN_UNITS = Tally(**{k: [(s, i) for s in stages_of(k) if s not in ELU for i in range(NI)] for k in KINDS})
L0_UNITS = Tally(**{k: [("L0", i) for s in stages_of(k) if s == "L0" for i in range(NI)] for k in KINDS})
ELU_UNITS = Tally(**{k: [(s, i) for s in stages_of(k) if s in ELU for i in range(NI)] for k in KINDS})


NEXT = {"x0T", "f0", "f0_high", "f0_raw", "V0", "x0sum", "ln0"} | {f"ln0_{s}" for s in ("stats", "aggr", "var", "out")}


def in_turn(stream, *steps):
    def kinds(step):
        if stream == "B":
            return B_KINDS
        return PRE_KINDS if (step if isinstance(step, str) else step[0]) in NEXT else A_KINDS

    return Tally(**{k: [s for s in steps if k in kinds(s)] for k in KINDS})


PE_A = in_turn(
    "A", ("x1T", 0), ("x1T", 1), "fH", ("V0H", 0), ("V0H", 1), ("V1H", 0), ("V1H", 1), ("V2H", 0), ("T0H", 0),
    ("T0H", 1), ("V2H", 1), ("V3H", 0), ("V3H", 1), ("x0T", 0), ("x0T", 1), ("T1H", 0), ("T1H", 1), "f0",
    ("T2H", 0), ("T2H", 1), "V0", ("T3H", 0), ("T3H", 1), "fO", ("VO", 0), ("VO", 1))
PE_B = in_turn(
    "B", ("outT", 0), ("outT", 1), ("ffn1", 0), ("ffn1", 1), ("ffn2", 0), ("ffn2", 1), ("x2T", 0), ("x2T", 1),
    ("mi", 0), ("mj", 0), ("mj", 1), ("Amj", 0), ("mi", 1), ("Amj", 1), ("x3T", 0), ("x3T", 1), "f3",
    ("V3", 0), ("V3", 1))
ACT_A = in_turn(
    "A", ("x1T", 0), ("x1T", 1), ("V0H", 0), ("V0H", 1), ("V1H", 0), ("V1H", 1), ("V2H", 0), ("T0H", 0),
    ("T0H", 1), ("V2H", 1), ("V3H", 0), ("V3H", 1), ("x0T", 0), ("x0T", 1), ("T1H", 0), ("T1H", 1),
    ("T2H", 0), ("T2H", 1), "V0", ("T3H", 0), ("T3H", 1), ("VO", 0), ("VO", 1))
ACT_B = in_turn(
    "B", ("outT", 0), ("outT", 1), ("ffn1", 0), ("ffn1", 1), ("x2T", 0), ("x2T", 1), ("mj", 0), ("mj", 1),
    ("x3T", 0), ("x3T", 1), ("V3", 0), ("V3", 1))
DVE_A = in_turn(
    "A", ("x1T", 0), ("x1T", 1), "fH_high", "fH_raw", "fH", ("V0H", 0), ("V0H", 1), ("V1H", 0), ("V1H", 1), "h0",
    ("V2H", 0), ("T0H", 0), ("T0H", 1), ("V2H", 1), ("V3H", 0), ("V3H", 1), ("x0T", 0), "h1", ("x0T", 1),
    ("T1H", 0), "f0_high", "f0_raw", "f0", ("T1H", 1), "h2", ("T2H", 0), "x0sum", "V0", ("T2H", 1), "h3",
    ("T3H", 0), ("T3H", 1), "fO_high", "fO_raw", "fO", "ln0_stats", "ln0_aggr", "ln0_var", "ln0_out",
    ("VO", 0), ("VO", 1))
DVE_B = in_turn(
    "B", "h1b", ("outT", 0), ("outT", 1), ("ffn1", 0), ("ffn1", 1), ("ffn2", 0), ("ffn2", 1), "ln1_stats",
    "ln1_aggr", "ln1_var", "ln1_out", "res1", "ln1o_stats", "ln1o_aggr", "ln1o_var", "ln1o_out", ("x2T", 0),
    ("x2T", 1), ("mi", 0), ("mj", 0), ("mj", 1), ("Amj", 0), ("mi", 1), ("Amj", 1), "ln2_stats", "ln2_aggr",
    "ln2_var", "ln2_out", ("x3T", 0), ("x3T", 1), "f3_high", "f3_raw", "f3", ("V3", 0), ("V3", 1),
    "ln3_stats", "ln3_aggr", "ln3_var", "ln3_out")
POOL_A = in_turn("A", "x1b", "ln0")
POOL_B = in_turn(
    "B", "ob", ("glo", 0), ("glo", 1), "ln1", "xg", "ln1o", "xb", "ln2", "ln3")
X_LOADS = Tally(pre=["x"], first=["x"], loop=["x"])
NORMS = ["ln0", "ln1", "ln1o", "ln2", "ln3"]

PREP = ["edges", "mask", "has_edge", "adjT", "wl0", "wl1", "wl2", "wl3", "w0", "w3", "wa_high", "wa_low", "consts"]
PREP_ACT = ["deg", "wh", "wo", "w1", "w2", "wl0", "wl1", "wl2", "wl3", "w0", "w3"]
PREP_POOL = ["zero", "ident", "wh", "wo", "w1", "w2"]


def prepared(step):
    return PREP.index(step) + 1


def graph_net_kernel(nc, x_in, adj_in, w0_in, a0_in, wh_in, ah_in, wo_in, ao_in, w1_in, b1_in, w2_in, b2_in,
                     gamma_in, beta_in, wl2_in, bl2_in, w3_in, asrc_in, adst_in, out):
    f32, f32r, bf16, i32 = mybir.dt.float32, mybir.dt.float32r, mybir.dt.bfloat16, mybir.dt.int32
    ACT = mybir.ActivationFunctionType

    with ExitStack() as ctx:
        def sb(name, shape, dtype=f32):
            return ctx.enter_context(nc.sbuf_tensor(name, shape, dtype))

        def sem(name):
            return ctx.enter_context(nc.semaphore(name))

        def split_sb(name, width):
            return [sb(f"{name}_{part}", [P, width], f32r) for part in ("high", "low")]

        w0, wh, wo = split_sb("w0", KD * D0), split_sb("wh", KD * H * D), split_sb("wo", KH * D)
        w1, w2 = split_sb("w1", KD * D), split_sb("w2", KD * D)
        wi, wj, w3 = split_sb("wi", KD * D), split_sb("wj", KD * D), split_sb("w3", KD * D)
        WA = {"L0": (0, KD, 2), "H": (4, KD, 2 * H), "O1": (20, KH, 2), "L3": (36, KD, 2)}
        wa_raw = sb("wa_raw", [P, 40])
        wa = sb("wa", [P, 80], f32r)
        mask = sb("mask", [P, NI, N], bf16)
        adjT = sb("adjT", [P, NI, N], f32r)
        ident = sb("ident", [P, P])
        deg = sb("deg", [P, NI])
        has_edge = sb("has_edge", [P, NI])
        deg_b = sb("deg_b", [P, NI, D])
        b2m1, gamma, beta = sb("b2m1", [P, D]), sb("gamma", [P, D]), sb("beta", [P, D])
        b1c = sb("b1c", [P, KD])
        minus_half = sb("minus_half", [P, NI])
        settled = sb("settled", [P, NI + len(NORMS)])

        GP = sb("GP", [P, 2 * NI * N])
        G = GP[:, 0:NI * N].rearrange("p (r n) -> p r n", n=N)
        Pm = GP[:, NI * N:2 * NI * N].rearrange("p (r n) -> p r n", n=N)
        PT = [sb(f"PT_{part}", [P, T_RING, NI, P], f32r) for part in ("high", "low")]
        SLOTS = HEADS + ["L0", "L3", "O1"]
        row_sum, row_inv = sb("row_sum", [P, len(SLOTS), NI]), sb("row_inv", [P, len(SLOTS), NI])
        shift = sb("shift", [P, len(SLOTS), NI])
        gmax, gtop, gleaky = sb("gmax", [P, NI]), sb("gtop", [P, NI]), sb("gleaky", [P, NI])

        work = sb("work", [P, 8, NI * D])

        def view(k):
            return work[:, k, :].rearrange("p (i d) -> p i d", i=NI)

        hx, he, x1, x1b, xb, hb, eb, x0 = (view(k) for k in range(8))
        eb_wide = work[:, 6, :].rearrange("p (o n) -> p o n", n=N)

        scalar_row = work[0:4, 1, 0:N]

        xTa, xTb = split_sb("xTa", KD * N), split_sb("xTb", KD * N)
        V0 = sb("V0", [P, NI, 2, D0], f32r)
        VH = [split_sb("VH0", NI * D), split_sb("VH1", NI * D)]
        VB = split_sb("VB", NI * D)
        hT = split_sb("hT", KH * N)

        fcols = {s: (sb(f"f_{s}", [P, NI, 2 * nh]), sb(f"fa_{s}", [P, NI, nh]), sb(f"fb_{s}", [P, NI, nh]))
                 for s, nh in (("L0", 1), ("H", H), ("O1", 1), ("L3", 1))}
        norm = {s: (sb(f"bn_{s}", [P, NI, 6]), sb(f"mv_{s}", [P, NI, 2]), sb(f"var_{s}", [P, NI]),
                    sb(f"rstd_{s}", [P, NI])) for s in "ab"}

        bank = [ctx.enter_context(nc.psum_tensor(f"bank{k}", [P, N], f32)) for k in range(8)]
        T_bank, O_bank, A_bank, B_bank, F_bank = bank[0:2], bank[2:4], bank[4:6], bank[6], bank[7]

        loaded = {k: sem(f"loaded_{k}") for k in
                  ("adj", "wh", "wo", "ah", "wl", "rows", "w0", "w3", "a", "bl2")}
        prep_dve, prep_act, prep_pe, prep_pool = sem("prep_dve"), sem("prep_act"), sem("prep_pe"), sem("prep_pool")
        dot_done = sem("dot_done")
        x_loaded, eb_moved, EB_LOADS = sem("x_loaded"), sem("eb_moved"), 2
        g_ready, r_ready, z_ready, p_ready = sem("g_ready"), sem("r_ready"), sem("z_ready"), sem("p_ready")
        t_full, high_done, low_done, o_full = sem("t_full"), sem("high_done"), sem("low_done"), sem("o_full")
        o_dve, o_act = sem("o_dve"), sem("o_act")
        f_row, tops, shift_ready, inv_ready, l3_inv = (sem("f_row"), sem("tops"), sem("shift_ready"),
                                                       sem("inv_ready"), sem("l3_inv"))
        l0_left = sem("l0_left")
        rows_full, rows_copied = sem("rows_full"), sem("rows_copied")
        pe_a, act_a, dve_a, pool_a = sem("pe_a"), sem("act_a"), sem("dve_a"), sem("pool_a")
        pe_b, act_b, dve_b, pool_b = sem("pe_b"), sem("act_b"), sem("dve_b"), sem("pool_b")

        block = ctx.enter_context(nc.Block())

        second = work[:, 2:4, :].rearrange("p a n -> p (a n)")
        w0_stage, w3_stage = second[:, 0:KD * D0], second[:, KD * D0:KD * D0 + KD * D]
        bl2_stage = work[:, 4, 0:D]

        def tiles(operand, width):
            return operand[:, :].rearrange("p (k n) -> p k n", n=width)

        def wa_of(s, k):
            at, _, w = WA[s]
            return wa[:, 2 * (at + k * w):2 * (at + (k + 1) * w)]

        def wa_part(s, part):
            at, nk, w = WA[s]
            return wa[:, 2 * at:2 * (at + nk * w)].rearrange("p (k s c) -> p s k c", s=2, c=w)[:, part, :, :]

        def wa_raw_of(s):
            at, nk, w = WA[s]
            return wa_raw[:, at:at + nk * w].rearrange("p (k c) -> p k c", c=w)

        def f_of(stage):
            return (fcols["H"], int(stage[1]), H) if stage in HEADS else (fcols[stage], 0, 1)

        def alpha_of(stage):
            return ALPHA.get(stage, ALPHA["L1"])

        def v_of(stage):
            if stage in HEADS:
                return VH[int(stage[1]) % 2]
            return {"O1": VH[1], "L3": VB}[stage]

        def b_bank_of(n, step):
            if kind(n) != "end":
                return B_bank
            return (B_bank, A_bank[0], A_bank[1])[PE_B.steps["end"].index(step) % 3]

        def a_bank_of(n, step):
            return A_bank[PE_A.steps[kind(n)].index(step) % 2]

        @block.sync
        def _(sp):
            x_v = x_in.rearrange("b (i p) d -> b p i d", p=P)
            out_v = out.rearrange("b (i p) d -> b p i d", p=P)
            sp.dma_start(work[:, 2:4, :].rearrange("p a n -> p (a n)").bitcast(i32)
                         .rearrange("p (i n) -> p i n", n=N),
                         adj_in.rearrange("(i p) n -> p i n", p=P)).then_inc(loaded["adj"], 16)
            wh_stage = GP[:, 0:KD * H * D].rearrange("p (k h o) -> p k h o", k=KD, h=H)
            for k in range(KD):
                sp.dma_start(wh_stage[:, k, :, :], wh_in[:, k * P:(k + 1) * P, :].rearrange("h p o -> p h o"))\
                    .then_inc(loaded["wh"], 16)
            sp.dma_start(work[:, 0:2, :].rearrange("p a n -> p (a n)"),
                         ah_in.rearrange("h o -> (h o)").partition_broadcast(P)).then_inc(loaded["ah"], 16)
            sp.dma_start(GP[:, NI * N:2 * NI * N].rearrange("p (k o) -> p k o", k=KH),
                         wo_in.rearrange("(k p) o -> p k o", p=P)).then_inc(loaded["wo"], 16)
            sp.dma_start(work[:, 7, :].rearrange("p (k n) -> p k n", n=2 * D),
                         wl2_in.rearrange("(k p) n -> p k n", p=P)).then_inc(loaded["wl"], 16)
            sp.dma_start(work[:, 6, 0:KD * D].rearrange("p (k o) -> p k o", k=KD),
                         w1_in.rearrange("(k p) o -> p k o", p=P)).then_inc(eb_moved, 16)
            sp.dma_start(work[:, 6, KD * D:2 * KD * D].rearrange("p (k o) -> p k o", k=KD),
                         w2_in.rearrange("(k p) o -> p k o", p=P)).then_inc(eb_moved, 16)
            with nc.allow_non_contiguous_dma(reason="256 bias values, once"):
                sp.dma_start(b1c[:, :], b1_in.rearrange("(k p) -> p k", p=P)).then_inc(loaded["rows"], 16)
            sp.dma_start(b2m1[:, :], b2_in.partition_broadcast(P)).then_inc(loaded["rows"], 16)
            sp.dma_start(gamma[:, :], gamma_in.partition_broadcast(P)).then_inc(loaded["rows"], 16)
            sp.dma_start(beta[:, :], beta_in.partition_broadcast(P)).then_inc(loaded["rows"], 16)
            sp.wait_ge(prep_dve, prepared("edges"))
            sp.dma_start(w0_stage.rearrange("p (k o) -> p k o", k=KD),
                         w0_in.rearrange("(k p) o -> p k o", p=P)).then_inc(loaded["w0"], 16)
            sp.dma_start(w3_stage.rearrange("p (k o) -> p k o", k=KD),
                         w3_in.rearrange("(k p) o -> p k o", p=P)).then_inc(loaded["w3"], 16)
            sp.dma_start(second[:, 768:1024], a0_in.rearrange("a o c -> (a o c)").partition_broadcast(P))\
                .then_inc(loaded["a"], 16)
            sp.dma_start(second[:, 1024:1536], ao_in.partition_broadcast(P)).then_inc(loaded["a"], 16)
            sp.dma_start(second[:, 1536:1792], asrc_in.partition_broadcast(P)).then_inc(loaded["a"], 16)
            sp.dma_start(second[:, 1792:2048], adst_in.partition_broadcast(P)).then_inc(loaded["a"], 16)
            sp.wait_ge(prep_dve, prepared("mask"))
            sp.wait_ge(prep_pe, 1)
            sp.wait_ge(prep_act, 1)
            sp.dma_start(bl2_stage, bl2_in.partition_broadcast(P)).then_inc(loaded["bl2"], 16)
            sp.wait_ge(prep_pe, 1 + 2 * KD)
            sp.dma_start(x0, x_v[0]).then_inc(x_loaded, 16)

            def body(n):
                if kind(n) in A_KINDS and kind(n) in PRE_KINDS:
                    sp.wait_ge(dve_a, DVE_A.at(n - 1, "ln0_out"))
                    sp.dma_start(x0, x_v[n + 1]).then_inc(x_loaded, 16)
                if kind(n) in B_KINDS:
                    sp.wait_ge(dve_b, DVE_B.at(n, "ln3_out"))
                    sp.dma_start(out_v[n - 1], eb).then_inc(eb_moved, 16)

            body(0)
            with sp.Fori(1, B - 1) as n:
                body(n)
            body(B - 1)
            body(B)
            sp.wait_ge(eb_moved, 16 * (EB_LOADS + B))

        @block.gpsimd
        def _(pool):
            pool.memset(minus_half[:, :], -0.5)
            pool.memset(ident[:, :], 0.0).then_inc(prep_pool, 1)
            pool.wait_ge(prep_pool, 1)
            pool.affine_select(out=ident[:, :], in_=ident[:, :], compare_op=ALU.not_equal, fill=1.0, base=0,
                               pattern=[[-1, P]], channel_multiplier=1).then_inc(prep_pool, 1)
            for name, dst, src in (("wh", wh, GP[:, 0:NI * N]), ("wo", wo, GP[:, NI * N:2 * NI * N]),
                                   ("w1", w1, work[:, 6, 0:KD * D]), ("w2", w2, work[:, 6, KD * D:2 * KD * D])):
                pool.wait_ge(prep_act, PREP_ACT.index(name) + 1)
                pool.tensor_tensor(dst[1][:, :], src, dst[0][:, :].bitcast(f32), ALU.subtract).then_inc(prep_pool, 1)
            pool.wait_ge(prep_dve, len(PREP))

            def scores(stage, n, i):
                pool.wait_ge(r_ready, UNITS.at(n, (stage, i)))
                pool.tensor_tensor(G[:, i, :], G[:, i, :], Pm[:, i, :], ALU.add).then_inc(z_ready, 1)

            def rstd(stream, dve_sem, dve_tally, name, n, done):
                var, rs = norm[stream][2:]
                pool.wait_ge(dve_sem, dve_tally.at(n, f"{name}_var"))
                pool.tensor_tensor(rs[:, :], var[:, :], minus_half[:, :], ALU.pow).then_inc(done, 1)

            def all_rows(row):
                return row[:, :].unsqueeze(1).to_broadcast([P, NI, D])

            def out_bias(n):
                pool.wait_ge(pe_b, PE_B.at(n, ("outT", 1)))
                pool.tensor_tensor(hb, hb, all_rows(b2m1), ALU.add).then_inc(pool_b, 1)

            def hidden_low(n, o):
                pool.wait_ge(dve_b, DVE_B.at(n, ("ffn1", o)))
                pool.tensor_tensor(tiles(VB[1], N)[:, o, :], eb_wide[:, o, :],
                                   tiles(VB[0], N)[:, o, :].bitcast(f32), ALU.subtract).then_inc(pool_b, 1)

            def times_gamma(n):
                pool.wait_ge(dve_b, DVE_B.at(n, "ln1_out"))
                pool.tensor_tensor(eb, eb, all_rows(gamma), ALU.mult).then_inc(pool_b, 1)

            def message_bias(n):
                pool.wait_ge(pe_b, PE_B.at(n, ("x2T", 1)))
                pool.tensor_tensor(xb, xb, deg_b[:, :, :], ALU.add).then_inc(pool_b, 1)

            def plus_beta(n):
                if kind(n) in B_KINDS:
                    pool.wait_ge(dve_b, DVE_B.at(n, "res1"))
                else:
                    pool.wait_ge(dve_a, DVE_A.at(n - 1, "ln0_out"))
                pool.tensor_tensor(x1b, x1, all_rows(beta), ALU.add).then_inc(pool_a, 1)

            def rstd_b(name, n):
                rstd("b", dve_b, DVE_B, name, n, pool_b)

            def rstd_a(name, n):
                rstd("a", dve_a, DVE_A, name, n, pool_a)

            def body(n):
                k = kind(n)
                a, b, pre = k in A_KINDS, k in B_KINDS, k in PRE_KINDS
                if a:
                    scores("H0", n, 0)
                    scores("H0", n, 1)
                    scores("H0", n, 2)
                    scores("H0", n, 3)
                    scores("H1", n, 0)
                if b:
                    out_bias(n)
                if a:
                    scores("H1", n, 1)
                if b:
                    hidden_low(n, 0)
                if a:
                    scores("H1", n, 2)
                if b:
                    hidden_low(n, 1)
                if a:
                    scores("H1", n, 3)
                if b:
                    rstd_b("ln1", n)
                if a:
                    scores("H2", n, 0)
                if b:
                    times_gamma(n)
                if a:
                    scores("H2", n, 1)
                    scores("H2", n, 2)
                    scores("H2", n, 3)
                if b:
                    rstd_b("ln1o", n)
                    message_bias(n)
                if a:
                    scores("H3", n, 0)
                    scores("H3", n, 1)
                    scores("H3", n, 2)
                    scores("H3", n, 3)
                if pre:
                    scores("L0", n, 0)
                    scores("L0", n, 1)
                if b:
                    rstd_b("ln2", n)
                if pre:
                    scores("L0", n, 2)
                    scores("L0", n, 3)
                if b:
                    scores("L3", n, 0)
                    scores("L3", n, 1)
                    scores("L3", n, 2)
                    scores("L3", n, 3)
                if a:
                    plus_beta(n)
                    scores("O1", n, 0)
                    scores("O1", n, 1)
                if pre:
                    rstd_a("ln0", n)
                if a:
                    scores("O1", n, 2)
                    scores("O1", n, 3)
                if b:
                    rstd_b("ln3", n)

            body(-1)
            body(0)
            with pool.Fori(1, B - 1) as n:
                body(n)
            body(B - 1)
            body(B)

        @block.scalar
        def _(act):
            act.wait_ge(prep_dve, prepared("edges"))
            edges = work[:, 4:6, :].rearrange("p a n -> p (a n)").rearrange("p (i n) -> p i n", n=N)
            for i in range(NI):
                last = act.activation(tiles(hT[0], N)[:, i, :], edges[:, i, :], ACT.Copy, accum_out=deg[:, i:i + 1])
            last.then_inc(prep_act, 1)
            for arrived, count, dst, src in (
                    (loaded["wh"], 32, wh, GP[:, 0:NI * N]), (loaded["wo"], 16, wo, GP[:, NI * N:2 * NI * N]),
                    (eb_moved, 32, w1, work[:, 6, 0:KD * D]), (eb_moved, 32, w2, work[:, 6, KD * D:2 * KD * D])):
                act.wait_ge(arrived, count)
                act.activation(dst[0][:, :], src, ACT.Copy).then_inc(prep_act, 1)
            for c in range(2 * KD):
                act.wait_ge(prep_pe, 2 + c)
                act.activation(tiles((wi, wj)[c // KD][0], D)[:, c % KD, :], bank[4 + c][:, 0:D], ACT.Copy)\
                    .then_inc(prep_act, 1)
            for name, dst, src in (("w0", w0, w0_stage), ("w3", w3, w3_stage)):
                act.wait_ge(loaded[name], 16)
                act.activation(dst[0][:, :], src, ACT.Copy).then_inc(prep_act, 1)

            def relu(stage, n, i):
                alpha, (_, _, fb), h = alpha_of(stage), f_of(stage)[0], f_of(stage)[1]
                u = UNITS.at(n, (stage, i))
                act.wait_ge(g_ready, u)
                if kind(n) != "pre":
                    act.wait_ge(t_full, u - NI)
                act.activation(Pm[:, i, :], G[:, i, :], ACT.Relu, bias=fb[:, i, h:h + 1],
                               scale=(1 - alpha) / alpha).then_inc(r_ready, 1)

            def exp(stage, n, i):
                s = SLOTS.index(stage)
                act.wait_ge(z_ready, UNITS.at(n, (stage, i)))
                if i == 0:
                    act.wait_ge(shift_ready, GROUPS.at(n, stage))
                act.activation(Pm[:, i, :], G[:, i, :], ACT.Exp, bias=shift[:, s, i:i + 1],
                               accum_out=row_sum[:, s, i:i + 1]).then_inc(p_ready, 1)

            def high(stage, n, i):
                u = UNITS.at(n, (stage, i))
                act.wait_ge(t_full, u)
                if kind(n) != "pre" or i >= T_RING:
                    act.wait_ge(o_full, u - T_RING)
                act.activation(PT[0][:, i % T_RING, :, :], T_bank[i % T_RING][:, :]
                               .rearrange("p (j n) -> p j n", n=P), ACT.Copy).then_inc(high_done, 1)

            def elu_parts(stage, n, i):
                dst, e = (hb, eb) if stage == "O1" else (hx, he)
                inv = row_inv[:, SLOTS.index(stage), i:i + 1]
                if i == 0:
                    act.wait_ge(inv_ready, GROUPS.at(n, stage))
                    if stage in HEADS[1:]:
                        act.wait_ge(pe_a, PE_A.at(n, (f"T{int(stage[1]) - 1}H", 1)))
                    if stage == "H0" and kind(n) != "first":
                        act.wait_ge(dve_a, DVE_A.at(n - 1, "h3"))
                    if stage == "O1":
                        act.wait_ge(eb_moved, 16 * (n + EB_LOADS))
                act.wait_ge(o_full, UNITS.at(n, (stage, i)))
                act.activation(dst[:, i, :], O_bank[i % O_RING][:, 0:D], ACT.Relu, scale=inv)
                act.activation(e[:, i, :], O_bank[i % O_RING][:, 0:D], ACT.Exp, scale=inv).then_inc(o_act, 1)

            def split_a(n, step, dst, bias=0.0):
                act.wait_ge(pe_a, PE_A.at(n, step))
                act.activation(dst, a_bank_of(n, step)[:, :], ACT.Copy, bias=bias).then_inc(act_a, 1)

            def split_b(n, step, dst, bias=0.0):
                act.wait_ge(pe_b, PE_B.at(n, step))
                act.activation(dst, b_bank_of(n, step)[:, :], ACT.Copy, bias=bias).then_inc(act_b, 1)

            def tile_a(n, name, k, dst, bias=0.0):
                split_a(n, (name, k), tiles(dst, N)[:, k, :], bias)

            def tile_b(n, name, k, dst, bias=0.0):
                split_b(n, (name, k), tiles(dst, N)[:, k, :], bias)

            def v_head(n, h, m):
                last = {1: (n - 1, ("O1", NI - 1)), 2: (n, ("H0", NI - 1)), 3: (n, ("H1", NI - 1))}
                if m == 0 and h and (h > 1 or kind(n) != "first"):
                    act.wait_ge(o_full, UNITS.at(*last[h]))
                tile_a(n, f"V{h}H", m, VH[h % 2][0])

            def v_out(n, m):
                if m == 0:
                    act.wait_ge(o_full, UNITS.at(n, ("H3", NI - 1)))
                tile_a(n, "VO", m, VH[1][0])

            def t_head(n, h, c):
                split_a(n, (f"T{h}H", c), tiles(hT[0], N)[:, KD * h + c, :], -1.0)

            def x0_turn(n, c):
                if kind(n) != "pre":
                    act.wait_ge(pe_a, PE_A.at(n, ("V3H", 1)))
                tile_a(n, "x0T", c, xTa[0])

            def v_first(n):
                act.wait_ge(pe_a, PE_A.at(n, "V0"))
                act.activation(V0[:, :, 0, :], a_bank_of(n, "V0")[:, :].rearrange("p (i d) -> p i d", d=D0), ACT.Copy)\
                    .then_inc(act_a, 1)

            def hidden(n, o):
                act.wait_ge(pe_b, PE_B.at(n, ("ffn1", o)))
                act.activation(tiles(VB[0], N)[:, o, :], b_bank_of(n, ("ffn1", o))[:, :], ACT.Relu,
                               bias=b1c[:, o:o + 1])\
                    .then_inc(act_b, 1)

            def body(n):
                k = kind(n)
                a, b, pre = k in A_KINDS, k in B_KINDS, k in PRE_KINDS
                if b:
                    high("O1", n - 1, 0)
                if a:
                    tile_a(n, "x1T", 0, xTa[0])
                if b:
                    high("O1", n - 1, 1)
                if a:
                    tile_a(n, "x1T", 1, xTa[0])
                if b:
                    high("O1", n - 1, 2)
                    elu_parts("O1", n - 1, 0)
                    elu_parts("O1", n - 1, 1)
                    high("O1", n - 1, 3)
                if a:
                    relu("H0", n, 0)
                    relu("H0", n, 1)
                if b:
                    elu_parts("O1", n - 1, 2)
                if a:
                    relu("H0", n, 2)
                    v_head(n, 0, 0)
                    relu("H0", n, 3)
                if b:
                    elu_parts("O1", n - 1, 3)
                if a:
                    exp("H0", n, 0)
                    exp("H0", n, 1)
                    v_head(n, 0, 1)
                    exp("H0", n, 2)
                if b:
                    tile_b(n, "outT", 0, xTb[0], -1.0)
                if a:
                    high("H0", n, 0)
                    relu("H1", n, 0)
                    exp("H0", n, 3)
                if b:
                    tile_b(n, "outT", 1, xTb[0], -1.0)
                if a:
                    high("H0", n, 1)
                    relu("H1", n, 1)
                    v_head(n, 1, 0)
                    elu_parts("H0", n, 0)
                    high("H0", n, 2)
                if b:
                    hidden(n, 0)
                if a:
                    exp("H1", n, 0)
                    v_head(n, 1, 1)
                    relu("H1", n, 2)
                    high("H0", n, 3)
                    elu_parts("H0", n, 1)
                if b:
                    hidden(n, 1)
                if a:
                    relu("H1", n, 3)
                    exp("H1", n, 1)
                    high("H1", n, 0)
                    exp("H1", n, 2)
                    high("H1", n, 1)
                    elu_parts("H0", n, 2)
                    elu_parts("H0", n, 3)
                    exp("H1", n, 3)
                    v_head(n, 2, 0)
                    relu("H2", n, 0)
                    high("H1", n, 2)
                    t_head(n, 0, 0)
                    t_head(n, 0, 1)
                    elu_parts("H1", n, 0)
                    relu("H2", n, 1)
                    relu("H2", n, 2)
                    high("H1", n, 3)
                    v_head(n, 2, 1)
                    relu("H2", n, 3)
                    elu_parts("H1", n, 1)
                    exp("H2", n, 0)
                    elu_parts("H1", n, 2)
                    exp("H2", n, 1)
                    v_head(n, 3, 0)
                    high("H2", n, 0)
                    exp("H2", n, 2)
                    v_head(n, 3, 1)
                    elu_parts("H1", n, 3)
                    high("H2", n, 1)
                if pre and k != "pre":
                    x0_turn(n, 0)
                if a:
                    exp("H2", n, 3)
                if b:
                    tile_b(n, "x2T", 0, xTb[0])
                if pre and k != "pre":
                    x0_turn(n, 1)
                if a:
                    high("H2", n, 2)
                if b:
                    tile_b(n, "x2T", 1, xTb[0])
                if a:
                    high("H2", n, 3)
                    t_head(n, 1, 0)
                    relu("H3", n, 0)
                    t_head(n, 1, 1)
                    relu("H3", n, 1)
                    elu_parts("H2", n, 0)
                    relu("H3", n, 2)
                if b:
                    tile_b(n, "mj", 0, VB[0])
                if a:
                    elu_parts("H2", n, 1)
                    relu("H3", n, 3)
                    exp("H3", n, 0)
                    exp("H3", n, 1)
                if b:
                    tile_b(n, "mj", 1, VB[0])
                if a:
                    elu_parts("H2", n, 2)
                    exp("H3", n, 2)
                    high("H3", n, 0)
                    elu_parts("H2", n, 3)
                    high("H3", n, 1)
                    exp("H3", n, 3)
                if pre:
                    relu("L0", n, 0)
                    relu("L0", n, 1)
                    relu("L0", n, 2)
                if a:
                    high("H3", n, 2)
                    t_head(n, 2, 0)
                    elu_parts("H3", n, 0)
                if pre:
                    relu("L0", n, 3)
                    exp("L0", n, 0)
                if a:
                    high("H3", n, 3)
                    elu_parts("H3", n, 1)
                if pre:
                    exp("L0", n, 1)
                if a:
                    t_head(n, 2, 1)
                if pre:
                    v_first(n)
                    exp("L0", n, 2)
                if b:
                    tile_b(n, "x3T", 0, xTb[0])
                if pre:
                    high("L0", n, 0)
                if a:
                    elu_parts("H3", n, 2)
                if b:
                    tile_b(n, "x3T", 1, xTb[0])
                if a:
                    elu_parts("H3", n, 3)
                if pre:
                    exp("L0", n, 3)
                    high("L0", n, 1)
                if a:
                    t_head(n, 3, 0)
                    t_head(n, 3, 1)
                if b:
                    relu("L3", n, 0)
                if pre:
                    high("L0", n, 2)
                    high("L0", n, 3)
                if b:
                    relu("L3", n, 1)
                    tile_b(n, "V3", 0, VB[0])
                    relu("L3", n, 2)
                    exp("L3", n, 0)
                    exp("L3", n, 1)
                    tile_b(n, "V3", 1, VB[0])
                    high("L3", n, 0)
                    exp("L3", n, 2)
                    relu("L3", n, 3)
                    high("L3", n, 1)
                    exp("L3", n, 3)
                    high("L3", n, 2)
                if a:
                    relu("O1", n, 0)
                if b:
                    high("L3", n, 3)
                if a:
                    relu("O1", n, 1)
                    relu("O1", n, 2)
                    exp("O1", n, 0)
                    relu("O1", n, 3)
                    exp("O1", n, 1)
                    exp("O1", n, 2)
                    v_out(n, 0)
                    exp("O1", n, 3)
                    v_out(n, 1)

            for c in range(KD):
                x0_turn(-1, c)
            act.wait_ge(prep_dve, len(PREP))
            act.wait_ge(prep_pool, len(PREP_POOL))
            body(-1)
            body(0)
            with act.Fori(1, B - 1) as n:
                body(n)
            body(B - 1)
            body(B)

        @block.tensor
        def _(pe):
            def product(dst, left, right, first=True, last=True):
                passes = [(0, 0), (0, 1), (1, 0)]
                for m, (a, b) in enumerate(passes):
                    mm = pe.matmul(dst, left(a), right(b), start=first and m == 0, stop=last and m == 2)
                return mm

            def sum_of(dst, terms):
                for m, (left, right) in enumerate(terms):
                    mm = product(dst, left, right, m == 0, m == len(terms) - 1)
                return mm

            pe.wait_ge(prep_pool, 2)
            pe.wait_ge(prep_dve, prepared("edges"))
            edges = work[:, 4:6, :].rearrange("p a n -> p (a n)").rearrange("p (i n) -> p i n", n=N)
            for j in range(NI):
                for i in range(NI):
                    mm = pe.transpose(bank[j][:, i * P:(i + 1) * P], edges[:, i, j * P:(j + 1) * P], ident[:, :])
            mm.then_inc(prep_pe, 1)
            pe.wait_ge(loaded["wl"], 16)
            wl = work[:, 7, :].rearrange("p (k n) -> p k n", n=2 * D)
            for c in range(2 * KD):
                for o in range(KD):
                    mm = pe.transpose(bank[4 + c][:, o * P:(o + 1) * P], wl[:, o, c * P:(c + 1) * P], ident[:, :])
                mm.then_inc(prep_pe, 1)

            def f_rows(stage, n):
                raw, h, nh = f_of(stage)[0][0], f_of(stage)[1], f_of(stage)[2]
                if stage == "L3":
                    pe.wait_ge(dve_b, DVE_B.at(n, "f3"))
                else:
                    pe.wait_ge(dve_a, DVE_A.at(n, {"L0": "f0", "O1": "fO"}.get(stage, "fH")))
                if kind(n) != "pre":
                    pe.wait_ge(g_ready, UNITS.at(n, (stage, 0)) - 1)
                for i in range(NI):
                    mm = pe.transpose(F_bank[:, i * P:(i + 1) * P],
                                      raw[:, i, nh + h:nh + h + 1].to_broadcast([P, P]), ident[:, :])
                mm.then_inc(f_row, 1)

            def turn(stage, n, i):
                u = UNITS.at(n, (stage, i))
                pe.wait_ge(p_ready, u)
                if kind(n) != "pre" or i >= T_RING:
                    pe.wait_ge(low_done, u - T_RING)
                for j in range(NI):
                    mm = pe.transpose(T_bank[i % T_RING][:, j * P:(j + 1) * P], Pm[:, i, j * P:(j + 1) * P],
                                      ident[:, :])
                mm.then_inc(t_full, 1)

            def weighted(stage, n, i):
                pe.wait_ge(low_done, UNITS.at(n, (stage, i)))
                if i == 0:
                    if stage == "L3":
                        pe.wait_ge(dve_b, DVE_B.at(n, ("V3", 1)))
                    else:
                        step = {"L0": "V0", "O1": ("VO", 1)}.get(stage, (f"V{stage[1]}H", 1))
                        pe.wait_ge(dve_a, DVE_A.at(n, step))
                m, s = (n, stage) if i >= O_RING else group_before(n, stage)
                before = (s, (i - O_RING) % NI)
                if kind(n) != "pre" or i >= O_RING:
                    if s in ELU:
                        pe.wait_ge(o_act, ELU_UNITS.at(m, before))
                    else:
                        pe.wait_ge(o_dve, PLAIN_UNITS.at(m, before))
                O = O_bank[i % O_RING]
                if stage == "L0":
                    for j in range(NI):
                        pe.matmul(O[:, 0:2 * D0], PT[0][:, i % T_RING, j, :], V0[:, j, :, :], start=j == 0,
                                  stop=False)
                        mm = pe.matmul(O[:, 0:D0], PT[1][:, i % T_RING, j, :], V0[:, j, 0, :], start=False,
                                       stop=j == NI - 1)
                    mm.then_inc(o_full, 1)
                else:
                    V = v_of(stage)
                    sum_of(O[:, 0:D], [(lambda a, j=j: PT[a][:, i % T_RING, j, :],
                                        lambda b, j=j: tiles(V[b], D)[:, j, :]) for j in range(NI)])\
                        .then_inc(o_full, 1)

            def free_a(n, step):
                steps = PE_A.steps[kind(n)]
                m = steps.index(step)
                if m >= 2:
                    pe.wait_ge(dve_a, DVE_A.at(n, steps[m - 2]))
                elif kind(n) != "pre":
                    last = PE_A.steps["pre" if kind(n) == "first" else "loop"]
                    pe.wait_ge(dve_a, DVE_A.at(n - 1, last[m - 2]))
                return a_bank_of(n, step)

            def free_b(n, step):
                steps = PE_B.steps[kind(n)]
                m, banks = steps.index(step), 3 if kind(n) == "end" else 1
                if m >= banks:
                    pe.wait_ge(dve_b, DVE_B.at(n, steps[m - banks]))
                elif m:
                    pe.wait_ge(dve_a, DVE_A.before(n))
                return b_bank_of(n, step)

            def transposed(free, done, n, step, src, k):
                dst = free(n, step)
                for i in range(NI):
                    mm = pe.transpose(dst[:, i * P:(i + 1) * P], src[:, i, k * P:(k + 1) * P], ident[:, :])
                mm.then_inc(done, 1)

            def rows_times(dst, left, nk, right, i):
                return sum_of(dst, [(lambda a, k=k: tiles(left[a], N)[:, k, i * P:(i + 1) * P],
                                     lambda b, k=k: right(b)[:, k, :]) for k in range(nk)])

            def scalars(free, done, n, step, left, s):
                nk, w = WA[s][1:]
                dst = free(n, step)
                for i in range(NI):
                    for k in range(nk):
                        for part in range(2):
                            mm = pe.matmul(dst[:, i * 2 * w:(i + 1) * 2 * w],
                                           tiles(left[part], N)[:, k, i * P:(i + 1) * P], wa_of(s, k),
                                           start=k == part == 0, stop=k == nk - 1 and part == 1)
                mm.then_inc(done, 1)

            def half(free, done, n, name, m, left, nk, right):
                dst = free(n, (name, m))
                for i in (2 * m, 2 * m + 1):
                    mm = rows_times(dst[:, i % 2 * D:(i % 2 + 1) * D], left, nk, right, i)
                mm.then_inc(done, 1)

            def x1_turn(n, c):
                pe.wait_ge(dve_a, DVE_A.at(n - 1, "ln0_out"))
                transposed(free_a, pe_a, n, ("x1T", c), x1, c)

            def scalars_a(n, step):
                before, left, s = {"fH": (("x1T", 1), xTa, "H"), "f0": (("x0T", 1), xTa, "L0")}[step]
                if kind(n) == "pre":
                    pe.wait_ge(prep_dve, len(PREP))
                pe.wait_ge(dve_a, DVE_A.at(n, before))
                scalars(free_a, pe_a, n, step, left, s)

            def v_head(n, h, m):
                pe.wait_ge(dve_a, DVE_A.at(n, ("x1T", 1)))
                half(free_a, pe_a, n, f"V{h}H", m, xTa, KD,
                     lambda b: wh[b][:, :].rearrange("p (k c) -> p k c", k=KD)[:, :, h * D:(h + 1) * D])

            def t_head(n, h, c):
                pe.wait_ge(dve_a, DVE_A.at(n, f"h{h}"))
                transposed(free_a, pe_a, n, (f"T{h}H", c), hx, c)

            def x0_turn(n, c):
                pe.wait_ge(x_loaded, X_LOADS.at(n, "x") * 16)
                transposed(free_a, pe_a, n, ("x0T", c), x0, c)

            def v_first(n):
                pe.wait_ge(dve_a, DVE_A.at(n, ("x0T", 1)))
                dst = free_a(n, "V0")
                for i in range(NI):
                    mm = rows_times(dst[:, i * D0:(i + 1) * D0], xTa, KD, lambda b: tiles(w0[b], D0), i)
                mm.then_inc(pe_a, 1)

            def scalar_rows(n):
                pe.wait_ge(dve_a, DVE_A.at(n, ("T3H", 1)))
                dst = free_a(n, "fO")[0:4, :]
                for k in range(KH):
                    for part in range(2):
                        mm = pe.matmul(dst, wa_of("O1", k), tiles(hT[part], N)[:, k, :],
                                       start=k == part == 0, stop=k == KH - 1 and part == 1)
                mm.then_inc(rows_full, 1)

            def rows_turn(n):
                pe.wait_ge(rows_copied, n + 1)
                dst = a_bank_of(n, "fO")
                for i in range(NI):
                    mm = pe.matmul(dst[:, 4 * i:4 * i + 4], scalar_row[:, i * P:(i + 1) * P], ident[0:4, 0:4],
                                   start=True, stop=True)
                mm.then_inc(pe_a, 1)

            def v_out(n, m):
                pe.wait_ge(dve_a, DVE_A.at(n, ("T3H", 1)))
                half(free_a, pe_a, n, "VO", m, hT, KH, lambda b: tiles(wo[b], D))

            def out_turn(n, k):
                pe.wait_ge(dve_b, DVE_B.at(n, "h1b"))
                transposed(free_b, pe_b, n, ("outT", k), hb, k)

            def hidden(n, o):
                pe.wait_ge(dve_b, DVE_B.at(n, ("outT", 1)))
                dst = free_b(n, ("ffn1", o))
                sum_of(dst[:, :], [(lambda a, k=k: tiles(w1[a], D)[:, k, o * P:(o + 1) * P],
                                    lambda b, k=k: tiles(xTb[b], N)[:, k, :]) for k in range(KD)])\
                    .then_inc(pe_b, 1)

            def ffn_out(n, m):
                pe.wait_ge(pool_b, POOL_B.at(n, ("glo", 1)))
                half(free_b, pe_b, n, "ffn2", m, VB, KD, lambda b: tiles(w2[b], D))

            def x2_turn(n, k):
                pe.wait_ge(dve_b, DVE_B.at(n, "ln1o_out"))
                transposed(free_b, pe_b, n, ("x2T", k), xb, k)

            def message(n, name, m):
                pe.wait_ge(dve_b, DVE_B.at(n, ("x2T", 1)))
                half(free_b, pe_b, n, name, m, xTb, KD, lambda b: tiles((wi if name == "mi" else wj)[b], D))

            def neighbours(n, m):
                pe.wait_ge(dve_b, DVE_B.at(n, ("mj", 1)))
                dst = free_b(n, ("Amj", m))
                for i in (2 * m, 2 * m + 1):
                    for t in range(2 * NI):
                        mm = pe.matmul(dst[:, i % 2 * D:(i % 2 + 1) * D], adjT[:, t // 2, i * P:(i + 1) * P],
                                       tiles(VB[t % 2], D)[:, t // 2, :], start=t == 0, stop=t == 2 * NI - 1)
                mm.then_inc(pe_b, 1)

            def x3_turn(n, c):
                pe.wait_ge(dve_b, DVE_B.at(n, "ln2_out"))
                transposed(free_b, pe_b, n, ("x3T", c), xb, c)

            def scalars_b(n):
                pe.wait_ge(dve_b, DVE_B.at(n, ("x3T", 1)))
                scalars(free_b, pe_b, n, "f3", xTb, "L3")

            def v_last(n, m):
                pe.wait_ge(dve_b, DVE_B.at(n, ("x3T", 1)))
                half(free_b, pe_b, n, "V3", m, xTb, KD, lambda b: tiles(w3[b], D))

            def body(n):
                k = kind(n)
                a, b, pre = k in A_KINDS, k in B_KINDS, k in PRE_KINDS
                if b:
                    turn("O1", n - 1, 0)
                    turn("O1", n - 1, 1)
                if a:
                    x1_turn(n, 0)
                    x1_turn(n, 1)
                if b:
                    weighted("O1", n - 1, 0)
                    turn("O1", n - 1, 2)
                if a:
                    scalars_a(n, "fH")
                if b:
                    weighted("O1", n - 1, 1)
                if a:
                    f_rows("H0", n)
                if b:
                    turn("O1", n - 1, 3)
                    weighted("O1", n - 1, 2)
                if a:
                    v_head(n, 0, 0)
                if b:
                    weighted("O1", n - 1, 3)
                if a:
                    v_head(n, 0, 1)
                    f_rows("H1", n)
                    v_head(n, 1, 0)
                if b:
                    out_turn(n, 0)
                if a:
                    turn("H0", n, 0)
                    turn("H0", n, 1)
                    v_head(n, 1, 1)
                if b:
                    out_turn(n, 1)
                if a:
                    weighted("H0", n, 0)
                    turn("H0", n, 2)
                if b:
                    hidden(n, 0)
                if a:
                    f_rows("H2", n)
                    turn("H0", n, 3)
                    weighted("H0", n, 1)
                if b:
                    hidden(n, 1)
                if a:
                    turn("H1", n, 0)
                    weighted("H0", n, 2)
                    weighted("H0", n, 3)
                    turn("H1", n, 1)
                if b:
                    ffn_out(n, 0)
                if a:
                    v_head(n, 2, 0)
                if b:
                    ffn_out(n, 1)
                if a:
                    weighted("H1", n, 0)
                    turn("H1", n, 2)
                    t_head(n, 0, 0)
                    turn("H1", n, 3)
                    t_head(n, 0, 1)
                    weighted("H1", n, 1)
                    v_head(n, 2, 1)
                    f_rows("H3", n)
                    v_head(n, 3, 0)
                    weighted("H1", n, 2)
                    weighted("H1", n, 3)
                    turn("H2", n, 0)
                    v_head(n, 3, 1)
                    turn("H2", n, 1)
                if pre and k != "pre":
                    x0_turn(n, 0)
                if a:
                    weighted("H2", n, 0)
                if b:
                    x2_turn(n, 0)
                if a:
                    turn("H2", n, 2)
                if pre and k != "pre":
                    x0_turn(n, 1)
                if a:
                    weighted("H2", n, 1)
                if b:
                    x2_turn(n, 1)
                if a:
                    turn("H2", n, 3)
                    t_head(n, 1, 0)
                    t_head(n, 1, 1)
                if b:
                    message(n, "mi", 0)
                if pre:
                    scalars_a(n, "f0")
                if b:
                    message(n, "mj", 0)
                if a:
                    weighted("H2", n, 2)
                if pre:
                    f_rows("L0", n)
                if b:
                    message(n, "mj", 1)
                if a:
                    weighted("H2", n, 3)
                    turn("H3", n, 0)
                    turn("H3", n, 1)
                if b:
                    neighbours(n, 0)
                if a:
                    weighted("H3", n, 0)
                if b:
                    message(n, "mi", 1)
                if a:
                    turn("H3", n, 2)
                    t_head(n, 2, 0)
                    t_head(n, 2, 1)
                if b:
                    neighbours(n, 1)
                if a:
                    turn("H3", n, 3)
                    weighted("H3", n, 1)
                if pre:
                    v_first(n)
                if a:
                    weighted("H3", n, 2)
                if b:
                    x3_turn(n, 0)
                if pre:
                    turn("L0", n, 0)
                if a:
                    weighted("H3", n, 3)
                if b:
                    x3_turn(n, 1)
                if pre:
                    turn("L0", n, 1)
                    weighted("L0", n, 0)
                    turn("L0", n, 2)
                if b:
                    scalars_b(n)
                if a:
                    t_head(n, 3, 0)
                    t_head(n, 3, 1)
                if pre:
                    weighted("L0", n, 1)
                    turn("L0", n, 3)
                if b:
                    f_rows("L3", n)
                    v_last(n, 0)
                if a:
                    scalar_rows(n)
                if pre:
                    weighted("L0", n, 2)
                if b:
                    v_last(n, 1)
                    turn("L3", n, 0)
                if a:
                    rows_turn(n)
                if pre:
                    weighted("L0", n, 3)
                if b:
                    turn("L3", n, 1)
                    weighted("L3", n, 0)
                    turn("L3", n, 2)
                if a:
                    f_rows("O1", n)
                if b:
                    weighted("L3", n, 1)
                    turn("L3", n, 3)
                if a:
                    v_out(n, 0)
                if b:
                    weighted("L3", n, 2)
                    weighted("L3", n, 3)
                if a:
                    v_out(n, 1)

            pe.wait_ge(prep_dve, prepared("wl1"))
            for c in range(KD):
                x0_turn(-1, c)
            pe.wait_ge(prep_dve, prepared("w3"))
            pe.wait_ge(prep_pool, len(PREP_POOL))
            body(-1)
            body(0)
            with pe.Fori(1, B - 1) as n:
                body(n)
            body(B - 1)
            body(B)

        @block.vector
        def _(dve):
            edges = work[:, 4:6, :].rearrange("p a n -> p (a n)").rearrange("p (i n) -> p i n", n=N)
            dots = itertools.count()
            dve.wait_ge(loaded["adj"], 16)
            dve.tensor_copy(edges, work[:, 2:4, :].rearrange("p a n -> p (a n)").bitcast(i32)
                            .rearrange("p (i n) -> p i n", n=N)).then_inc(prep_dve, 1)
            dve.wait_ge(prep_dve, prepared("edges"))
            dve.tensor_scalar(mask[:, :, :], edges, -NEG, NEG, ALU.mult, ALU.add).then_inc(prep_dve, 1)

            def dot_columns(s, k, col, w, a):
                m = next(dots)
                if m >= NI:
                    dve.wait_ge(dot_done, m - NI + 1)
                dve.tensor_tensor_reduce(deg_b[:, m % NI, 0:w.shape[-1]], w, a, 1.0, 0.0, ALU.mult, ALU.add,
                                         wa_raw_of(s)[:, k, col:col + 1]).then_inc(dot_done, 1)

            dve.wait_ge(loaded["wh"], 32)
            dve.wait_ge(loaded["ah"], 16)
            a_heads = work[:, 0:2, :].rearrange("p a n -> p (a n)")
            for k in range(KD):
                for h in range(H):
                    for c in range(2):
                        dot_columns("H", k, c * H + h, GP[:, (k * H + h) * D:(k * H + h + 1) * D],
                                    a_heads[:, (2 * h + c) * D:(2 * h + c + 1) * D])

            def low_part(name, dst, src):
                dve.wait_ge(prep_act, PREP_ACT.index(name) + 1)
                dve.tensor_tensor(dst[1], src, dst[0].bitcast(f32), ALU.subtract).then_inc(prep_dve, 1)

            def flat(w):
                return [part[:, :] for part in w]

            dve.wait_ge(prep_act, 1)
            dve.tensor_scalar(has_edge[:, :], deg[:, :], 1.0, None, ALU.min).then_inc(prep_dve, 1)
            dve.wait_ge(prep_pe, 1)
            for j in range(NI):
                last = dve.tensor_copy(adjT[:, j, :], bank[j][:, :])
            last.then_inc(prep_dve, 1)
            for c in range(2 * KD):
                low_part(f"wl{c}", [tiles(part, D)[:, c % KD, :] for part in (wi, wj)[c // KD]], bank[4 + c][:, 0:D])
            dve.wait_ge(loaded["wo"], 16)
            dve.wait_ge(loaded["a"], 64)
            for k in range(KH):
                for c in range(2):
                    dot_columns("O1", k, c, GP[:, NI * N + k * D:NI * N + (k + 1) * D],
                                second[:, 1024 + c * D:1024 + (c + 1) * D])
            dve.wait_ge(loaded["w0"], 16)
            for k in range(KD):
                for c in range(2):
                    dot_columns("L0", k, c, second[:, k * D0:(k + 1) * D0],
                                second[:, 768 + c * D0:768 + (c + 1) * D0])
            low_part("w0", flat(w0), w0_stage)
            dve.wait_ge(loaded["w3"], 16)
            for k in range(KD):
                for c, a in enumerate((second[:, 1536:1792], second[:, 1792:2048])):
                    dot_columns("L3", k, c, second[:, 256 + k * D:256 + (k + 1) * D], a)
            low_part("w3", flat(w3), w3_stage)
            def settle(place):
                dve.memset(settled[:, place:place + 1], 0.0)

            def mask_max(stage, n, i):
                u = UNITS.at(n, (stage, i))
                if i == 0:
                    dve.wait_ge(f_row, GROUPS.at(n, stage))
                if kind(n) != "pre":
                    dve.wait_ge(p_ready, u - NI)
                settle(i)
                dve.tensor_tensor_reduce(G[:, i, :], F_bank[:, :], mask[:, i, :], alpha_of(stage), -3e38,
                                         ALU.add, ALU.max, gmax[:, i:i + 1]).then_inc(g_ready, 1)

            def shifts(stage, n):
                (_, fa, _), h, _ = f_of(stage)
                g = GROUPS.at(n, stage)
                dve.wait_ge(g_ready, UNITS.at(n, (stage, NI - 1)))
                dve.tensor_tensor(gtop[:, :], gmax[:, :], fa[:, :, h], ALU.add).then_inc(tops, 1)
                dve.wait_ge(tops, 2 * g - 1)
                dve.scalar_tensor_tensor(gleaky[:, :], gtop[:, :], 1 / alpha_of(stage), gtop[:, :],
                                         ALU.mult, ALU.max).then_inc(tops, 1)
                dve.wait_ge(tops, 2 * g)
                dve.tensor_tensor(shift[:, SLOTS.index(stage), :], fa[:, :, h], gleaky[:, :], ALU.subtract)\
                    .then_inc(shift_ready, 1)

            def inverses(stage, n):
                s = SLOTS.index(stage)
                dve.wait_ge(p_ready, UNITS.at(n, (stage, NI - 1)))
                if stage == "L3":
                    dve.reciprocal(row_inv[:, s, :], row_sum[:, s, :]).then_inc(l3_inv, 1)
                    dve.wait_ge(l3_inv, n)
                    dve.tensor_tensor(row_inv[:, s, :], row_inv[:, s, :], has_edge[:, :], ALU.mult)\
                        .then_inc(inv_ready, 1)
                else:
                    dve.reciprocal(row_inv[:, s, :], row_sum[:, s, :]).then_inc(inv_ready, 1)

            def low(stage, n, i):
                dve.wait_ge(high_done, UNITS.at(n, (stage, i)))
                dve.tensor_tensor(PT[1][:, i % T_RING, :, :],
                                  T_bank[i % T_RING][:, :].rearrange("p (j n) -> p j n", n=P),
                                  PT[0][:, i % T_RING, :, :].bitcast(f32), ALU.subtract).then_inc(low_done, 1)

            def evacuate(stage, n, i):
                inv = row_inv[:, SLOTS.index(stage), i:i + 1]
                O = O_bank[i % O_RING]
                if i == 0:
                    dve.wait_ge(inv_ready, GROUPS.at(n, stage))
                dve.wait_ge(o_full, UNITS.at(n, (stage, i)))
                if stage == "L0":
                    dve.scalar_tensor_tensor(x0[:, i, 0:D0], O[:, 0:D0], inv, x0[:, i, 0:D0], ALU.mult, ALU.add)\
                        .then_inc(l0_left, 1)
                    dve.wait_ge(l0_left, L0_UNITS.at(n, (stage, i)))
                    dve.scalar_tensor_tensor(x0[:, i, 0:D0], O[:, D0:2 * D0], inv, x0[:, i, 0:D0], ALU.mult, ALU.add)\
                        .then_inc(o_dve, 1)
                else:
                    dve.scalar_tensor_tensor(xb[:, i, :], O[:, 0:D], inv, xb[:, i, :], ALU.mult, ALU.add)\
                        .then_inc(o_dve, 1)

            def split_a(n, step, dst, high_part, bias=0.0):
                dve.wait_ge(act_a, ACT_A.at(n, step))
                dve.scalar_tensor_tensor(dst, a_bank_of(n, step)[:, :], bias, high_part.bitcast(f32),
                                         ALU.add, ALU.subtract).then_inc(dve_a, 1)

            def split_b(n, step, dst, high_part, bias=0.0):
                dve.wait_ge(act_b, ACT_B.at(n, step))
                dve.scalar_tensor_tensor(dst, b_bank_of(n, step)[:, :], bias, high_part.bitcast(f32),
                                         ALU.add, ALU.subtract).then_inc(dve_b, 1)

            def tile_a(n, name, k, dst, bias=0.0):
                split_a(n, (name, k), tiles(dst[1], N)[:, k, :], tiles(dst[0], N)[:, k, :], bias)

            def tile_b(n, name, k, dst, bias=0.0):
                split_b(n, (name, k), tiles(dst[1], N)[:, k, :], tiles(dst[0], N)[:, k, :], bias)

            def t_head(n, h, c):
                k = KD * h + c
                split_a(n, (f"T{h}H", c), tiles(hT[1], N)[:, k, :], tiles(hT[0], N)[:, k, :], -1.0)

            def elu(n, h):
                dve.wait_ge(o_act, ELU_UNITS.at(n, (f"H{h}", NI - 1)))
                dve.scalar_tensor_tensor(hx, he, 1.0, hx, ALU.min, ALU.add).then_inc(dve_a, 1)

            def scalars(n, s, step, stream="a"):
                raw, fa, fb = fcols[s]
                nh, alpha = WA[s][2] // 2, ALPHA.get(s, ALPHA["L1"])
                src, pe_sem, pe_tally, done, tally = (
                    (a_bank_of(n, step), pe_a, PE_A, dve_a, DVE_A) if stream == "a" else
                    (b_bank_of(n, step), pe_b, PE_B, dve_b, DVE_B))
                F = src[:, 0:NI * 4 * nh].rearrange("p (i s c) -> p i s c", i=NI, s=2)
                dve.wait_ge(pe_sem, pe_tally.at(n, step))
                dve.tensor_copy(raw[:, :, :], F[:, :, 0, :]).then_inc(done, 1)
                dve.wait_ge(done, tally.at(n, f"{step}_high"))
                dve.tensor_tensor(raw[:, :, :], raw[:, :, :], F[:, :, 1, :], ALU.add).then_inc(done, 1)
                dve.wait_ge(done, tally.at(n, f"{step}_raw"))
                dve.tensor_scalar(fa[:, :, :], raw[:, :, 0:nh], alpha, None, ALU.mult)
                dve.tensor_scalar(fb[:, :, :], raw[:, :, 0:nh], 1 - alpha, None, ALU.mult).then_inc(done, 1)

            def copy_rows(n):
                dve.wait_ge(rows_full, n + 1)
                dve.tensor_copy(scalar_row[:, :], a_bank_of(n, "fO")[0:4, :]).then_inc(rows_copied, 1)

            def first_sum(n):
                dve.wait_ge(act_a, ACT_A.at(n, "V0"))
                V = a_bank_of(n, "V0")[:, :]
                dve.tensor_tensor(x0[:, :, D0:D], V.rearrange("p (i d) -> p i d", d=D0), x0[:, :, D0:D], ALU.add)\
                    .then_inc(dve_a, 1)

            def v_first(n):
                dve.wait_ge(act_a, ACT_A.at(n, "V0"))
                dve.tensor_tensor(V0[:, :, 1, :], a_bank_of(n, "V0")[:, :].rearrange("p (i d) -> p i d", d=D0),
                                  V0[:, :, 0, :].bitcast(f32), ALU.subtract)\
                    .then_inc(dve_a, 1)

            def counts(name):
                return ((norm["a"], dve_a, DVE_A, pool_a, POOL_A) if name == "ln0" else
                        (norm["b"], dve_b, DVE_B, pool_b, POOL_B))

            def norm_stats(name, n, src):
                (bn, _, _, _), steps, tally, _, _ = counts(name)
                if name == "ln0":
                    dve.wait_ge(dve_a, DVE_A.at(n, "x0sum"))
                    dve.wait_ge(o_dve, PLAIN_UNITS.at(n, ("L0", NI - 1)))
                elif name == "ln3":
                    dve.wait_ge(o_dve, PLAIN_UNITS.at(n, ("L3", NI - 1)))
                else:
                    dve.wait_ge(dve_b, DVE_B.at(n, {"ln1": ("ffn2", 1), "ln1o": "res1", "ln2": ("Amj", 1)}[name]))
                for i in range(NI):
                    last = dve.bn_stats(bn[:, i, :], src[:, i, :])
                last.then_inc(steps, 1)

            def norm_aggr(name, n):
                (bn, mv, _, _), steps, tally, _, _ = counts(name)
                dve.wait_ge(steps, tally.at(n, f"{name}_stats"))
                settle(NI + NORMS.index(name))
                for i in range(NI):
                    last = dve.bn_aggr(mv[:, i, :], bn[:, i, :])
                last.then_inc(steps, 1)

            def norm_var(name, n):
                (_, mv, var, _), steps, tally, _, _ = counts(name)
                dve.wait_ge(steps, tally.at(n, f"{name}_aggr"))
                dve.tensor_scalar(var[:, :], mv[:, :, 1], EPS, None, ALU.add).then_inc(steps, 1)

            def norm_out(name, n, src, dst):
                (_, mv, _, rs), steps, tally, rsteps, rtally = counts(name)
                if name == "ln0" and kind(n) in A_KINDS:
                    dve.wait_ge(pool_a, POOL_A.at(n, "x1b"))
                dve.wait_ge(rsteps, rtally.at(n, name))
                for i in range(NI):
                    last = dve.tensor_scalar(dst[:, i, :], src[:, i, :], mv[:, i, 0:1], rs[:, i:i + 1],
                                             ALU.subtract, ALU.mult)
                last.then_inc(steps, 1)

            def elu_out(n):
                dve.wait_ge(o_act, ELU_UNITS.at(n - 1, ("O1", NI - 1)))
                dve.scalar_tensor_tensor(hb, eb, 1.0, hb, ALU.min, ALU.add).then_inc(dve_b, 1)

            def hidden(n, o):
                dve.wait_ge(act_b, ACT_B.at(n, ("ffn1", o)))
                dve.tensor_scalar(eb_wide[:, o, :], b_bank_of(n, ("ffn1", o))[:, :], b1c[:, o:o + 1], 0.0,
                                  ALU.add, ALU.max)\
                    .then_inc(dve_b, 1)

            def add_bank(n, name, m, dst):
                if name == "ffn2":
                    dve.wait_ge(pool_b, POOL_B.at(n, "ob"))
                else:
                    dve.wait_ge(dve_b, DVE_B.at(n, ("mi", m)))
                dve.wait_ge(pe_b, PE_B.at(n, (name, m)))
                part = dst[:, 2 * m:2 * m + 2, :]
                dve.tensor_tensor(part, b_bank_of(n, (name, m))[:, :].rearrange("p (i d) -> p i d", d=D), part,
                                  ALU.add)\
                    .then_inc(dve_b, 1)

            def residual(n):
                dve.wait_ge(pool_b, POOL_B.at(n, "xg"))
                dve.wait_ge(pool_a, POOL_A.at(n - 1, "x1b"))
                dve.tensor_tensor(xb, eb, x1b, ALU.add).then_inc(dve_b, 1)

            def own_message(n, m):
                dve.wait_ge(pool_b, POOL_B.at(n, "xb"))
                dve.wait_ge(pe_b, PE_B.at(n, ("mi", m)))
                for i in (2 * m, 2 * m + 1):
                    last = dve.scalar_tensor_tensor(xb[:, i, :], b_bank_of(n, ("mi", m))[:, i % 2 * D:(i % 2 + 1) * D],
                                                    deg[:, i:i + 1], xb[:, i, :], ALU.mult, ALU.add)
                last.then_inc(dve_b, 1)

            def body(n):
                k = kind(n)
                a, b, pre = k in A_KINDS, k in B_KINDS, k in PRE_KINDS
                if b:
                    low("O1", n - 1, 0)
                    inverses("O1", n - 1)
                if a:
                    tile_a(n, "x1T", 0, xTa)
                    tile_a(n, "x1T", 1, xTa)
                if b:
                    low("O1", n - 1, 1)
                    low("O1", n - 1, 2)
                if a:
                    scalars(n, "H", "fH")
                    mask_max("H0", n, 0)
                    mask_max("H0", n, 1)
                if b:
                    low("O1", n - 1, 3)
                if a:
                    mask_max("H0", n, 2)
                    mask_max("H0", n, 3)
                    shifts("H0", n)
                    tile_a(n, "V0H", 0, VH[0])
                if b:
                    elu_out(n)
                if a:
                    mask_max("H1", n, 0)
                    tile_a(n, "V0H", 1, VH[0])
                if b:
                    tile_b(n, "outT", 0, xTb, -1.0)
                if a:
                    low("H0", n, 0)
                    mask_max("H1", n, 1)
                    mask_max("H1", n, 2)
                if b:
                    tile_b(n, "outT", 1, xTb, -1.0)
                if a:
                    inverses("H0", n)
                    mask_max("H1", n, 3)
                    low("H0", n, 1)
                    shifts("H1", n)
                    low("H0", n, 2)
                if b:
                    hidden(n, 0)
                if a:
                    tile_a(n, "V1H", 0, VH[1])
                    low("H0", n, 3)
                    mask_max("H2", n, 0)
                if b:
                    hidden(n, 1)
                if a:
                    tile_a(n, "V1H", 1, VH[1])
                    mask_max("H2", n, 1)
                    low("H1", n, 0)
                    mask_max("H2", n, 2)
                    low("H1", n, 1)
                if b:
                    add_bank(n, "ffn2", 0, hb)
                if a:
                    elu(n, 0)
                    inverses("H1", n)
                    tile_a(n, "V2H", 0, VH[0])
                if b:
                    add_bank(n, "ffn2", 1, hb)
                    norm_stats("ln1", n, hb)
                    norm_aggr("ln1", n)
                    norm_var("ln1", n)
                if a:
                    mask_max("H2", n, 3)
                    t_head(n, 0, 0)
                if b:
                    norm_out("ln1", n, hb, eb)
                if a:
                    t_head(n, 0, 1)
                    shifts("H2", n)
                    low("H1", n, 2)
                    low("H1", n, 3)
                    tile_a(n, "V2H", 1, VH[0])
                if b:
                    residual(n)
                    norm_stats("ln1o", n, xb)
                    norm_aggr("ln1o", n)
                    norm_var("ln1o", n)
                if a:
                    tile_a(n, "V3H", 0, VH[1])
                    low("H2", n, 0)
                if b:
                    norm_out("ln1o", n, xb, xb)
                if a:
                    tile_a(n, "V3H", 1, VH[1])
                    low("H2", n, 1)
                if pre and k != "pre":
                    tile_a(n, "x0T", 0, xTa)
                if b:
                    tile_b(n, "x2T", 0, xTb)
                if a:
                    elu(n, 1)
                if pre and k != "pre":
                    tile_a(n, "x0T", 1, xTa)
                if b:
                    tile_b(n, "x2T", 1, xTb)
                if a:
                    mask_max("H3", n, 0)
                    t_head(n, 1, 0)
                    mask_max("H3", n, 1)
                if b:
                    own_message(n, 0)
                if a:
                    inverses("H2", n)
                    mask_max("H3", n, 2)
                    low("H2", n, 2)
                    mask_max("H3", n, 3)
                if pre:
                    scalars(n, "L0", "f0")
                if b:
                    tile_b(n, "mj", 0, VB)
                if a:
                    shifts("H3", n)
                    low("H2", n, 3)
                if pre:
                    mask_max("L0", n, 0)
                if b:
                    tile_b(n, "mj", 1, VB)
                if pre:
                    mask_max("L0", n, 1)
                if a:
                    t_head(n, 1, 1)
                    low("H3", n, 0)
                if pre:
                    mask_max("L0", n, 2)
                if b:
                    add_bank(n, "Amj", 0, xb)
                if a:
                    elu(n, 2)
                if pre:
                    mask_max("L0", n, 3)
                if b:
                    own_message(n, 1)
                if a:
                    low("H3", n, 1)
                if pre:
                    shifts("L0", n)
                if a:
                    inverses("H3", n)
                    t_head(n, 2, 0)
                if b:
                    add_bank(n, "Amj", 1, xb)
                    norm_stats("ln2", n, xb)
                    norm_aggr("ln2", n)
                    norm_var("ln2", n)
                if a:
                    low("H3", n, 2)
                    low("H3", n, 3)
                if b:
                    norm_out("ln2", n, xb, xb)
                if pre:
                    first_sum(n)
                    v_first(n)
                if b:
                    tile_b(n, "x3T", 0, xTb)
                if pre:
                    low("L0", n, 0)
                if a:
                    t_head(n, 2, 1)
                if b:
                    tile_b(n, "x3T", 1, xTb)
                if a:
                    elu(n, 3)
                if pre:
                    low("L0", n, 1)
                    inverses("L0", n)
                    evacuate("L0", n, 0)
                if b:
                    scalars(n, "L3", "f3", "b")
                if a:
                    t_head(n, 3, 0)
                    t_head(n, 3, 1)
                if b:
                    mask_max("L3", n, 0)
                    mask_max("L3", n, 1)
                    mask_max("L3", n, 2)
                    mask_max("L3", n, 3)
                    shifts("L3", n)
                if pre:
                    low("L0", n, 2)
                if b:
                    tile_b(n, "V3", 0, VB)
                if pre:
                    evacuate("L0", n, 1)
                    low("L0", n, 3)
                if a:
                    copy_rows(n)
                if pre:
                    evacuate("L0", n, 2)
                if b:
                    tile_b(n, "V3", 1, VB)
                    low("L3", n, 0)
                if a:
                    scalars(n, "O1", "fO")
                if pre:
                    evacuate("L0", n, 3)
                if b:
                    low("L3", n, 1)
                if a:
                    mask_max("O1", n, 0)
                    mask_max("O1", n, 1)
                if b:
                    inverses("L3", n)
                if a:
                    mask_max("O1", n, 2)
                    mask_max("O1", n, 3)
                if pre:
                    norm_stats("ln0", n, x0)
                if a:
                    shifts("O1", n)
                if pre:
                    norm_aggr("ln0", n)
                if b:
                    evacuate("L3", n, 0)
                    low("L3", n, 2)
                if pre:
                    norm_var("ln0", n)
                if b:
                    evacuate("L3", n, 1)
                    low("L3", n, 3)
                if pre:
                    norm_out("ln0", n, x0, x1)
                if b:
                    evacuate("L3", n, 2)
                    evacuate("L3", n, 3)
                if a:
                    tile_a(n, "VO", 0, VH[1])
                if b:
                    norm_stats("ln3", n, xb)
                    norm_aggr("ln3", n)
                    norm_var("ln3", n)
                    norm_out("ln3", n, xb, eb)
                if a:
                    tile_a(n, "VO", 1, VH[1])

            for c in range(KD):
                tile_a(-1, "x0T", c, xTa)
            dve.wait_ge(dot_done, next(dots))
            for stage in WA:
                last = dve.tensor_copy(wa_part(stage, 0), wa_raw_of(stage))
            last.then_inc(prep_dve, 1)
            dve.wait_ge(prep_dve, prepared("wa_high"))
            for stage in WA:
                last = dve.tensor_tensor(wa_part(stage, 1), wa_raw_of(stage), wa_part(stage, 0).bitcast(f32),
                                         ALU.subtract)
            last.then_inc(prep_dve, 1)
            dve.wait_ge(loaded["bl2"], 16)
            dve.wait_ge(loaded["rows"], 64)
            for i in range(NI):
                dve.tensor_scalar(deg_b[:, i, :], bl2_stage, deg[:, i:i + 1], None, ALU.mult)
            dve.tensor_scalar(b2m1[:, :], b2m1[:, :], -1.0, None, ALU.add).then_inc(prep_dve, 1)
            dve.wait_ge(prep_dve, len(PREP))
            dve.wait_ge(prep_pool, len(PREP_POOL))
            body(-1)
            body(0)
            with dve.Fori(1, B - 1) as n:
                body(n)
            body(B - 1)
            body(B)


_INS = ['x', 'adj', 'L0_gnn_W', 'L0_gnn_a', 'L1_gnn_W_heads', 'L1_gnn_a_heads', 'L1_gnn_W_out', 'L1_gnn_a_out',
        'L1_gnn_w1', 'L1_gnn_b1', 'L1_gnn_w2', 'L1_gnn_b2', 'L1_gnn_ln_gamma', 'L1_gnn_ln_beta', 'L2_gnn_W',
        'L2_gnn_b', 'L3_gnn_W', 'L3_gnn_a_src', 'L3_gnn_a_dst']


def kernel(**inputs):
    import numpy as _np
    import concourse.bacc as _bacc
    from concourse import mybir as _mybir
    from concourse.bass_utils import run_bass_kernel_spmd as _run

    nc = _bacc.Bacc("TRN2", target_bir_lowering=False, num_devices=1)
    arrays, args = {}, []
    for name in _INS:
        a = _np.ascontiguousarray(inputs[name])
        arrays[f"in_{name}"] = a
        args.append(nc.dram_tensor(f"in_{name}", a.shape, _mybir.dt.from_np(a.dtype), kind="ExternalInput").ap())
    args.append(nc.dram_tensor("out_x", (B, N, D), _mybir.dt.float32, kind="ExternalOutput").ap())
    graph_net_kernel(nc, *args)
    r = _run(nc, [arrays], core_ids=[0])
    return r.results[0]["out_x"]
```
